# Optimizing a Trainium2 kernel written in Bass

```python
import numpy as np
import jax
import jax.numpy as jnp

def _softmax(x, axis=-1):
    return jax.nn.softmax(x, axis=axis)

def _gelu(x):
    return jax.nn.gelu(x, approximate=True)

def _silu(x):
    return jax.nn.silu(x)

def _sigmoid(x):
    return jax.nn.sigmoid(x)

def _layernorm(x, axis=-1, eps=1e-05):
    m = jnp.mean(x, axis=axis, keepdims=True)
    v = jnp.var(x, axis=axis, keepdims=True)
    return (x - m) / jnp.sqrt(v + eps)

def _scatter_add(tgt, idx, src, axis=0):
    return tgt.at[idx].add(src)

def _segment_sum(src, seg, n):
    return jax.ops.segment_sum(src, seg, n)
kernel_name = 'mk_lm_tower_d1_tok_ids2048_r4_551424'

def setup_inputs(seed: int=0):
    np.random.seed(seed)
    _w = jnp.asarray

    def _rec_inputs():
        import jax
        import jax.numpy as jnp
        _rk = jax.random.key(seed)
        x = jax.random.randint(jax.random.fold_in(_rk, 1), (4, 512), 0, 127990, jnp.int32)
        return x
    x = _rec_inputs()

    def _L0_tok_setup():
        import jax, jax.numpy as jnp
        import numpy as np
        VOCAB = 32000
        EMBED = 512
        N_TRAIN = 64
        BATCH, SEQ = (4, 1024)
        key = jax.random.key(seed)
        k1, k2, k3, k4 = jax.random.split(key, 4)
        x = jax.random.randint(k1, (BATCH, SEQ), 0, VOCAB, dtype=jnp.int64 if jax.config.jax_enable_x64 else jnp.int32)
        W = jax.random.normal(k2, (VOCAB, EMBED), dtype=jnp.float32)
        delta_values = jax.random.normal(k3, (N_TRAIN * EMBED,), dtype=jnp.float32)
        token_indices = jnp.sort(jax.random.randint(k4, (N_TRAIN,), 0, VOCAB, dtype=jnp.int32))
        return {'x': x, 'W': W, 'delta_values': delta_values, 'token_indices': token_indices}
    _L0_tok_all = _L0_tok_setup()
    _L0_tok_in = {k: v for k, v in _L0_tok_all.items() if k in ('W', 'delta_values', 'token_indices')}
    del _L0_tok_all

    def _L0_attn_setup():
        import jax, jax.numpy as jnp
        import numpy as np
        DIM = 512
        D_STATE = 128
        D_CONV = 4
        N_HEADS = 48
        N_GROUPS = 1
        D_HEAD = 64
        D_INNER = N_HEADS * D_HEAD
        EPS = 1e-05
        RES_MULT = 1.0
        SEQ = 256
        BATCH = 1

        def _rms(x, w, eps=EPS):
            return x * jax.lax.rsqrt(jnp.mean(x * x, axis=-1, keepdims=True) + eps) * w

        def _forward(x, norm_w, in_proj_w, conv_w, conv_b, dt_bias, A_log, D_param, inner_norm_w, out_proj_w, conv_state, ssm_state):
            b, s, _ = x.shape
            xn = _rms(x, norm_w)
            proj = xn @ in_proj_w.T
            gn = N_GROUPS * D_STATE
            z, xc, B, C, dt = jnp.split(proj, [D_INNER, 2 * D_INNER, 2 * D_INNER + gn, 2 * D_INNER + 2 * gn], axis=-1)
            xc = jnp.moveaxis(xc, 1, 2)
            xp = jnp.concatenate([jnp.broadcast_to(conv_state, (b, D_INNER, D_CONV - 1)), xc], axis=-1)
            conv_out = conv_b[None, :, None] + sum((conv_w[None, :, k, None] * xp[:, :, k:k + s] for k in range(D_CONV)))
            xc = jax.nn.silu(conv_out)
            x_ssm = jnp.moveaxis(xc, 1, 2).reshape(b, s, N_HEADS, D_HEAD)
            hpg = N_HEADS // N_GROUPS
            B = jnp.repeat(B.reshape(b, s, N_GROUPS, D_STATE), hpg, axis=2)
            C = jnp.repeat(C.reshape(b, s, N_GROUPS, D_STATE), hpg, axis=2)
            dt = jax.nn.softplus(dt + dt_bias)
            A = -jnp.exp(A_log)
            h0 = jnp.broadcast_to(ssm_state, (b, N_HEADS, D_STATE, D_HEAD))

            def step(h, ins):
                x_t, B_t, C_t, dt_t = ins
                dA = jnp.exp(A * dt_t)[..., None, None]
                h = dA * h + B_t[..., :, None] * x_t[..., None, :]
                y_t = jnp.einsum('bhnp,bhn->bhp', h, C_t) + D_param[None, :, None] * x_t
                return (h, y_t)
            _, ys = jax.lax.scan(step, h0, (jnp.moveaxis(x_ssm, 1, 0), jnp.moveaxis(B, 1, 0), jnp.moveaxis(C, 1, 0), jnp.moveaxis(dt, 1, 0)))
            y = jnp.moveaxis(ys, 0, 1).reshape(b, s, D_INNER)
            y = _rms(y, inner_norm_w)
            y = y * jax.nn.silu(z)
            out = y @ out_proj_w.T
            return x + out * RES_MULT
        key = jax.random.key(seed)
        ks = jax.random.split(key, 12)
        d_in_proj = 2 * D_INNER + 2 * N_GROUPS * D_STATE + N_HEADS
        return {'x': jax.random.normal(ks[0], (BATCH, SEQ, DIM), jnp.float32), 'norm_w': jnp.ones((DIM,), jnp.float32), 'in_proj_w': 0.02 * jax.random.normal(ks[1], (d_in_proj, DIM), jnp.float32), 'conv_w': 0.02 * jax.random.normal(ks[2], (D_INNER, D_CONV), jnp.float32), 'conv_b': 0.01 * jax.random.normal(ks[3], (D_INNER,), jnp.float32), 'dt_bias': 0.1 * jax.random.normal(ks[4], (N_HEADS,), jnp.float32), 'A_log': 0.1 * jax.random.normal(ks[5], (N_HEADS,), jnp.float32), 'D_param': 0.1 * jax.random.normal(ks[6], (N_HEADS,), jnp.float32), 'inner_norm_w': jnp.ones((D_INNER,), jnp.float32), 'out_proj_w': 0.02 * jax.random.normal(ks[7], (DIM, D_INNER), jnp.float32), 'conv_state': jnp.zeros((1, D_INNER, D_CONV - 1), jnp.float32), 'ssm_state': jnp.zeros((1, N_HEADS, D_STATE, D_HEAD), jnp.float32)}
    _L0_attn_all = _L0_attn_setup()
    _L0_attn_in = {k: v for k, v in _L0_attn_all.items() if k in ('norm_w', 'in_proj_w', 'conv_w', 'conv_b', 'dt_bias', 'A_log', 'D_param', 'inner_norm_w', 'out_proj_w', 'conv_state', 'ssm_state')}
    del _L0_attn_all

    def _L0_ffn_setup():
        import jax, jax.numpy as jnp
        import numpy as np
        EPS = 1e-08

        def _rmsnorm(x, g):
            return g * (x * jax.lax.rsqrt(jnp.mean(x * x, axis=-1, keepdims=True) + EPS))

        def _act_quant(x):
            scale = 127.0 / jnp.clip(jnp.max(jnp.abs(x), axis=-1, keepdims=True), 0.0001, None)
            y = jnp.clip(jnp.round(x * scale), -128, 127) / scale
            return x + jax.lax.stop_gradient(y - x)

        def _ternary_quant(w):
            s = jnp.mean(jnp.abs(w))
            wq = jnp.round(jnp.tanh(w / (s + EPS))) * jnp.arctanh(s)
            return w + jax.lax.stop_gradient(wq - w)

        def _linear_bit(x, w, g):
            xq = _act_quant(_rmsnorm(x, g))
            wq = _ternary_quant(w)
            return jnp.einsum('bsd,od->bso', xq, wq)
        key = jax.random.key(seed)
        k = jax.random.split(key, 4)
        B, S, D, H = (4, 512, 512, 2048)
        std_up = float(np.sqrt(2.0 / (D + H)))
        std_dn = float(np.sqrt(2.0 / (H + D)))
        return {'x': jax.random.normal(k[0], (B, S, D), dtype=jnp.float32), 'w1': jax.random.normal(k[1], (H, D), dtype=jnp.float32) * std_up, 'g1': jnp.ones((D,), dtype=jnp.float32), 'w2': jax.random.normal(k[2], (H, D), dtype=jnp.float32) * std_up, 'g2': jnp.ones((D,), dtype=jnp.float32), 'w3': jax.random.normal(k[3], (D, H), dtype=jnp.float32) * std_dn, 'g3': jnp.ones((H,), dtype=jnp.float32)}
    _L0_ffn_all = _L0_ffn_setup()
    _L0_ffn_in = {k: v for k, v in _L0_ffn_all.items() if k in ('w1', 'g1', 'w2', 'g2', 'w3', 'g3')}
    del _L0_ffn_all
    return {'x': x, 'L0_tok_W': _L0_tok_in['W'], 'L0_tok_delta_values': _L0_tok_in['delta_values'], 'L0_tok_token_indices': _L0_tok_in['token_indices'], 'L0_attn_norm_w': _L0_attn_in['norm_w'], 'L0_attn_in_proj_w': _L0_attn_in['in_proj_w'], 'L0_attn_conv_w': _L0_attn_in['conv_w'], 'L0_attn_conv_b': _L0_attn_in['conv_b'], 'L0_attn_dt_bias': _L0_attn_in['dt_bias'], 'L0_attn_A_log': _L0_attn_in['A_log'], 'L0_attn_D_param': _L0_attn_in['D_param'], 'L0_attn_inner_norm_w': _L0_attn_in['inner_norm_w'], 'L0_attn_out_proj_w': _L0_attn_in['out_proj_w'], 'L0_attn_conv_state': _L0_attn_in['conv_state'], 'L0_attn_ssm_state': _L0_attn_in['ssm_state'], 'L0_ffn_w1': _L0_ffn_in['w1'], 'L0_ffn_g1': _L0_ffn_in['g1'], 'L0_ffn_w2': _L0_ffn_in['w2'], 'L0_ffn_g2': _L0_ffn_in['g2'], 'L0_ffn_w3': _L0_ffn_in['w3'], 'L0_ffn_g3': _L0_ffn_in['g3']}

def reference(x, L0_tok_W, L0_tok_delta_values, L0_tok_token_indices, L0_attn_norm_w, L0_attn_in_proj_w, L0_attn_conv_w, L0_attn_conv_b, L0_attn_dt_bias, L0_attn_A_log, L0_attn_D_param, L0_attn_inner_norm_w, L0_attn_out_proj_w, L0_attn_conv_state, L0_attn_ssm_state, L0_ffn_w1, L0_ffn_g1, L0_ffn_w2, L0_ffn_g2, L0_ffn_w3, L0_ffn_g3):
    import jax
    import jax.numpy as jnp

    def _L0_tok_ref(x, W, delta_values, token_indices):
        import jax, jax.numpy as jnp
        import numpy as np
        VOCAB = 32000
        EMBED = 512
        N_TRAIN = 64
        BATCH, SEQ = (4, 1024)
        delta = delta_values.reshape(EMBED, N_TRAIN).T
        W_eff = W.at[token_indices].add(delta)
        return W_eff[x]

    def _L0_attn_ref(x, norm_w, in_proj_w, conv_w, conv_b, dt_bias, A_log, D_param, inner_norm_w, out_proj_w, conv_state, ssm_state):
        import jax, jax.numpy as jnp
        import numpy as np
        DIM = 512
        D_STATE = 128
        D_CONV = 4
        N_HEADS = 48
        N_GROUPS = 1
        D_HEAD = 64
        D_INNER = N_HEADS * D_HEAD
        EPS = 1e-05
        RES_MULT = 1.0
        SEQ = 256
        BATCH = 1

        def _rms(x, w, eps=EPS):
            return x * jax.lax.rsqrt(jnp.mean(x * x, axis=-1, keepdims=True) + eps) * w

        def _forward(x, norm_w, in_proj_w, conv_w, conv_b, dt_bias, A_log, D_param, inner_norm_w, out_proj_w, conv_state, ssm_state):
            b, s, _ = x.shape
            xn = _rms(x, norm_w)
            proj = xn @ in_proj_w.T
            gn = N_GROUPS * D_STATE
            z, xc, B, C, dt = jnp.split(proj, [D_INNER, 2 * D_INNER, 2 * D_INNER + gn, 2 * D_INNER + 2 * gn], axis=-1)
            xc = jnp.moveaxis(xc, 1, 2)
            xp = jnp.concatenate([jnp.broadcast_to(conv_state, (b, D_INNER, D_CONV - 1)), xc], axis=-1)
            conv_out = conv_b[None, :, None] + sum((conv_w[None, :, k, None] * xp[:, :, k:k + s] for k in range(D_CONV)))
            xc = jax.nn.silu(conv_out)
            x_ssm = jnp.moveaxis(xc, 1, 2).reshape(b, s, N_HEADS, D_HEAD)
            hpg = N_HEADS // N_GROUPS
            B = jnp.repeat(B.reshape(b, s, N_GROUPS, D_STATE), hpg, axis=2)
            C = jnp.repeat(C.reshape(b, s, N_GROUPS, D_STATE), hpg, axis=2)
            dt = jax.nn.softplus(dt + dt_bias)
            A = -jnp.exp(A_log)
            h0 = jnp.broadcast_to(ssm_state, (b, N_HEADS, D_STATE, D_HEAD))

            def step(h, ins):
                x_t, B_t, C_t, dt_t = ins
                dA = jnp.exp(A * dt_t)[..., None, None]
                h = dA * h + B_t[..., :, None] * x_t[..., None, :]
                y_t = jnp.einsum('bhnp,bhn->bhp', h, C_t) + D_param[None, :, None] * x_t
                return (h, y_t)
            _, ys = jax.lax.scan(step, h0, (jnp.moveaxis(x_ssm, 1, 0), jnp.moveaxis(B, 1, 0), jnp.moveaxis(C, 1, 0), jnp.moveaxis(dt, 1, 0)))
            y = jnp.moveaxis(ys, 0, 1).reshape(b, s, D_INNER)
            y = _rms(y, inner_norm_w)
            y = y * jax.nn.silu(z)
            out = y @ out_proj_w.T
            return x + out * RES_MULT
        return _forward(x, norm_w, in_proj_w, conv_w, conv_b, dt_bias, A_log, D_param, inner_norm_w, out_proj_w, conv_state, ssm_state)

    def _L0_ffn_ref(x, w1, g1, w2, g2, w3, g3):
        import jax, jax.numpy as jnp
        import numpy as np
        EPS = 1e-08

        def _rmsnorm(x, g):
            return g * (x * jax.lax.rsqrt(jnp.mean(x * x, axis=-1, keepdims=True) + EPS))

        def _act_quant(x):
            scale = 127.0 / jnp.clip(jnp.max(jnp.abs(x), axis=-1, keepdims=True), 0.0001, None)
            y = jnp.clip(jnp.round(x * scale), -128, 127) / scale
            return x + jax.lax.stop_gradient(y - x)

        def _ternary_quant(w):
            s = jnp.mean(jnp.abs(w))
            wq = jnp.round(jnp.tanh(w / (s + EPS))) * jnp.arctanh(s)
            return w + jax.lax.stop_gradient(wq - w)

        def _linear_bit(x, w, g):
            xq = _act_quant(_rmsnorm(x, g))
            wq = _ternary_quant(w)
            return jnp.einsum('bsd,od->bso', xq, wq)
        swish = jax.nn.silu(_linear_bit(x, w1, g1))
        x_v = _linear_bit(x, w2, g2)
        h = swish * x_v
        return _linear_bit(h, w3, g3)
    h = _L0_tok_ref(x, L0_tok_W, L0_tok_delta_values, L0_tok_token_indices)
    h = h + _L0_attn_ref(_layernorm(h, axis=-1), L0_attn_norm_w, L0_attn_in_proj_w, L0_attn_conv_w, L0_attn_conv_b, L0_attn_dt_bias, L0_attn_A_log, L0_attn_D_param, L0_attn_inner_norm_w, L0_attn_out_proj_w, L0_attn_conv_state, L0_attn_ssm_state)
    h = h + _L0_ffn_ref(_layernorm(h, axis=-1), L0_ffn_w1, L0_ffn_g1, L0_ffn_w2, L0_ffn_g2, L0_ffn_w3, L0_ffn_g3)
    return h

_drawn_inputs = setup_inputs


def setup_inputs(seed=0):
    import zlib

    import numpy as np

    out = dict(_drawn_inputs(seed))
    spreads = {'L0_attn_norm_w': (1.0, 0.2),
     'L0_attn_inner_norm_w': (1.0, 0.554),
     'L0_attn_conv_state': (0.0, 0.8),
     'L0_attn_ssm_state': (0.0, 0.393),
     'L0_ffn_g1': (1.0, 0.2),
     'L0_ffn_g2': (1.0, 0.2),
     'L0_ffn_g3': (1.0, 0.2)}
    factors = {'L0_attn_dt_bias': 3.65, 'L0_attn_A_log': 3.109}
    for name, (base, spread) in spreads.items():
        noise = np.random.default_rng([zlib.crc32(name.encode()), seed]).standard_normal(out[name].shape)
        drawn = base * np.exp(spread * noise) if base else spread * noise
        out[name] = jnp.asarray(drawn.astype(out[name].dtype))
    for name, factor in factors.items():
        out[name] = (out[name] * factor).astype(out[name].dtype)
    return out
```

```python
from contextlib import ExitStack

import numpy as np

import concourse.bass as bass
from concourse import mybir

F32 = mybir.dt.float32
F32R = mybir.dt.float32r
BF16 = mybir.dt.bfloat16
I32 = mybir.dt.int32
ALU = mybir.AluOpType
ACT = mybir.ActivationFunctionType
AX = mybir.AxisListType

P = 128
VOCAB, DIM, TRAINED = 32000, 512, 64
BATCH, SEQ = 4, 512
TOKENS = BATCH * SEQ
TILES = TOKENS // P
KT = DIM // P
HEADS, HEAD, STATE, TAPS = 48, 64, 128, 4
INNER = HEADS * HEAD
GH = 4
GC = GH * HEAD
GROUPS = HEADS // GH
GT = GC // P
CHUNKS = SEQ // P
SLOTS = BATCH * CHUNKS
HIDDEN = 2048
HT = HIDDEN // P
EPS_NORM, EPS_RMS, EPS_BIT = 1e-5, 1e-5, 1e-8
MAGIC = 12582912.0
ATANH_HALF = 0.5493061443340549
RSQRT_GUESS = 1597463007.0
WCOLS = 2048


def newton_rsqrt(eng, sem, count, y, v, t, steps=3):
    def link(ins):
        nonlocal count
        count += 1
        ins.then_inc(sem, 1)
        eng.wait_ge(sem, count)

    link(eng.tensor_scalar(t.bitcast(I32), v.bitcast(I32), 1, None, ALU.logical_shift_right))
    link(eng.tensor_scalar(y.bitcast(I32), t.bitcast(I32), -1.0, RSQRT_GUESS, ALU.mult, ALU.add))
    for _ in range(steps):
        link(eng.tensor_tensor(t, y, y, ALU.mult))
        link(eng.scalar_tensor_tensor(out=t, in0=t, scalar=-0.5, in1=v, op0=ALU.mult, op1=ALU.mult))
        link(eng.scalar_tensor_tensor(out=y, in0=t, scalar=1.5, in1=y, op0=ALU.add, op1=ALU.mult))
    return count


def embed(nc, d, k):
    with ExitStack() as ctx:
        def sb(name, shape, dt=F32):
            return ctx.enter_context(nc.sbuf_tensor(name, shape, dt))

        def sem(name):
            return ctx.enter_context(nc.semaphore(name))

        id_row = sb("id_row", [TRAINED, TOKENS], I32)
        row_f = sb("row_f", [TRAINED, TOKENS])
        hit = sb("hit", [TRAINED, TOKENS])
        id_col = sb("id_col", [P, TILES], I32)
        col_f = sb("col_f", [P, TILES])
        col_wrap = sb("col_wrap", [P, TILES])
        row_id = sb("row_id", [P, TILES], I32)
        tok = sb("tok", [TRAINED, 1], I32)
        tok_f = sb("tok_f", [TRAINED, 1])
        tok_wrap = sb("tok_wrap", [TRAINED, 1])
        delta = sb("delta", [TRAINED, DIM])
        norm_row = sb("norm_row", [P, DIM])
        stats = sb("stats", [P, TILES, 6])
        mv = sb("mv", [P, TILES, 2])
        var, rstd, ms, rrms, tmp = (sb(n, [P, TILES]) for n in ("var", "rstd", "ms", "rrms", "tmp_c"))
        x1 = sb("x1", [P, 2, DIM])
        resid = sb("resid", [P, 2, DIM])
        xs = sb("xs", [P, 2, DIM])
        w_raw = sb("w_raw", [P, 2, WCOLS])
        p_delta = [ctx.enter_context(nc.psum_tensor(f"p_delta{i}", [P, DIM], F32)) for i in range(2)]
        p_xt = [ctx.enter_context(nc.psum_tensor(f"p_xt{i}", [P, KT, P], F32)) for i in range(2)]

        loaded, ids_ready, chain = sem("em_loaded"), sem("em_ids"), sem("em_chain")
        gathered, hit_ready, delta_done = sem("em_gathered"), sem("em_hit"), sem("em_delta")
        added, x1_ready, resid_ready, xs_ready = sem("em_added"), sem("em_x1"), sem("em_resid"), sem("em_xs")
        resid_stored = [sem(f"em_stored{i}") for i in range(2)]
        xt_done, hi_done, lo_done = sem("em_xt"), sem("em_hi"), sem("em_lo")
        w_loaded = [sem(f"em_w{i}") for i in range(2)]
        w_summed = sem("em_wsum")
        h0 = k["acc"]
        n_w = 3 * HIDDEN * DIM // P // WCOLS
        block = ctx.enter_context(nc.Block())

        @block.sync
        def _(sp):
            sp.dma_start(id_col[:, :], d["id_col"]).then_inc(loaded, 16)
            sp.dma_start(tok[:, :], d["tok"]).then_inc(loaded, 16)
            sp.dma_start(id_row[:, :], d["id_row"].partition_broadcast(TRAINED)).then_inc(loaded, 16)
            sp.dma_start(delta[:, :], d["delta"]).then_inc(loaded, 16)
            sp.dma_start(norm_row[:, :], d["norm_w"].partition_broadcast(P)).then_inc(loaded, 16)
            sp.dma_start(k["ident"][:, :], d["ident"]).then_inc(loaded, 16)
            for n in range(n_w):
                if n >= 2:
                    sp.wait_ge(w_summed, n - 1)
                sp.dma_start(w_raw[:, n % 2, :], d["w_ffn"][n]).then_inc(w_loaded[n % 2], 16)
            for t in range(TILES):
                sp.wait_ge(resid_ready, t + 1)
                sp.dma_start(d["resid"][t], resid[:, t % 2, :]).then_inc(resid_stored[t % 2], 16)
            for i in range(2):
                sp.wait_ge(resid_stored[i], 16 * TILES // 2)

        @block.gpsimd
        def _(pool):
            pool.wait_ge(ids_ready, 1)
            for t in range(TILES):
                pool.indirect_dma_start(out=h0[:, t, :], out_offset=None, in_=d["W"],
                                        in_offset=bass.IndirectOffsetOnAxis(ap=row_id[:, t:t + 1], axis=0)
                                        ).then_inc(gathered, 16)
            for t in range(TILES):
                pool.wait_ge(x1_ready, t + 1)
                if t >= 2:
                    pool.wait_ge(resid_stored[t % 2], 16 * (t // 2))
                pool.tensor_tensor(resid[:, t % 2, :], h0[:, t, :], x1[:, t % 2, :], ALU.add
                                   ).then_inc(resid_ready, 1)

        @block.scalar
        def _(act):
            for n in range(n_w):
                act.wait_ge(w_loaded[n % 2], 16 * (n // 2 + 1))
                act.activation(w_raw[:, n % 2, :], w_raw[:, n % 2, :], ACT.Abs,
                               accum_out=k["w_sum"][:, n:n + 1]).then_inc(w_summed, 1)
            for t in range(TILES):
                act.wait_ge(xt_done, t + 1)
                act.activation(k["x_hi"][:, :, t * P:(t + 1) * P], p_xt[t % 2][:, :, :], ACT.Identity
                               ).then_inc(hi_done, 1)

        @block.tensor
        def _(pe):
            pe.wait_ge(hit_ready, 1)
            for t in range(TILES):
                if t >= 2:
                    pe.wait_ge(added, t - 1)
                pe.matmul(p_delta[t % 2][:, :], hit[:, t * P:(t + 1) * P], delta[:, :],
                          start=True, stop=True).then_inc(delta_done, 1)
            for t in range(TILES):
                pe.wait_ge(xs_ready, t + 1)
                if t >= 2:
                    pe.wait_ge(lo_done, t - 1)
                for j in range(KT):
                    last = pe.transpose(p_xt[t % 2][:, j, :], xs[:, t % 2, j * P:(j + 1) * P],
                                        k["ident"][:, :])
                last.then_inc(xt_done, 1)

        @block.vector
        def _(dve):
            n = 0

            def link(ins):
                nonlocal n
                n += 1
                ins.then_inc(chain, 1)
                dve.wait_ge(chain, n)

            def wrapped(f, wrap, ints):
                link(dve.tensor_copy(f, ints))
                link(dve.tensor_scalar(wrap, f, 0.0, float(VOCAB), ALU.is_lt, ALU.mult))
                link(dve.tensor_tensor(f, f, wrap, ALU.add))

            dve.wait_ge(loaded, 6 * 16)
            wrapped(col_f[:, :], col_wrap[:, :], id_col[:, :])
            link(dve.tensor_scalar(col_f[:, :], col_f[:, :], 0.0, float(VOCAB - 1), ALU.max, ALU.min))
            dve.tensor_copy(row_id[:, :], col_f[:, :]).then_inc(ids_ready, 1)
            wrapped(tok_f[:, :], tok_wrap[:, :], tok[:, :])
            wrapped(row_f[:, :], hit[:, :], id_row[:, :])
            link(dve.tensor_scalar(row_f[:, :], row_f[:, :], 0.0, float(VOCAB - 1), ALU.max, ALU.min))
            dve.tensor_scalar(hit[:, :], row_f[:, :], tok_f[:, 0:1], None, ALU.is_equal).then_inc(hit_ready, 1)
            for t in range(TILES):
                if t == 0:
                    dve.wait_ge(gathered, 16 * TILES)
                dve.wait_ge(delta_done, t + 1)
                dve.tensor_tensor(h0[:, t, :], h0[:, t, :], p_delta[t % 2][:, :], ALU.add).then_inc(added, 1)
                dve.wait_ge(added, t + 1)
                link(dve.bn_stats(stats[:, t, :], h0[:, t, :]))
                link(dve.bn_aggr(mv[:, t, :], stats[:, t, :]))
            link(dve.tensor_scalar(var[:, :], mv[:, :, 1], EPS_NORM, None, ALU.add))
            n = newton_rsqrt(dve, chain, n, rstd[:, :], var[:, :], tmp[:, :])
            link(dve.tensor_tensor(ms[:, :], rstd[:, :], rstd[:, :], ALU.mult))
            link(dve.tensor_tensor(ms[:, :], ms[:, :], mv[:, :, 1], ALU.mult))
            link(dve.tensor_scalar(ms[:, :], ms[:, :], EPS_RMS, None, ALU.add))
            n = newton_rsqrt(dve, chain, n, rrms[:, :], ms[:, :], tmp[:, :])
            for t in range(TILES + 1):
                if t < TILES:
                    if t >= 2:
                        dve.wait_ge(resid_ready, t - 1)
                    dve.tensor_scalar(x1[:, t % 2, :], h0[:, t, :], mv[:, t, 0:1], rstd[:, t:t + 1],
                                      ALU.subtract, ALU.mult).then_inc(x1_ready, 1)
                    dve.wait_ge(x1_ready, t + 1)
                    if t >= 2:
                        dve.wait_ge(xt_done, t - 1)
                    dve.scalar_tensor_tensor(out=xs[:, t % 2, :], in0=x1[:, t % 2, :], scalar=rrms[:, t:t + 1],
                                             in1=norm_row[:, :], op0=ALU.mult, op1=ALU.mult).then_inc(xs_ready, 1)
                if t >= 1:
                    u = t - 1
                    dve.wait_ge(hi_done, u + 1)
                    dve.tensor_tensor(k["x_lo"][:, :, u * P:(u + 1) * P], p_xt[u % 2][:, :, :],
                                      k["x_hi"][:, :, u * P:(u + 1) * P], ALU.subtract).then_inc(lo_done, 1)


def decays(nc, d, k):
    with ExitStack() as ctx:
        def sb(name, shape, dt=F32):
            return ctx.enter_context(nc.sbuf_tensor(name, shape, dt))

        def sem(name):
            return ctx.enter_context(nc.semaphore(name))

        TC = TILES * HEADS
        w_raw = sb("bw_raw", [P, KT, 3 * P])
        w_hi = sb("bw_hi", [P, KT, 3 * P], F32R)
        w_lo = sb("bw_lo", [P, KT, 3 * P], F32R)
        b_t = sb("b_t", [P, TOKENS])
        dt_pre = sb("dt_pre", [HEADS, TOKENS])
        soft = sb("soft", [HEADS, TOKENS])
        cum = sb("cum", [HEADS, TOKENS])
        cum_hi = sb("cum_hi", [HEADS, TOKENS], F32R)
        cum_lo = sb("cum_lo", [HEADS, TOKENS], F32R)
        cum_tok = sb("cum_tok", [P, TC])
        tri = sb("tri", [P, P])
        pick_last = sb("pick_last", [P, P])
        dt_bias = sb("dt_bias", [HEADS, 1])
        a_log = sb("a_log", [HEADS, 1])
        neg_a = sb("neg_a", [HEADS, 1])
        neg_mask_f = sb("neg_mask_f", [P, P])
        rows_f = soft[0:10, 0:2 * GH * P].rearrange("r (n c) -> r n c", n=2)
        cols_f = soft[0:10, 2 * GH * P:2 * GH * P + 2 * P].rearrange("r (n c) -> r n c", n=2)
        p_proj = [ctx.enter_context(nc.psum_tensor(f"p_bcd{i}", [P, SEQ], F32)) for i in range(2)]
        p_cb = ctx.enter_context(nc.psum_tensor("p_cb", [P, 4, P], F32))
        p_bt = ctx.enter_context(nc.psum_tensor("p_bt", [P, 4, P], F32))
        p_ct = [ctx.enter_context(nc.psum_tensor(f"p_ct{i}", [P, 512], F32)) for i in range(2)]
        p_cq = [ctx.enter_context(nc.psum_tensor(f"p_cq{i}", [P, 512], F32)) for i in range(2)]
        HC = TC // 2

        loaded, w_hi_done, w_lo_done = sem("bd_loaded"), sem("bd_whi"), sem("bd_wlo")
        proj_done, evicted_a, evicted_v = sem("bd_proj"), sem("bd_eva"), sem("bd_evv")
        steps_a, steps_v, consts = sem("bd_sa"), sem("bd_sv"), sem("bd_consts")
        cb_done, cb_masked, bt_done, bt_copied = sem("bd_cb"), sem("bd_cbm"), sem("bd_bt"), sem("bd_btc")
        cum_ready, hi_ready, lo_ready, stored = sem("bd_cum"), sem("bd_hi"), sem("bd_lo"), sem("bd_stored")
        ct_done, tok_ready, cq_done, diff_ready = sem("bd_ct"), sem("bd_tok"), sem("bd_cq"), sem("bd_diff")
        keep_in, zeroed = sem("bd_keep"), sem("bd_zero")
        block = ctx.enter_context(nc.Block())

        @block.sync
        def _(sp):
            for to, of in ((w_raw[:, :, :], d["w_bcd"]), (dt_bias[:, :], d["dt_bias"]), (a_log[:, :], d["a_log"]),
                           (tri[:, :], d["tri"]),
                           (pick_last[:, :], d["pick_last"]), (neg_mask_f[:, :], d["neg_mask"]),
                           (rows_f, d["rows"]), (cols_f, d["cols"]),
                           (k["d_row"][:, :], d["D"].partition_broadcast(P)),
                           (k["params"][:, :, :], d["params"])):
                sp.dma_start(to, of).then_inc(loaded, 16)
            sp.wait_ge(steps_v, 1)
            sp.dma_start(dt_pre[:, :], d["keep"].partition_broadcast(HEADS)).then_inc(keep_in, 16)
            sp.wait_ge(hi_ready, 1)
            sp.dma_start(d["cum"][0], cum_hi[:, :].bitcast(F32)).then_inc(stored, 16)
            sp.wait_ge(lo_ready, 1)
            sp.dma_start(d["cum"][1], cum_lo[:, :].bitcast(F32)).then_inc(stored, 16)
            sp.wait_ge(stored, 32)

        @block.gpsimd
        def _(pool):
            pool.memset(k["acc"][:, :, :], 0.0).then_inc(zeroed, 1)

        @block.tensor
        def _(pe):
            pe.wait_ge(w_lo_done, 1)
            for n in range(3 * BATCH):
                b, j = n // 3, n % 3
                if n >= 2:
                    m = n - 2
                    if m % 3 == 1:
                        pe.wait_ge(evicted_v, m // 3 + 1)
                    else:
                        pe.wait_ge(evicted_a, 2 * (m // 3) + (1 if m % 3 == 0 else 2))
                i = 0
                for w, x in ((w_hi, k["x_hi"]), (w_hi, k["x_lo"]), (w_lo, k["x_hi"])):
                    for c in range(KT):
                        last = pe.matmul(p_proj[n % 2][:, :], w[:, c, j * P:(j + 1) * P],
                                         x[:, c, b * SEQ:(b + 1) * SEQ], start=(i == 0), stop=(i == 3 * KT - 1))
                        i += 1
                last.then_inc(proj_done, 1)
            pe.wait_ge(evicted_a, 2 * BATCH)
            pe.wait_ge(evicted_v, BATCH)
            for b in range(BATCH):
                if b:
                    pe.wait_ge(cb_masked, b)
                    pe.wait_ge(bt_copied, b)
                for q in range(CHUNKS):
                    at = slice((b * CHUNKS + q) * P, (b * CHUNKS + q + 1) * P)
                    last = pe.matmul(p_cb[:, q, :], b_t[:, at], k["c_t"][:, at], start=True, stop=True)
                last.then_inc(cb_done, 1)
                for q in range(CHUNKS):
                    at = slice((b * CHUNKS + q) * P, (b * CHUNKS + q + 1) * P)
                    last = pe.transpose(p_bt[:, q, :], b_t[:, at], k["ident"][:, :])
                last.then_inc(bt_done, 1)
            pe.wait_ge(cum_ready, 1)
            for t in range(TILES):
                h, c = t // (TILES // 2), t % (TILES // 2)
                last = pe.transpose(p_ct[h][:, c * HEADS:(c + 1) * HEADS], cum[:, t * P:(t + 1) * P],
                                    k["ident"][0:HEADS, 0:HEADS])
            last.then_inc(ct_done, 1)
            pe.wait_ge(tok_ready, 2)
            for h in range(2):
                last = pe.matmul(p_cq[h][:, 0:HC], pick_last[:, :], cum_tok[:, h * HC:(h + 1) * HC],
                                 start=True, stop=True)
            last.then_inc(cq_done, 1)

        @block.scalar
        def _(act):
            act.wait_ge(loaded, 10 * 16)
            act.activation(w_hi[:, :, :], w_raw[:, :, :], ACT.Identity).then_inc(w_hi_done, 1)
            act.activation(neg_a[:, :], a_log[:, :], ACT.Exp).then_inc(steps_a, 1)
            for b in range(BATCH):
                at = slice(b * SEQ, (b + 1) * SEQ)
                act.wait_ge(proj_done, 3 * b + 1)
                act.activation(b_t[:, at], p_proj[(3 * b) % 2][:, :], ACT.Identity).then_inc(evicted_a, 1)
                act.wait_ge(proj_done, 3 * b + 3)
                act.activation(dt_pre[:, at], p_proj[(3 * b + 2) % 2][0:HEADS, :], ACT.Identity,
                               bias=dt_bias[:, 0:1]).then_inc(evicted_a, 1)
            act.wait_ge(evicted_a, 2 * BATCH)
            act.wait_ge(consts, 4)
            act.activation(soft[:, :], dt_pre[:, :], ACT.Abs).then_inc(steps_a, 1)
            act.wait_ge(steps_a, 2)
            act.activation(soft[:, :], soft[:, :], ACT.Exp, scale=-1.0).then_inc(steps_a, 1)
            act.wait_ge(steps_a, 3)
            act.activation(soft[:, :], soft[:, :], ACT.Ln, bias=1.0).then_inc(steps_a, 1)
            for b in range(BATCH):
                act.wait_ge(bt_done, b + 1)
                act.activation(k["b_tok"][:, b * CHUNKS:(b + 1) * CHUNKS, :], p_bt[:, :, :], ACT.Identity
                               ).then_inc(bt_copied, 1)
            act.wait_ge(cum_ready, 1)
            act.activation(cum_hi[:, :], cum[:, :], ACT.Identity).then_inc(hi_ready, 1)
            act.wait_ge(tok_ready, 2)
            act.activation(k["e_cum"][:, :], cum_tok[:, :], ACT.Exp)
            act.wait_ge(cq_done, 1)
            for h in range(2):
                act.activation(k["e_all"][:, h * HC:(h + 1) * HC], p_cq[h][:, 0:HC], ACT.Exp).then_inc(steps_a, 1)
            act.wait_ge(diff_ready, 2)
            act.activation(k["e_rest"][:, :], k["e_rest"][:, :], ACT.Exp)

        @block.vector
        def _(dve):
            dve.wait_ge(loaded, 10 * 16)
            dve.wait_ge(w_hi_done, 1)
            dve.tensor_tensor(w_lo[:, :, :], w_raw[:, :, :], w_hi[:, :, :], ALU.subtract).then_inc(w_lo_done, 1)
            dve.tensor_copy(k["ident_b"][:, :], k["ident"][:, :]).then_inc(consts, 1)
            dve.tensor_copy(k["neg_mask"][:, :], neg_mask_f[:, :]).then_inc(consts, 1)
            dve.tensor_copy(k["rows"][:, :, :], rows_f).then_inc(consts, 1)
            dve.tensor_copy(k["cols"][:, :, :], cols_f).then_inc(consts, 1)
            for b in range(BATCH):
                dve.wait_ge(proj_done, 3 * b + 2)
                dve.tensor_copy(k["c_t"][:, b * SEQ:(b + 1) * SEQ], p_proj[(3 * b + 1) % 2][:, :]
                                ).then_inc(evicted_v, 1)
            dve.wait_ge(evicted_a, 2 * BATCH)
            dve.wait_ge(steps_a, 4)
            dve.scalar_tensor_tensor(out=soft[:, :], in0=dt_pre[:, :], scalar=0.0, in1=soft[:, :],
                                     op0=ALU.max, op1=ALU.add).then_inc(steps_v, 1)
            dve.wait_ge(steps_v, 1)
            dve.tensor_scalar(soft[:, :], soft[:, :], neg_a[:, 0:1], -1.0, ALU.mult, ALU.mult).then_inc(steps_v, 1)
            dve.wait_ge(steps_v, 2)
            dve.wait_ge(keep_in, 16)
            dve.tensor_tensor_scan(cum[:, :], dt_pre[:, :], soft[:, :], 0.0, ALU.mult, ALU.add).then_inc(cum_ready, 1)
            for b in range(BATCH):
                dve.wait_ge(cb_done, b + 1)
                dve.tensor_tensor(k["cb"][:, b * CHUNKS:(b + 1) * CHUNKS, :], p_cb[:, :, :],
                                  tri[:, :].unsqueeze(1).to_broadcast([P, CHUNKS, P]), ALU.mult
                                  ).then_inc(cb_masked, 1)
            dve.wait_ge(hi_ready, 1)
            dve.tensor_tensor(cum_lo[:, :], cum[:, :], cum_hi[:, :], ALU.subtract).then_inc(lo_ready, 1)
            dve.wait_ge(ct_done, 1)
            for h in range(2):
                dve.tensor_copy(cum_tok[:, h * HC:(h + 1) * HC], p_ct[h][:, 0:HC]).then_inc(tok_ready, 1)
            dve.wait_ge(tok_ready, 2)
            dve.wait_ge(steps_a, 6)
            for h in range(2):
                dve.tensor_tensor(k["e_rest"][:, h * HC:(h + 1) * HC], p_cq[h][:, 0:HC],
                                  cum_tok[:, h * HC:(h + 1) * HC], ALU.subtract).then_inc(diff_ready, 1)


def count(per_group, g, local):
    return g * per_group + local


def mixer(nc, d, k):
    with ExitStack() as ctx:
        def sb(name, shape, dt=F32):
            return ctx.enter_context(nc.sbuf_tensor(name, shape, dt))

        def sem(name):
            return ctx.enter_context(nc.semaphore("mx_" + name))

        stage = sb("stage", [P, 2, DIM])
        wi_hi = sb("wi_hi", [P, 2 * GT, KT, P], F32R)
        wi_lo = sb("wi_lo", [P, 2 * GT, KT, P], F32R)
        wo_hi = sb("wo_hi", [P, GT, DIM], F32R)
        wo_lo = sb("wo_lo", [P, GT, DIM], F32R)
        half = sb("half", [P, 12])
        d_now = sb("d_now", [P, GH])
        all_now = sb("all_now", [P, TILES, GH])
        pad = sb("pad", [P, GT, TAPS - 1 + SEQ])
        conv = sb("conv", [P, GT, SEQ])
        th_x = sb("th_x", [P, SEQ])
        z2 = sb("z2", [P, 2, GT, SEQ])
        x_tok = sb("x_tok", [P, 2, CHUNKS, GC])
        m_t = sb("m_t", [P, 2, GH, P])
        x_dec = sb("x_dec", [P, GH, HEAD])
        xd = sb("xd", [P, GH, HEAD])
        y = sb("y", [P, 2, GC])
        h_first = sb("h_first", [P, GH, HEAD])
        h_next = sb("h_next", [P, GH, HEAD])
        h_dec = sb("h_dec", [P, GH, HEAD])
        sq = sb("sq", [P, GC], BF16)
        gate = sb("gate", [P, GT, P])
        g_hi = sb("g_hi", [P, 2, GT, P], F32R)
        g_lo = sb("g_lo", [P, 2, GT, P], F32R)

        def bank(name, shape):
            return ctx.enter_context(nc.psum_tensor(name, shape, F32))

        p_proj = [bank(f"p_proj{i}", [P, SEQ]) for i in range(2)]
        p_d = bank("p_d", [P, GH, P])
        p_y = bank("p_y", [P, 2, GH, HEAD])
        p_s = bank("p_s", [P, 512])
        p_yt = bank("p_yt", [P, 512])
        p_xt = bank("p_xt", [P, CHUNKS, P])
        p_o = bank("p_o", [P, DIM])

        raw_in = [sem(f"raw_in{i}") for i in range(2)]
        rows_in = [sem(f"rows_in{i}") for i in range(2)]
        h_in = sem("h_in")
        w_hi_done, w_lo_done = sem("w_hi"), sem("w_lo")
        par_done = sem("par")
        tables_done = sem("tables")
        proj_done = sem("proj")
        raw_done, tap_done = sem("raw"), sem("tap")
        conv_done = sem("conv")
        xth_done, zth_done = sem("xth"), sem("zth")
        x_done, z_done = sem("x"), sem("z")
        xt_done, xtok_done = sem("xt"), sem("xtok")
        d_done, e_done, m_done = sem("d"), sem("e"), sem("m")
        y_mm, ys_done, xd_done, yx_done, y_done = sem("y_mm"), sem("ys"), sem("xd"), sem("yx"), sem("y")
        xdec_done, s_done, hdec_done, h_done = sem("xdec"), sem("s"), sem("hdec"), sem("h")
        yt_done, gate_done, ghi_done, glo_done = sem("yt"), sem("gate"), sem("ghi"), sem("glo")
        sq_done, o_done, acc_done = sem("sq"), sem("o"), sem("acc")

        def wait(eng, s, per_group, g, local, unit=1):
            v = count(per_group, g, local)
            if isinstance(v, int) and v <= 0:
                return
            eng.wait_ge(s, v * unit)

        def exists(g, slot):
            return not isinstance(g, int) or 0 <= g * SLOTS + slot < GROUPS * SLOTS

        def groups(eng, body):
            for s in range(-4, SLOTS):
                body(0, s)
            with eng.Fori(1, GROUPS - 1) as g:
                for s in range(SLOTS):
                    body(g, s)
            for s in range(SLOTS + 2):
                body(GROUPS - 1, s)

        def kind(s):
            return (s + 4) // 4, s % 4, s % 4 < GT

        def x_count(i, j):
            return GT * i + j + 1

        def state_count(i, q):
            return (CHUNKS - 1) * i + min(q + 1, CHUNKS - 1)

        block = ctx.enter_context(nc.Block())

        @block.sync
        def _(sp):
            def load_weights(g, n, src):
                wait(sp, w_lo_done, 6, g, 4 + n - 2 + 1)
                sp.dma_start(stage[:, n % 2, :], src).then_inc(raw_in[n % 2], 16)

            def load_rows(g, s):
                wait(sp, d_done, 16, g, s - 1)
                at = slice((s % SLOTS) * P, (s % SLOTS + 1) * P)
                gg = g + s // SLOTS
                heads = bass.ds(gg * GH, GH)
                sp.dma_start(k["rows"][0:2, s % 2, :].bitcast(F32).rearrange("r (h t) -> r h t", h=GH),
                             d["cum"][:, heads, at]).then_inc(rows_in[s % 2], 16)
                for part in range(2):
                    sp.dma_start(k["cols"][2 + part * GH:2 + (part + 1) * GH, s % 2, :].bitcast(F32),
                                 d["cum"][part, heads, at]).then_inc(rows_in[s % 2], 16)

            def body(g, s):
                if s == -4:
                    for n in range(2, 6):
                        load_weights(-1, n, d["w_in"][0, n - 2])
                    sp.dma_start(h_first[:, :, :], d["h_first"][0]).then_inc(h_in, 16)
                    for n in range(2):
                        load_rows(0, n)
                if s == 0:
                    for n in range(2):
                        load_weights(g, n, d["w_out"][g, n])
                if 0 <= s and exists(g, s + 2):
                    load_rows(g, s + 2)
                if s in (4, 5, 8, 9) and exists(g, SLOTS):
                    j = (4, 5, 8, 9).index(s)
                    load_weights(g, j + 2, d["w_in"][g + 1, j])
                if s == 14 and exists(g, SLOTS):
                    wait(sp, y_mm, 16, g, 13)
                    wait(sp, hdec_done, 12, g, 10)
                    sp.dma_start(h_first[:, :, :], d["h_first"][g + 1]).then_inc(h_in, 16)
            groups(sp, body)

        @block.tensor
        def _(pe):
            def split_products(out, w_hi, w_lo, x_hi, x_lo, order=(0, 1, 2)):
                n = len(w_hi)
                for p, k_th in enumerate(order):
                    w, x = ((w_hi, x_hi), (w_hi, x_lo), (w_lo, x_hi))[k_th]
                    for c in range(n):
                        last = pe.matmul(out, w[c], x[c], start=(p == 0 and c == 0),
                                         stop=(p == 2 and c == n - 1))
                return last

            def body(g, s):
                if exists(g, s + 4):
                    i, j, is_x = kind(s)
                    b = i % BATCH
                    if i % BATCH == 0:
                        wait(pe, w_lo_done, 6, g, (6 if i else 0) + j + 1)
                    if is_x:
                        wait(pe, z_done, 8, g, x_count(i - 1, j))
                    else:
                        wait(pe, raw_done, 8, g, x_count(i, j - GT))
                        wait(pe, tap_done, 8, g, x_count(i, j - GT))
                    at = slice(b * SEQ, (b + 1) * SEQ)
                    split_products(p_proj[j % 2][:, :],
                                   [wi_hi[:, j, c, :] for c in range(KT)], [wi_lo[:, j, c, :] for c in range(KT)],
                                   [k["x_hi"][:, c, at] for c in range(KT)], [k["x_lo"][:, c, at] for c in range(KT)]
                                   ).then_inc(proj_done, 1)
                if exists(g, s + 1):
                    wait(pe, e_done, 16, g, s + 1)
                    wait(pe, rows_in[(s + 1) % 2], 24, g, 3 * ((s + 1) // 2 + 1), 16)
                    pe.matmul(p_d[:, :, :], k["cols"][:, (s + 1) % 2, :],
                              k["rows"][:, (s + 1) % 2, :].rearrange("r (h t) -> r h t", h=GH),
                              start=True, stop=False)
                    pe.matmul(p_d[:, :, :], k["ident_b"][:, :],
                              k["neg_mask"][:, :].unsqueeze(1).to_broadcast([P, GH, P]),
                              start=False, stop=True).then_inc(d_done, 1)
                if exists(g, s - 2):
                    wait(pe, glo_done, 16, g, s - 1)
                    wait(pe, acc_done, 16, g, s - 2)
                    if s == 2:
                        wait(pe, w_lo_done, 6, g, 6)
                    o = s % 2
                    split_products(p_o[:, :], [g_hi[:, o, c, :] for c in range(GT)],
                                   [g_lo[:, o, c, :] for c in range(GT)],
                                   [wo_hi[:, c, :] for c in range(GT)], [wo_lo[:, c, :] for c in range(GT)]
                                   ).then_inc(o_done, 1)
                i, q = s // CHUNKS, s % CHUNKS
                if exists(g, s):
                    wait(pe, y_done, 16, g, s)
                    if q == 0:
                        state = h_first
                        if i == 0:
                            wait(pe, h_in, 1, g, 1, 16)
                        wait(pe, xtok_done, 8, g, x_count(i, GT - 1))
                    else:
                        state = h_next
                        wait(pe, h_done, 12, g, state_count(i, q - 1))
                    at = slice((s % SLOTS) * P, (s % SLOTS + 1) * P)
                    pe.matmul(p_y[:, 1, :, :], k["c_t"][:, at], state[:, :, :], start=True, stop=True)
                    wait(pe, m_done, 16, g, s + 1)
                    for h in range(GH):
                        last = pe.matmul(p_y[:, 0, h, :], m_t[:, s % 2, h, :],
                                         x_tok[:, i % 2, q, h * HEAD:(h + 1) * HEAD], start=True, stop=True)
                    last.then_inc(y_mm, 1)
                if q >= 2 and exists(g, s + 4):
                    j = q - 2
                    wait(pe, x_done, 8, g, x_count(i + 1, j))
                    wait(pe, xtok_done, 8, g, x_count(i + 1, j) - 1)
                    for c in range(CHUNKS):
                        last = pe.transpose(p_xt[:, c, :], conv[:, j, c * P:(c + 1) * P], k["ident"][:, :])
                    last.then_inc(xt_done, 1)
                if q < CHUNKS - 1 and exists(g, s):
                    wait(pe, xdec_done, 12, g, state_count(i, q))
                    wait(pe, h_done, 12, g, state_count(i, q) - 1)
                    pe.matmul(p_s[:, 0:GC], k["b_tok"][:, s % SLOTS, :],
                              x_dec[:, :, :].rearrange("p h c -> p (h c)"), start=True, stop=True
                              ).then_inc(s_done, 1)
                if exists(g, s - 1):
                    wait(pe, y_done, 16, g, s)
                    wait(pe, gate_done, 16, g, s - 1)
                    for c in range(GT):
                        last = pe.transpose(p_yt[:, c * P:(c + 1) * P], y[:, (s - 1) % 2, c * P:(c + 1) * P],
                                            k["ident"][:, :])
                    last.then_inc(yt_done, 1)
            groups(pe, body)

        @block.scalar
        def _(act):
            def weight_hi(g, n):
                wait(act, raw_in[n % 2], 3, g, (4 + n) // 2 + 1, 16)
                if n < 2:
                    wait(act, o_done, 16, g, 0)
                    wait(act, par_done, 2, g, 2)
                    act.activation(wo_hi[:, n, :], stage[:, n % 2, :], ACT.Identity,
                                   scale=half[:, 6 * n + 5:6 * n + 6]).then_inc(w_hi_done, 1)
                else:
                    wait(act, proj_done, 16, g, 12 + n - 2 + 1)
                    act.activation(wi_hi[:, n - 2, :, :].rearrange("p c m -> p (c m)"), stage[:, n % 2, :],
                                   ACT.Identity).then_inc(w_hi_done, 1)

            def body(g, s):
                if s == -4:
                    for n in range(2, 6):
                        weight_hi(-1, n)
                if exists(g, s - 2):
                    wait(act, gate_done, 16, g, s - 1)
                    wait(act, o_done, 16, g, s - 3)
                    act.activation(g_hi[:, s % 2, :, :], gate[:, :, :], ACT.Identity).then_inc(ghi_done, 1)
                if exists(g, s - 1):
                    wait(act, y_done, 16, g, s)
                    wait(act, sq_done, 16, g, s - 1)
                    gg = g if s else g - 1
                    at = ((s - 1) % SLOTS) * GROUPS + gg
                    act.activation(sq[:, :], y[:, (s - 1) % 2, :], ACT.Square,
                                   accum_out=k["y_sq"][:, bass.ds(at, 1)]).then_inc(sq_done, 1)
                i, j, is_x = kind(s)
                if exists(g, s + 4):
                    wait(act, proj_done, 16, g, 4 * i + j + 1)
                    if is_x:
                        wait(act, conv_done, 24, g, 3 * x_count(i - 1, j))
                        act.activation(pad[:, j, TAPS - 1:], p_proj[j % 2][:, :], ACT.Identity).then_inc(raw_done, 1)
                        wait(act, par_done, 2, g, 2 * (i // BATCH) + 2)
                        wait(act, xt_done, 8, g, x_count(i - 1, j))
                        act.activation(conv[:, j, :], p_proj[j % 2][:, :], ACT.Identity,
                                       bias=half[:, 6 * j + 4:6 * j + 5], scale=half[:, 6 * j + 3:6 * j + 4]
                                       ).then_inc(tap_done, 1)
                    else:
                        wait(act, gate_done, 16, g, 4 * (i - 1))
                        act.activation(z2[:, i % 2, j - GT, :], p_proj[j % 2][:, :], ACT.Tanh, scale=0.5
                                       ).then_inc(zth_done, 1)
                if exists(g, s + 1):
                    wait(act, d_done, 16, g, s + 2)
                    wait(act, y_mm, 16, g, s)
                    act.activation(m_t[:, (s + 1) % 2, :, :], p_d[:, :, :], ACT.Exp).then_inc(e_done, 1)
                if j in (1, 2) and exists(g, s + 3):
                    wait(act, conv_done, 24, g, 3 * x_count(i, j - 1))
                    wait(act, x_done, 8, g, x_count(i, j - 1) - 1)
                    act.activation(th_x[:, :], conv[:, j - 1, :], ACT.Tanh).then_inc(xth_done, 1)
                if s == 1:
                    for n in range(2):
                        weight_hi(g, n)
                i, q = s // CHUNKS, s % CHUNKS
                if q >= 2 and exists(g, s + 4):
                    j = q - 2
                    wait(act, xt_done, 8, g, x_count(i + 1, j))
                    wait(act, y_mm, 16, g, 4 * i)
                    wait(act, xd_done, 16, g, 4 * i)
                    wait(act, xdec_done, 12, g, 3 * i)
                    act.activation(x_tok[:, (i + 1) % 2, :, j * P:(j + 1) * P], p_xt[:, :, :], ACT.Identity
                                   ).then_inc(xtok_done, 1)
                if 8 <= s < 12 and exists(g, SLOTS):
                    weight_hi(g, s - 6)
            groups(act, body)

        @block.vector
        def _(dve):
            def weight_lo(g, n):
                wait(dve, w_hi_done, 6, g, 4 + n + 1)
                if n < 2:
                    dve.scalar_tensor_tensor(out=wo_lo[:, n, :], in0=stage[:, n % 2, :],
                                             scalar=half[:, 6 * n + 5:6 * n + 6], in1=wo_hi[:, n, :],
                                             op0=ALU.mult, op1=ALU.subtract).then_inc(w_lo_done, 1)
                else:
                    dve.tensor_tensor(wi_lo[:, n - 2, :, :].rearrange("p c m -> p (c m)"), stage[:, n % 2, :],
                                      wi_hi[:, n - 2, :, :].rearrange("p c m -> p (c m)"), ALU.subtract
                                      ).then_inc(w_lo_done, 1)

            def parameters(g):
                dve.tensor_scalar(half[:, :], k["params"][:, bass.ds(g, 1), 0:12], 0.5, None, ALU.mult
                                  ).then_inc(par_done, 1)
                dve.tensor_copy(pad[:, :, 0:TAPS - 1], k["params"][:, bass.ds(g, 1), 12:18]
                                .rearrange("p g (j t) -> p (g j) t", j=GT)).then_inc(par_done, 1)

            def tables(g):
                dve.tensor_copy(d_now[:, :], k["d_row"][:, bass.ds(g * GH, GH)]).then_inc(tables_done, 1)
                dve.tensor_copy(all_now[:, :, :], k["e_all"][:, :].rearrange("p (t h) -> p t h", h=HEADS)
                                [:, :, bass.ds(g * GH, GH)]).then_inc(tables_done, 1)

            def per_head(e, t, g):
                return e[:, bass.ds(g * GH + t * HEADS, GH)].unsqueeze(2).to_broadcast([P, GH, HEAD])

            def body(g, s):
                if s == -4:
                    parameters(0)
                    tables(0)
                    for n in range(2, 6):
                        weight_lo(-1, n)
                if s == 2:
                    for n in range(2):
                        weight_lo(g, n)
                if exists(g, s - 2):
                    wait(dve, yt_done, 16, g, s - 1)
                    wait(dve, glo_done, 16, g, s - 2)
                    i, q = (s - 2) // CHUNKS, (s - 2) % CHUNKS
                    wait(dve, z_done, 8, g, x_count(i, GT - 1))
                    dve.tensor_tensor(gate[:, :, :], p_yt[:, 0:GC].rearrange("p (c t) -> p c t", c=GT),
                                      z2[:, i % 2, :, q * P:(q + 1) * P], ALU.mult).then_inc(gate_done, 1)
                i, q = s // CHUNKS, s % CHUNKS
                if q < CHUNKS - 1 and exists(g, s):
                    wait(dve, xtok_done, 8, g, x_count(i, GT - 1))
                    wait(dve, s_done, 12, g, state_count(i, q) - 1)
                    dve.tensor_tensor(x_dec[:, :, :],
                                      x_tok[:, i % 2, q, :].rearrange("p (h c) -> p h c", h=GH),
                                      per_head(k["e_rest"], s % SLOTS, g), ALU.mult).then_inc(xdec_done, 1)
                if exists(g, s - 2):
                    wait(dve, ghi_done, 16, g, s - 1)
                    dve.tensor_tensor(g_lo[:, s % 2, :, :], gate[:, :, :], g_hi[:, s % 2, :, :], ALU.subtract
                                      ).then_inc(glo_done, 1)
                i, j, is_x = kind(s)
                if j in (2, 3) and exists(g, s + 2):
                    wait(dve, xth_done, 8, g, x_count(i, j - 2))
                    dve.scalar_tensor_tensor(out=conv[:, j - 2, :], in0=th_x[:, :], scalar=1.0,
                                             in1=conv[:, j - 2, :], op0=ALU.add, op1=ALU.mult).then_inc(x_done, 1)
                i, j, is_x = kind(s - 1)
                if s > -4 and exists(g, s + 3):
                    if is_x:
                        n = x_count(i, j)
                        wait(dve, raw_done, 8, g, n)
                        wait(dve, par_done, 2, g, 2 * (i // BATCH) + 2)
                        wait(dve, tap_done, 8, g, n)
                        for tap in range(TAPS - 1):
                            wait(dve, conv_done, 24, g, 3 * (n - 1) + tap)
                            dve.scalar_tensor_tensor(out=conv[:, j, :], in0=pad[:, j, tap:tap + SEQ],
                                                     scalar=half[:, 6 * j + tap:6 * j + tap + 1], in1=conv[:, j, :],
                                                     op0=ALU.mult, op1=ALU.add).then_inc(conv_done, 1)
                    else:
                        n = x_count(i, j - GT)
                        wait(dve, zth_done, 8, g, n)
                        dve.scalar_tensor_tensor(out=z2[:, i % 2, j - GT, :], in0=z2[:, i % 2, j - GT, :], scalar=1.0,
                                                 in1=p_proj[j % 2][:, :], op0=ALU.add, op1=ALU.mult
                                                 ).then_inc(z_done, 1)
                if exists(g, s + 1):
                    wait(dve, e_done, 16, g, s + 2)
                    dve.tensor_tensor(m_t[:, (s + 1) % 2, :, :], m_t[:, (s + 1) % 2, :, :],
                                      k["cb"][:, (s + 1) % SLOTS, :].unsqueeze(1).to_broadcast([P, GH, P]), ALU.mult
                                      ).then_inc(m_done, 1)
                i, q = s // CHUNKS, s % CHUNKS
                yv = y[:, s % 2, :].rearrange("p (h c) -> p h c", h=GH)
                if exists(g, s):
                    t = s % SLOTS
                    wait(dve, y_mm, 16, g, s + 1)
                    wait(dve, yt_done, 16, g, s - 1)
                    wait(dve, sq_done, 16, g, s - 1)
                    dve.tensor_tensor(yv, p_y[:, 1, :, :], per_head(k["e_cum"], t, g), ALU.mult
                                      ).then_inc(ys_done, 1)
                    if q < CHUNKS - 1:
                        wait(dve, s_done, 12, g, state_count(i, q))
                        wait(dve, hdec_done, 12, g, state_count(i, q))
                        dve.tensor_tensor(h_next[:, :, :], h_dec[:, :, :],
                                          p_s[:, 0:GC].rearrange("p (h c) -> p h c", h=GH), ALU.add
                                          ).then_inc(h_done, 1)
                if exists(g, s - 2):
                    wait(dve, o_done, 16, g, s - 1)
                    t = (s - 2) % SLOTS
                    dve.tensor_tensor(k["acc"][:, t, :], k["acc"][:, t, :], p_o[:, :], ALU.add
                                      ).then_inc(acc_done, 1)
                if exists(g, s):
                    wait(dve, yx_done, 16, g, s + 1)
                    dve.tensor_tensor(yv, yv, p_y[:, 0, :, :], ALU.add).then_inc(y_done, 1)
                if 8 <= s < 12 and exists(g, SLOTS):
                    weight_lo(g, s - 6)
                if s == 15 and exists(g, SLOTS):
                    tables(g + 1)
                if s == 10 and exists(g, SLOTS):
                    wait(dve, tap_done, 8, g, 8)
                    wait(dve, conv_done, 24, g, 24)
                    parameters(g + 1)
            groups(dve, body)

        @block.gpsimd
        def _(pool):
            def per_head(e):
                return e.unsqueeze(2).to_broadcast([P, GH, HEAD])

            def body(g, s):
                if not exists(g, s) or s < 0:
                    return
                i, q, t = s // CHUNKS, s % CHUNKS, s % SLOTS
                wait(pool, xtok_done, 8, g, x_count(i, GT - 1))
                wait(pool, yx_done, 16, g, s)
                if s == 0:
                    wait(pool, tables_done, 2, g, 2)
                pool.tensor_tensor(xd[:, :, :], x_tok[:, i % 2, q, :].rearrange("p (h c) -> p h c", h=GH),
                                   per_head(d_now[:, :]), ALU.mult).then_inc(xd_done, 1)
                if q < CHUNKS - 1:
                    if q == 0:
                        state = h_first
                        if i == 0:
                            wait(pool, h_in, 1, g, 1, 16)
                    else:
                        state = h_next
                    wait(pool, h_done, 12, g, state_count(i, q) - 1)
                    pool.tensor_tensor(h_dec[:, :, :], state[:, :, :],
                                       per_head(all_now[:, t, :]), ALU.mult).then_inc(hdec_done, 1)
                wait(pool, ys_done, 16, g, s + 1)
                wait(pool, xd_done, 16, g, s + 1)
                yv = y[:, s % 2, :].rearrange("p (h c) -> p h c", h=GH)
                pool.tensor_tensor(yv, yv, xd[:, :, :], ALU.add).then_inc(yx_done, 1)
            groups(pool, body)


def ffn(nc, d, k):
    with ExitStack() as ctx:
        def sb(name, shape, dt=F32):
            return ctx.enter_context(nc.sbuf_tensor(name, shape, dt))

        def sem(name):
            return ctx.enter_context(nc.semaphore("ff_" + name))

        h1 = k["acc"]
        n_w = 3 * HIDDEN * DIM // P // WCOLS
        per_w = n_w // 3
        tern = sb("tern", [P, 3, KT * HIDDEN], BF16)
        raw = sb("ff_raw", [P, 2, WCOLS])
        below = sb("below", [P, WCOLS], BF16)
        resid = sb("ff_resid", [P, 2, DIM])
        ones = sb("ones", [P, P])
        g12 = sb("g12", [P, 2, DIM])
        g3 = sb("g3", [P, HIDDEN])
        stats = sb("ff_stats", [P, TILES, 6])
        mv = sb("ff_mv", [P, TILES, 2])
        names = ("ff_r", "ff_tmp", "ff_v", "ff_rstd", "ff_ms", "ff_rb", "ff_rn")
        r, tmp, v, rstd, ms, rb, rn = (sb(n, [P, TILES]) for n in names)
        s3, pos, neg, den, ath = (sb(n, [P, 3]) for n in ("s3", "pos", "neg", "den", "ath"))
        sum3 = sb("sum3", [P, 3])
        u12 = sb("u12", [P, 2, DIM])
        top = sb("top", [P, 4])
        scale12 = sb("scale12", [P, 4])
        q12 = sb("q12", [P, 2, DIM], BF16)
        q_t = sb("q_t", [P, 2, 2 * KT, P], BF16)
        deq = sb("deq", [P, 2, 2])
        sw = sb("sw", [P, 2, DIM])
        h = sb("ff_h", [P, HIDDEN])
        u3 = sb("u3", [P, HIDDEN])
        hsq = sb("hsq", [P, HIDDEN], BF16)
        hss = sb("hss", [P, 1])
        c3 = sb("c3", [P, 8])
        q3 = sb("q3", [P, HIDDEN], BF16)
        q3_t = sb("q3_t", [P, HT, P], BF16)
        res = sb("res", [P, 2, DIM])

        def bank(name, shape, dt=F32):
            return ctx.enter_context(nc.psum_tensor(name, shape, dt))

        p1 = [bank(f"p_w1_{i}", [P, DIM]) for i in range(2)]
        p2 = [bank(f"p_w2_{i}", [P, DIM]) for i in range(2)]
        p_q = bank("p_q", [P, 2 * KT, P], BF16)
        p_h = [bank(f"p_h{i}", [P, HT // 2, P], BF16) for i in range(2)]
        p_o = bank("p_out", [P, DIM])

        loaded, chain, achain = sem("loaded"), sem("chain"), sem("achain")
        resid_in = [sem(f"resid{i}") for i in range(2)]
        raw_in = [sem(f"raw{i}") for i in range(2)]
        h1_done, sums_ready, mean_done, ln_in, ln_done = sem("h1"), sem("sums"), sem("mean"), sem("lnin"), sem("ln")
        below_done, tern_done = sem("below"), sem("tern")
        q12_done, qt_done, qtc_done = sem("q12"), sem("qt"), sem("qtc")
        w12_done, sw_done, h_done, hss_done = sem("w12"), sem("sw"), sem("h"), sem("hss")
        u3_done, q3_done, ht_done, htc_done = sem("u3"), sem("q3"), sem("ht"), sem("htc")
        o_done, deq_done, res_done = sem("o"), sem("deq"), sem("res")
        out_done = [sem(f"out{i}") for i in range(2)]
        t1 = lambda w, c: tern[:, w, c * HIDDEN:(c + 1) * HIDDEN]
        NQ = HIDDEN // DIM
        block = ctx.enter_context(nc.Block())

        @block.sync
        def _(sp):
            sp.dma_start(ones[:, :], d["ones"]).then_inc(loaded, 16)
            for n in range(2):
                sp.dma_start(g12[:, n, :], d["g12"][n].partition_broadcast(P)).then_inc(loaded, 16)
            sp.dma_start(g3[:, :], d["g3"].partition_broadcast(P)).then_inc(loaded, 16)
            for n in range(max(TILES, n_w)):
                if n < TILES:
                    if n >= 2:
                        sp.wait_ge(h1_done, n - 1)
                    sp.dma_start(resid[:, n % 2, :], d["resid"][n]).then_inc(resid_in[n % 2], 16)
            for n in range(n_w):
                if n >= 2:
                    sp.wait_ge(tern_done, n - 1)
                sp.dma_start(raw[:, n % 2, :], d["w_ffn"][n]).then_inc(raw_in[n % 2], 16)
            for t in range(TILES):
                sp.wait_ge(res_done, t + 1)
                sp.dma_start(d["out"][t * P:(t + 1) * P, :], res[:, t % 2, :]).then_inc(out_done[t % 2], 16)
            for i in range(2):
                sp.wait_ge(out_done[i], 16 * TILES // 2)

        @block.tensor
        def _(pe):
            pe.wait_ge(loaded, 4 * 16)
            pe.wait_ge(sums_ready, 1)
            pe.matmul(p_o[:, 0:3], ones[:, :], sum3[:, :], start=True, stop=True).then_inc(mean_done, 1)

            def turn_q(t):
                pe.wait_ge(q12_done, 2 * (t + 1))
                if t:
                    pe.wait_ge(qtc_done, t)
                for w in range(2):
                    for c in range(KT):
                        last = pe.transpose(p_q[:, w * KT + c, :], q12[:, w, c * P:(c + 1) * P], k["ident_b"][:, :])
                last.then_inc(qt_done, 1)

            def down(t):
                pe.wait_ge(q3_done, t + 1)
                if t:
                    pe.wait_ge(htc_done, 2 * t)
                for c in range(HT):
                    last = pe.transpose(p_h[c // (HT // 2)][:, c % (HT // 2), :], q3[:, c * P:(c + 1) * P],
                                        k["ident_b"][:, :])
                    if c % (HT // 2) == HT // 2 - 1:
                        last.then_inc(ht_done, 1)
                pe.wait_ge(res_done, t) if t else pe.wait_ge(ln_in, 1)
                for c in range(HT):
                    if c % (HT // 2) == 0:
                        pe.wait_ge(htc_done, 2 * t + 1 + c // (HT // 2))
                    if t == 0 and c == 0:
                        pe.wait_ge(tern_done, n_w)
                    last = pe.matmul(p_o[:, :], q3_t[:, c, :], tern[:, 2, c * DIM:(c + 1) * DIM],
                                     start=(c == 0), stop=(c == HT - 1))
                last.then_inc(o_done, 1)

            turn_q(0)
            for t in range(TILES + 1):
                if t < TILES:
                    pe.wait_ge(qtc_done, t + 1)
                    if t == 0:
                        pe.wait_ge(tern_done, 2 * per_w)
                    for n in range(NQ):
                        m = t * NQ + n
                        if m >= 2:
                            pe.wait_ge(h_done, m - 1)
                        for w, p in ((0, p1), (1, p2)):
                            for c in range(KT):
                                last = pe.matmul(p[m % 2][:, :], q_t[:, t % 2, w * KT + c, :],
                                                 t1(w, c)[:, n * DIM:(n + 1) * DIM],
                                                 start=(c == 0), stop=(c == KT - 1))
                        last.then_inc(w12_done, 1)
                if t >= 1:
                    down(t - 1)
                if t + 1 < TILES:
                    turn_q(t + 1)

        @block.scalar
        def _(act):
            act.wait_ge(ln_in, 1)
            act.activation(ath[:, :], den[:, :], ACT.Ln).then_inc(ln_done, 1)

            def turned(t):
                act.wait_ge(qt_done, t + 1)
                if t >= 2:
                    act.wait_ge(w12_done, NQ * (t - 1))
                act.activation(q_t[:, t % 2, :, :], p_q[:, :, :], ACT.Copy).then_inc(qtc_done, 1)

            turned(0)
            for t in range(TILES + 1):
                if t < TILES:
                    for n in range(NQ):
                        m = t * NQ + n
                        act.wait_ge(w12_done, m + 1)
                        act.wait_ge(deq_done, t + 1)
                        if m >= 2:
                            act.wait_ge(h_done, m - 1)
                        act.activation(sw[:, m % 2, :], p1[m % 2][:, :], ACT.Silu,
                                       scale=deq[:, t % 2, 0:1]).then_inc(sw_done, 1)
                if t >= 1:
                    u = t - 1
                    for half in range(2):
                        act.wait_ge(ht_done, 2 * u + half + 1)
                        if u:
                            act.wait_ge(o_done, u)
                        act.activation(q3_t[:, half * (HT // 2):(half + 1) * (HT // 2), :], p_h[half][:, :, :],
                                       ACT.Copy).then_inc(htc_done, 1)
                if t < TILES:
                    act.wait_ge(h_done, NQ * (t + 1))
                    if t:
                        act.wait_ge(hss_done, t)
                        act.wait_ge(q3_done, t)
                    act.activation(hsq[:, :], h[:, :], ACT.Square, accum_out=hss[:, 0:1]).then_inc(hss_done, 1)
                    act.wait_ge(u3_done, t + 1)
                    if t:
                        act.wait_ge(ht_done, 2 * t)
                    act.activation(q3[:, :], u3[:, :], ACT.Copy, bias=-MAGIC).then_inc(q3_done, 1)
                    if t + 1 < TILES:
                        turned(t + 1)

        @block.vector
        def _(dve):
            n = 0

            def link(ins):
                nonlocal n
                n += 1
                ins.then_inc(chain, 1)
                dve.wait_ge(chain, n)

            link(dve.tensor_reduce(v[:, :], k["y_sq"][:, :].rearrange("p (t g) -> p t g", g=GROUPS), AX.X, ALU.add))
            link(dve.tensor_scalar(v[:, :], v[:, :], 1.0 / INNER, EPS_RMS, ALU.mult, ALU.add))
            n = newton_rsqrt(dve, chain, n, r[:, :], v[:, :], tmp[:, :])
            dve.tensor_reduce(sum3[:, :], k["w_sum"][:, :].rearrange("p (w c) -> p w c", w=3), AX.X, ALU.add
                              ).then_inc(sums_ready, 1)
            for t in range(TILES):
                dve.wait_ge(resid_in[t % 2], 16 * (t // 2 + 1))
                dve.scalar_tensor_tensor(out=h1[:, t, :], in0=h1[:, t, :], scalar=r[:, t:t + 1],
                                         in1=resid[:, t % 2, :], op0=ALU.mult, op1=ALU.add).then_inc(h1_done, 1)
                dve.wait_ge(h1_done, t + 1)
                link(dve.bn_stats(stats[:, t, :], h1[:, t, :]))
                link(dve.bn_aggr(mv[:, t, :], stats[:, t, :]))
            link(dve.tensor_scalar(v[:, :], mv[:, :, 1], EPS_NORM, None, ALU.add))
            n = newton_rsqrt(dve, chain, n, rstd[:, :], v[:, :], tmp[:, :])
            link(dve.tensor_tensor(ms[:, :], rstd[:, :], rstd[:, :], ALU.mult))
            link(dve.tensor_tensor(ms[:, :], ms[:, :], mv[:, :, 1], ALU.mult))
            link(dve.tensor_scalar(ms[:, :], ms[:, :], EPS_BIT, None, ALU.add))
            n = newton_rsqrt(dve, chain, n, rb[:, :], ms[:, :], tmp[:, :])
            link(dve.tensor_tensor(rn[:, :], rb[:, :], rstd[:, :], ALU.mult))

            dve.wait_ge(mean_done, 1)
            link(dve.tensor_scalar(s3[:, :], p_o[:, 0:3], 1.0 / (HIDDEN * DIM), None, ALU.mult))
            link(dve.tensor_scalar(pos[:, :], s3[:, :], EPS_BIT, ATANH_HALF, ALU.add, ALU.mult))
            link(dve.tensor_scalar(neg[:, :], pos[:, :], -1.0, None, ALU.mult))
            link(dve.tensor_scalar(den[:, :], s3[:, :], -1.0, 1.0, ALU.mult, ALU.add))
            link(dve.reciprocal(den[:, :], den[:, :]))
            dve.scalar_tensor_tensor(out=den[:, :], in0=s3[:, :], scalar=1.0, in1=den[:, :],
                                     op0=ALU.add, op1=ALU.mult).then_inc(ln_in, 1)
            dve.wait_ge(ln_done, 1)
            link(dve.tensor_scalar(ath[:, :], ath[:, :], 0.5 / 127.0, None, ALU.mult))
            dve.wait_ge(loaded, 4 * 16)

            def ternary(i):
                w = i // per_w
                dve.wait_ge(raw_in[i % 2], 16 * (i // 2 + 1))
                if i:
                    dve.wait_ge(tern_done, i)
                dve.tensor_scalar(below[:, :], raw[:, i % 2, :], neg[:, w:w + 1], None, ALU.is_lt
                                  ).then_inc(below_done, 1)
                dve.wait_ge(below_done, i + 1)
                dve.scalar_tensor_tensor(out=tern[:, w, (i % per_w) * WCOLS:(i % per_w + 1) * WCOLS],
                                         in0=raw[:, i % 2, :], scalar=pos[:, w:w + 1], in1=below[:, :],
                                         op0=ALU.is_gt, op1=ALU.subtract).then_inc(tern_done, 1)

            def prepare(t):
                if t >= 2:
                    dve.wait_ge(h_done, NQ * (t - 1))
                for w in range(2):
                    link(dve.tensor_scalar(tmp[:, 0:1], mv[:, t, 0:1], -1.0, None, ALU.mult))
                    link(dve.scalar_tensor_tensor(out=u12[:, w, :], in0=h1[:, t, :], scalar=tmp[:, 0:1],
                                                  in1=g12[:, w, :], op0=ALU.add, op1=ALU.mult))
                    link(dve.tensor_reduce(top[:, w:w + 1], u12[:, w, :], AX.X, ALU.max,
                                           apply_absolute_value=True))
                link(dve.tensor_scalar(top[:, 0:2], top[:, 0:2], rn[:, t:t + 1], 1e-4, ALU.mult, ALU.max))
                dve.tensor_tensor(deq[:, t % 2, :], top[:, 0:2], ath[:, 0:2], ALU.mult).then_inc(deq_done, 1)
                link(dve.reciprocal(scale12[:, 0:2], top[:, 0:2]))
                link(dve.tensor_scalar(scale12[:, 0:2], scale12[:, 0:2], 127.0, rn[:, t:t + 1], ALU.mult, ALU.mult))
                for w in range(2):
                    link(dve.tensor_scalar(u12[:, w, :], u12[:, w, :], scale12[:, w:w + 1], MAGIC,
                                           ALU.mult, ALU.add))
                if t:
                    dve.wait_ge(qt_done, t)
                for w in range(2):
                    dve.tensor_scalar(q12[:, w, :], u12[:, w, :], MAGIC, None, ALU.subtract).then_inc(q12_done, 1)

            for i in range(per_w):
                ternary(i)
            prepare(0)
            for i in range(per_w, n_w):
                ternary(i)
            for t in range(TILES + 1):
                if t < TILES:
                    for m in range(t * NQ, (t + 1) * NQ):
                        at = slice((m % NQ) * DIM, (m % NQ + 1) * DIM)
                        dve.wait_ge(sw_done, m + 1)
                        dve.wait_ge(deq_done, t + 1)
                        if m % NQ == 0 and t:
                            dve.wait_ge(hss_done, t)
                        dve.scalar_tensor_tensor(out=h[:, at], in0=p2[m % 2][:, :], scalar=deq[:, t % 2, 1:2],
                                                 in1=sw[:, m % 2, :], op0=ALU.mult, op1=ALU.mult).then_inc(h_done, 1)
                if t >= 1:
                    u = t - 1
                    dve.wait_ge(o_done, u + 1)
                    if u >= 2:
                        dve.wait_ge(out_done[u % 2], 16 * (u // 2))
                    dve.scalar_tensor_tensor(out=res[:, u % 2, :], in0=p_o[:, :], scalar=c3[:, 6:7],
                                             in1=h1[:, u, :], op0=ALU.mult, op1=ALU.add).then_inc(res_done, 1)
                if t < TILES:
                    dve.wait_ge(h_done, NQ * (t + 1))
                    if t:
                        dve.wait_ge(q3_done, t)
                        dve.wait_ge(res_done, t)
                    link(dve.tensor_tensor(u3[:, :], h[:, :], g3[:, :], ALU.mult))
                    link(dve.tensor_reduce(c3[:, 0:1], u3[:, :], AX.X, ALU.max, apply_absolute_value=True))
                    dve.wait_ge(hss_done, t + 1)
                    link(dve.tensor_scalar(c3[:, 1:2], hss[:, 0:1], 1.0 / HIDDEN, EPS_BIT, ALU.mult, ALU.add))
                    n = newton_rsqrt(dve, chain, n, c3[:, 2:3], c3[:, 1:2], c3[:, 3:4])
                    link(dve.tensor_scalar(c3[:, 4:5], c3[:, 0:1], c3[:, 2:3], 1e-4, ALU.mult, ALU.max))
                    link(dve.tensor_tensor(c3[:, 6:7], c3[:, 4:5], ath[:, 2:3], ALU.mult))
                    link(dve.reciprocal(c3[:, 5:6], c3[:, 4:5]))
                    link(dve.tensor_scalar(c3[:, 5:6], c3[:, 5:6], 127.0, c3[:, 2:3], ALU.mult, ALU.mult))
                    dve.tensor_scalar(u3[:, :], u3[:, :], c3[:, 5:6], MAGIC, ALU.mult, ALU.add).then_inc(u3_done, 1)
                    if t + 1 < TILES:
                        prepare(t + 1)


def build(nc, d):
    d = dict(d)
    d["resid"] = nc.dram_tensor("resid_scratch", [TILES, P, DIM], F32, kind="Internal").ap()
    d["cum"] = nc.dram_tensor("cum_scratch", [2, HEADS, TOKENS], F32, kind="Internal").ap()
    with ExitStack() as ctx:
        def sb(name, shape, dt=F32):
            return ctx.enter_context(nc.sbuf_tensor(name, shape, dt))

        TC = TILES * HEADS
        k = {
            "acc": sb("acc", [P, TILES, DIM]),
            "w_sum": sb("w_sum", [P, 12]),
            "y_sq": sb("y_sq", [P, TILES * GROUPS]),
            "ident": sb("ident_f", [P, P]),
            "ident_b": sb("ident_b", [P, P], BF16),
        }
        with ExitStack() as inner:
            def sbi(name, shape, dt=F32):
                return inner.enter_context(nc.sbuf_tensor(name, shape, dt))

            k.update({
                "x_hi": sbi("x_hi", [P, KT, TOKENS], F32R),
                "x_lo": sbi("x_lo", [P, KT, TOKENS], F32R),
                "b_tok": sbi("b_tok", [P, TILES, P]),
                "c_t": sbi("c_t", [P, TOKENS]),
                "cb": sbi("cb", [P, TILES, P]),
                "e_cum": sbi("e_cum", [P, TC]),
                "e_all": sbi("e_all", [P, TC]),
                "e_rest": sbi("e_rest", [P, TC]),
                "d_row": sbi("d_row", [P, HEADS]),
                "params": sbi("params", [P, GROUPS, 18]),
                "neg_mask": sbi("neg_mask", [P, P], BF16),
                "rows": sbi("rows", [10, 2, GH * P], F32R),
                "cols": sbi("cols", [10, 2, P], F32R),
            })
            embed(nc, d, k)
            decays(nc, d, k)
            mixer(nc, d, k)
        ffn(nc, d, k)


def layouts(x, L0_tok_W, L0_tok_delta_values, L0_tok_token_indices, L0_attn_norm_w, L0_attn_in_proj_w,
            L0_attn_conv_w, L0_attn_conv_b, L0_attn_dt_bias, L0_attn_A_log, L0_attn_D_param,
            L0_attn_inner_norm_w, L0_attn_out_proj_w, L0_attn_conv_state, L0_attn_ssm_state,
            L0_ffn_w1, L0_ffn_g1, L0_ffn_w2, L0_ffn_g2, L0_ffn_w3, L0_ffn_g3):
    c = np.ascontiguousarray
    w = np.asarray(L0_attn_in_proj_w)
    turned = c(w.T).reshape(KT, P, w.shape[0]).transpose(1, 0, 2)
    z, xc = turned[:, :, :INNER], turned[:, :, INNER:2 * INNER]
    w_in = np.stack([xc.reshape(P, KT, GROUPS, GT, P), z.reshape(P, KT, GROUPS, GT, P)], 3)
    w_in = w_in.transpose(2, 3, 4, 0, 1, 5).reshape(GROUPS, 2 * GT, P, KT * P)
    at = 2 * INNER
    w_bcd = np.concatenate([turned[:, :, at:at + 2 * STATE], turned[:, :, at + 2 * STATE:],
                            turned[:, :, :P - HEADS]], 2)
    per_channel = np.concatenate([np.asarray(L0_attn_conv_w), np.asarray(L0_attn_conv_b)[:, None],
                                  np.asarray(L0_attn_inner_norm_w)[:, None]], 1)
    params = np.concatenate([per_channel.reshape(GROUPS, GT, P, 6).transpose(2, 0, 1, 3).reshape(P, GROUPS, 12),
                             np.asarray(L0_attn_conv_state)[0].reshape(GROUPS, GT, P, 3).transpose(2, 0, 1, 3)
                             .reshape(P, GROUPS, 6)], 2)
    kmajor = lambda a, n: c(np.asarray(a).T).reshape(n, P, -1).transpose(1, 0, 2).reshape(P, -1, WCOLS).transpose(1, 0, 2)
    first = np.asarray(L0_attn_ssm_state)[0].reshape(GROUPS, GH, STATE, HEAD).transpose(0, 2, 1, 3)
    i = np.arange(P)
    rows = np.zeros((10, 2, GH, P), np.float32)
    cols = np.zeros((10, 2, P), np.float32)
    cols[0:2] = 1.0
    for part in range(2):
        for h in range(GH):
            rows[2 + part * GH + h, :, h, :] = -1.0
    return {
        "id_col": c(np.asarray(x).reshape(TILES, P).T),
        "id_row": c(np.asarray(x).reshape(TOKENS)),
        "tok": c(np.asarray(L0_tok_token_indices).reshape(TRAINED, 1)),
        "delta": c(np.asarray(L0_tok_delta_values).reshape(DIM, TRAINED).T),
        "W": c(np.asarray(L0_tok_W)),
        "norm_w": c(np.asarray(L0_attn_norm_w)),
        "w_in": c(w_in), "w_bcd": c(w_bcd), "params": c(params),
        "w_out": c(np.asarray(L0_attn_out_proj_w).T).reshape(GROUPS, GT, P, DIM),
        "dt_bias": c(np.asarray(L0_attn_dt_bias).reshape(HEADS, 1)),
        "a_log": c(np.asarray(L0_attn_A_log).reshape(HEADS, 1)),
        "D": c(np.asarray(L0_attn_D_param)),
        "h_first": c(first),
        "w_ffn": c(np.concatenate([kmajor(L0_ffn_w1, KT), kmajor(L0_ffn_w2, KT), kmajor(L0_ffn_w3, HT)], 0)),
        "g12": c(np.stack([np.asarray(L0_ffn_g1), np.asarray(L0_ffn_g2)])),
        "g3": c(np.asarray(L0_ffn_g3)),
        "ident": np.eye(P, dtype=np.float32),
        "ones": np.ones((P, P), np.float32),
        "tri": (i[:, None] <= i[None, :]).astype(np.float32),
        "neg_mask": np.where(i[:, None] <= i[None, :], 0.0, -1e38).astype(np.float32),
        "pick_last": np.broadcast_to((i == P - 1)[:, None], (P, P)).astype(np.float32),
        "keep": (np.arange(TOKENS) % P != 0).astype(np.float32),
        "rows": rows.reshape(10, 2, GH * P), "cols": cols,
    }


def kernel(**inputs):
    import concourse.bacc as bacc
    from concourse.bass_utils import run_bass_kernel_spmd

    nc = bacc.Bacc("TRN2", target_bir_lowering=False, num_devices=1)
    arrays, d = {}, {}
    for name, a in layouts(**inputs).items():
        a = np.ascontiguousarray(a)
        arrays[f"in_{name}"] = a
        d[name] = nc.dram_tensor(f"in_{name}", a.shape, mybir.dt.from_np(a.dtype), kind="ExternalInput").ap()
    d["out"] = nc.dram_tensor("out_dram", [TOKENS, DIM], F32, kind="ExternalOutput").ap()
    build(nc, d)
    result = run_bass_kernel_spmd(nc, [arrays], core_ids=[0])
    return result.results[0]["out_dram"].reshape(BATCH, SEQ, DIM)
```

```python
from contextlib import ExitStack

import numpy as np

import concourse.bass as bass
from concourse import mybir

F32 = mybir.dt.float32
F32R = mybir.dt.float32r
BF16 = mybir.dt.bfloat16
I32 = mybir.dt.int32
ALU = mybir.AluOpType
ACT = mybir.ActivationFunctionType
AX = mybir.AxisListType

P = 128
VOCAB, DIM, TRAINED = 32000, 512, 64
BATCH, SEQ = 4, 512
TOKENS = BATCH * SEQ
TILES = TOKENS // P
KT = DIM // P
HEADS, HEAD, STATE, TAPS = 48, 64, 128, 4
INNER = HEADS * HEAD
GH = 4
GC = GH * HEAD
GROUPS = HEADS // GH
GT = GC // P
CHUNKS = SEQ // P
SLOTS = BATCH * CHUNKS
HIDDEN = 2048
HT = HIDDEN // P
EPS_NORM, EPS_RMS, EPS_BIT = 1e-5, 1e-5, 1e-8
MAGIC = 12582912.0
RSQRT_GUESS = 1597463007.0
WCOLS = 2048


def newton_rsqrt(eng, sem, count, y, v, t, steps=3):
    def link(ins):
        nonlocal count
        count += 1
        ins.then_inc(sem, 1)
        eng.wait_ge(sem, count)

    link(eng.tensor_scalar(t.bitcast(I32), v.bitcast(I32), 1, None, ALU.logical_shift_right))
    link(eng.tensor_scalar(y.bitcast(I32), t.bitcast(I32), -1.0, RSQRT_GUESS, ALU.mult, ALU.add))
    for _ in range(steps):
        link(eng.tensor_tensor(t, y, y, ALU.mult))
        link(eng.scalar_tensor_tensor(out=t, in0=t, scalar=-0.5, in1=v, op0=ALU.mult, op1=ALU.mult))
        link(eng.scalar_tensor_tensor(out=y, in0=t, scalar=1.5, in1=y, op0=ALU.add, op1=ALU.mult))
    return count


def embed(nc, d, k):
    with ExitStack() as ctx:
        def sb(name, shape, dt=F32):
            return ctx.enter_context(nc.sbuf_tensor(name, shape, dt))

        def sem(name):
            return ctx.enter_context(nc.semaphore(name))

        id_row = k["b_tok"][0:TRAINED, :, :].rearrange("p t c -> p (t c)").bitcast(I32)
        row_f = k["c_t"][0:TRAINED, :]
        row_wrap = k["cb"][0:TRAINED, :, :].rearrange("p t c -> p (t c)")
        hit = sb("hit", [TRAINED, TOKENS], BF16)
        id_col = sb("id_col", [P, TILES], I32)
        col_f = sb("col_f", [P, TILES])
        col_wrap = sb("col_wrap", [P, TILES])
        row_id = sb("row_id", [P, TILES], I32)
        tok = sb("tok", [TRAINED, 1], I32)
        tok_f = sb("tok_f", [TRAINED, 1])
        tok_wrap = sb("tok_wrap", [TRAINED, 1])
        delta = sb("delta", [TRAINED, DIM])
        delta_rest = sb("delta_rest", [TRAINED, DIM])
        delta_parts = sb("delta_parts", [TRAINED, 3, DIM], BF16)
        norm_row = sb("norm_row", [P, DIM])
        stats = sb("stats", [P, TILES, 6])
        mv = sb("mv", [P, TILES, 2])
        names = ("var", "rstd", "ms", "rrms", "tmp_c", "shift")
        var, rstd, ms, rrms, tmp, shift = (sb(n, [P, TILES]) for n in names)
        x1 = sb("x1", [P, 4, DIM])
        resid = sb("resid", [P, 2, DIM])
        xs = sb("xs", [P, 2, DIM])
        w_raw = sb("w_raw", [P, 2, WCOLS])
        p_delta = [ctx.enter_context(nc.psum_tensor(f"p_delta{i}", [P, DIM], F32)) for i in range(4)]
        p_xt = [ctx.enter_context(nc.psum_tensor(f"p_xt{i}", [P, KT, P], F32)) for i in range(2)]

        loaded, ids_ready, chain = sem("em_loaded"), sem("em_ids"), sem("em_chain")
        hit_ready, delta_done = sem("em_hit"), sem("em_delta")
        gathered = [sem(f"em_gathered{i}") for i in range(4)]
        bcd_loaded, bcd_hi_done, stats_ready = sem("em_bcd"), sem("em_bcdhi"), sem("em_stats")
        added, x1_ready, resid_ready, xs_ready = sem("em_added"), sem("em_x1"), sem("em_resid"), sem("em_xs")
        resid_stored = [sem(f"em_stored{i}") for i in range(2)]
        xt_done, hi_done, lo_done = sem("em_xt"), sem("em_hi"), sem("em_lo")
        w_loaded = [sem(f"em_w{i}") for i in range(2)]
        w_summed = sem("em_wsum")
        h0 = k["acc"]
        n_w = 3 * HIDDEN * DIM // P // WCOLS
        QT = TILES // 4
        block = ctx.enter_context(nc.Block())

        @block.sync
        def _(sp):
            sp.dma_start(id_col[:, :], d["id_col"]).then_inc(loaded, 16)
            sp.dma_start(tok[:, :], d["tok"]).then_inc(loaded, 16)
            sp.dma_start(id_row, d["id_row"].partition_broadcast(TRAINED)).then_inc(loaded, 16)
            sp.dma_start(delta[:, :], d["delta"]).then_inc(loaded, 16)
            sp.dma_start(norm_row[:, :], d["norm_w"].partition_broadcast(P)).then_inc(loaded, 16)
            sp.dma_start(k["ident"][:, :], d["ident"]).then_inc(loaded, 16)
            sp.dma_start(k["bcd_raw"][:, :, :], d["w_bcd"]).then_inc(bcd_loaded, 16)
            def chunk(n):
                if n >= 2:
                    sp.wait_ge(w_summed, n - 1)
                sp.dma_start(w_raw[:, n % 2, :], d["w_ffn"][n]).then_inc(w_loaded[n % 2], 16)

            for n in range(n_w - 2):
                chunk(n)
            for t in range(TILES):
                sp.wait_ge(resid_ready, t + 1)
                sp.dma_start(d["resid"][t], resid[:, t % 2, :]).then_inc(resid_stored[t % 2], 16)
                if t in (3, 7):
                    chunk(n_w - 2 + t // 4)
            for i in range(2):
                sp.wait_ge(resid_stored[i], 16 * TILES // 2)

        @block.gpsimd
        def _(pool):
            pool.wait_ge(ids_ready, 1)
            for t in range(TILES):
                pool.indirect_dma_start(out=h0[:, t, :], out_offset=None, in_=d["W"],
                                        in_offset=bass.IndirectOffsetOnAxis(ap=row_id[:, t:t + 1], axis=0)
                                        ).then_inc(gathered[t // QT], 16)
            for t in range(TILES):
                pool.wait_ge(x1_ready, t + 1)
                if t >= 2:
                    pool.wait_ge(resid_stored[t % 2], 16 * (t // 2))
                pool.tensor_tensor(resid[:, t % 2, :], h0[:, t, :], x1[:, t % 4, :], ALU.add
                                   ).then_inc(resid_ready, 1)

        @block.scalar
        def _(act):
            act.wait_ge(bcd_loaded, 16)
            act.activation(k["bcd_hi"][:, :, :], k["bcd_raw"][:, :, :], ACT.Identity).then_inc(bcd_hi_done, 1)

            def sizes(n):
                act.wait_ge(w_loaded[n % 2], 16 * (n // 2 + 1))
                act.activation(w_raw[:, n % 2, :], w_raw[:, n % 2, :], ACT.Abs,
                               accum_out=k["w_sum"][:, n:n + 1]).then_inc(w_summed, 1)

            def normalised(t):
                if t >= 4:
                    act.wait_ge(xs_ready, t - 3)
                    act.wait_ge(resid_ready, t - 3)
                act.activation(x1[:, t % 4, :], h0[:, t, :], ACT.Identity, scale=rstd[:, t:t + 1],
                               bias=shift[:, t:t + 1]).then_inc(x1_ready, 1)

            for n in range(n_w - 4):
                sizes(n)
            act.wait_ge(stats_ready, 1)
            normalised(0)
            normalised(1)
            for t in range(TILES):
                act.wait_ge(xt_done, t + 1)
                act.activation(k["x_hi"][:, :, t * P:(t + 1) * P], p_xt[t % 2][:, :, :], ACT.Identity
                               ).then_inc(hi_done, 1)
                if t + 2 < TILES:
                    normalised(t + 2)
                if t % 4 == 1:
                    sizes(n_w - 4 + t // 4)

        @block.tensor
        def _(pe):
            pe.wait_ge(hit_ready, 1)
            for t in range(TILES):
                if t >= 4:
                    pe.wait_ge(added, t - 3)
                for i in range(3):
                    last = pe.matmul(p_delta[t % 4][:, :], hit[:, t * P:(t + 1) * P], delta_parts[:, i, :],
                                     start=(i == 0), stop=(i == 2))
                last.then_inc(delta_done, 1)
            for t in range(TILES):
                pe.wait_ge(xs_ready, t + 1)
                if t >= 2:
                    pe.wait_ge(lo_done, t - 1)
                for j in range(KT):
                    last = pe.transpose(p_xt[t % 2][:, j, :], xs[:, t % 2, j * P:(j + 1) * P],
                                        k["ident"][:, :])
                last.then_inc(xt_done, 1)

        @block.vector
        def _(dve):
            n = 0

            def link(ins):
                nonlocal n
                n += 1
                ins.then_inc(chain, 1)
                dve.wait_ge(chain, n)

            def wrapped(f, wrap, ints):
                link(dve.tensor_copy(f, ints))
                link(dve.tensor_scalar(wrap, f, 0.0, float(VOCAB), ALU.is_lt, ALU.mult))
                link(dve.tensor_tensor(f, f, wrap, ALU.add))

            dve.wait_ge(loaded, 6 * 16)
            wrapped(col_f[:, :], col_wrap[:, :], id_col[:, :])
            link(dve.tensor_scalar(col_f[:, :], col_f[:, :], 0.0, float(VOCAB - 1), ALU.max, ALU.min))
            dve.tensor_copy(row_id[:, :], col_f[:, :]).then_inc(ids_ready, 1)
            wrapped(tok_f[:, :], tok_wrap[:, :], tok[:, :])
            link(dve.tensor_copy(delta_parts[:, 0, :], delta[:, :]))
            link(dve.tensor_tensor(delta_rest[:, :], delta[:, :], delta_parts[:, 0, :], ALU.subtract))
            link(dve.tensor_copy(delta_parts[:, 1, :], delta_rest[:, :]))
            link(dve.tensor_tensor(delta_parts[:, 2, :], delta_rest[:, :], delta_parts[:, 1, :], ALU.subtract))
            wrapped(row_f, row_wrap, id_row)
            link(dve.tensor_scalar(row_f, row_f, 0.0, float(VOCAB - 1), ALU.max, ALU.min))
            dve.tensor_scalar(hit[:, :], row_f, tok_f[:, 0:1], None, ALU.is_equal).then_inc(hit_ready, 1)
            dve.wait_ge(bcd_hi_done, 1)
            dve.tensor_tensor(k["bcd_lo"][:, :, :], k["bcd_raw"][:, :, :], k["bcd_hi"][:, :, :], ALU.subtract)
            for t in range(TILES):
                if t % QT == 0:
                    dve.wait_ge(gathered[t // QT], 16 * QT)
                dve.wait_ge(delta_done, t + 1)
                dve.tensor_tensor(h0[:, t, :], h0[:, t, :], p_delta[t % 4][:, :], ALU.add).then_inc(added, 1)
                if t:
                    dve.wait_ge(added, t)
                    dve.bn_stats(stats[:, t - 1, :], h0[:, t - 1, :]).then_inc(chain, 1)
                    n += 1
            dve.wait_ge(added, TILES)
            link(dve.bn_stats(stats[:, TILES - 1, :], h0[:, TILES - 1, :]))
            for t in range(TILES):
                dve.bn_aggr(mv[:, t, :], stats[:, t, :]).then_inc(chain, 1)
            n += TILES
            dve.wait_ge(chain, n)
            link(dve.tensor_scalar(var[:, :], mv[:, :, 1], EPS_NORM, None, ALU.add))
            n = newton_rsqrt(dve, chain, n, rstd[:, :], var[:, :], tmp[:, :])
            link(dve.tensor_tensor(ms[:, :], rstd[:, :], rstd[:, :], ALU.mult))
            link(dve.tensor_tensor(ms[:, :], ms[:, :], mv[:, :, 1], ALU.mult))
            link(dve.tensor_scalar(ms[:, :], ms[:, :], EPS_RMS, None, ALU.add))
            dve.scalar_tensor_tensor(out=shift[:, :], in0=mv[:, :, 0], scalar=-1.0, in1=rstd[:, :],
                                     op0=ALU.mult, op1=ALU.mult).then_inc(stats_ready, 1)
            n = newton_rsqrt(dve, chain, n, rrms[:, :], ms[:, :], tmp[:, :])
            for t in range(TILES + 1):
                if t < TILES:
                    dve.wait_ge(x1_ready, t + 1)
                    if t >= 2:
                        dve.wait_ge(xt_done, t - 1)
                    dve.scalar_tensor_tensor(out=xs[:, t % 2, :], in0=x1[:, t % 4, :], scalar=rrms[:, t:t + 1],
                                             in1=norm_row[:, :], op0=ALU.mult, op1=ALU.mult).then_inc(xs_ready, 1)
                if t >= 1:
                    u = t - 1
                    dve.wait_ge(hi_done, u + 1)
                    dve.tensor_tensor(k["x_lo"][:, :, u * P:(u + 1) * P], p_xt[u % 2][:, :, :],
                                      k["x_hi"][:, :, u * P:(u + 1) * P], ALU.subtract).then_inc(lo_done, 1)


def decays(nc, d, k):
    with ExitStack() as ctx:
        def sb(name, shape, dt=F32):
            return ctx.enter_context(nc.sbuf_tensor(name, shape, dt))

        def sem(name):
            return ctx.enter_context(nc.semaphore(name))

        TC = TILES * HEADS
        w_hi, w_lo = k["bcd_hi"], k["bcd_lo"]
        b_t = sb("b_t", [P, TOKENS])
        dt_pre = sb("dt_pre", [HEADS, TOKENS])
        soft = sb("soft", [HEADS, TOKENS])
        cum = sb("cum", [HEADS, TOKENS])
        cum_hi = sb("cum_hi", [HEADS, TOKENS], F32R)
        cum_lo = sb("cum_lo", [HEADS, TOKENS], F32R)
        cum_tok = sb("cum_tok", [P, TC])
        tri = sb("tri", [P, P])
        pick_last = sb("pick_last", [P, P])
        dt_bias = sb("dt_bias", [HEADS, 1])
        a_log = sb("a_log", [HEADS, 1])
        neg_a = sb("neg_a", [HEADS, 1])
        neg_mask_f = sb("neg_mask_f", [P, P])
        ones = k["c_t"][:, 0:P]
        sum3, s3, den = (sb(n, [P, 3]) for n in ("sum3", "s3", "den"))
        rows_f = soft[0:10, 0:2 * GH * P].rearrange("r (n c) -> r n c", n=2)
        cols_f = soft[0:10, 2 * GH * P:2 * GH * P + 2 * P].rearrange("r (n c) -> r n c", n=2)
        p_proj = [ctx.enter_context(nc.psum_tensor(f"p_bcd{i}", [P, SEQ], F32)) for i in range(2)]
        p_cb = ctx.enter_context(nc.psum_tensor("p_cb", [P, 4, P], F32))
        p_bt = ctx.enter_context(nc.psum_tensor("p_bt", [P, 4, P], F32))
        p_ct = [ctx.enter_context(nc.psum_tensor(f"p_ct{i}", [P, 512], F32)) for i in range(2)]
        p_cq = [ctx.enter_context(nc.psum_tensor(f"p_cq{i}", [P, 512], F32)) for i in range(2)]
        HC = TC // 2

        loaded, biases = sem("bd_loaded"), sem("bd_biases")
        proj_done, evicted_a, evicted_v = sem("bd_proj"), sem("bd_eva"), sem("bd_evv")
        steps_a, steps_v, consts = sem("bd_sa"), sem("bd_sv"), sem("bd_consts")
        cb_done, cb_masked, bt_done, bt_copied = sem("bd_cb"), sem("bd_cbm"), sem("bd_bt"), sem("bd_btc")
        cum_ready, hi_ready, lo_ready, stored = sem("bd_cum"), sem("bd_hi"), sem("bd_lo"), sem("bd_stored")
        ct_done, tok_ready, cq_done, diff_ready = sem("bd_ct"), sem("bd_tok"), sem("bd_cq"), sem("bd_diff")
        keep_in, zeroed = sem("bd_keep"), sem("bd_zero")
        sizes, mean_done, ln_in, ln_done = sem("bd_sizes"), sem("bd_mean"), sem("bd_lnin"), sem("bd_ln")
        block = ctx.enter_context(nc.Block())

        @block.sync
        def _(sp):
            for to, of in ((dt_bias[:, :], d["dt_bias"]), (a_log[:, :], d["a_log"])):
                sp.dma_start(to, of).then_inc(biases, 16)
            for to, of in ((ones, d["ones"]), (tri[:, :], d["tri"]),
                           (pick_last[:, :], d["pick_last"]), (neg_mask_f[:, :], d["neg_mask"]),
                           (rows_f, d["rows"]), (cols_f, d["cols"]),
                           (k["d_row"][:, :], d["D"].partition_broadcast(P)),
                           (k["params"][:, :, :], d["params"])):
                sp.dma_start(to, of).then_inc(loaded, 16)
            sp.wait_ge(steps_v, 1)
            sp.dma_start(dt_pre[:, :], d["keep"].partition_broadcast(HEADS)).then_inc(keep_in, 16)
            sp.wait_ge(hi_ready, 1)
            sp.dma_start(d["cum"][0], cum_hi[:, :].bitcast(F32)).then_inc(stored, 16)
            sp.wait_ge(lo_ready, 1)
            sp.dma_start(d["cum"][1], cum_lo[:, :].bitcast(F32)).then_inc(stored, 16)
            sp.wait_ge(stored, 32)

        @block.gpsimd
        def _(pool):
            pool.memset(k["acc"][:, :, :], 0.0).then_inc(zeroed, 1)

        @block.tensor
        def _(pe):
            def project(n, b, j):
                if n >= 2:
                    pe.wait_ge(*bank_read[n - 2])
                i = 0
                for w, x in ((w_hi, k["x_hi"]), (w_hi, k["x_lo"]), (w_lo, k["x_hi"])):
                    for c in range(KT):
                        last = pe.matmul(p_proj[n % 2][:, :], w[:, c, j * P:(j + 1) * P],
                                         x[:, c, b * SEQ:(b + 1) * SEQ], start=(i == 0), stop=(i == 3 * KT - 1))
                        i += 1
                last.then_inc(proj_done, 1)

            bank_read = [(evicted_a, b + 1) for b in range(BATCH)]
            for b in range(BATCH):
                bank_read += [(evicted_a, BATCH + b + 1), (evicted_v, b + 1)]
            for b in range(BATCH):
                project(b, b, 2)
            pe.wait_ge(sizes, 1)
            pe.matmul(p_cq[0][:, 0:3], ones, sum3[:, :], start=True, stop=True).then_inc(mean_done, 1)
            for b in range(BATCH):
                for j in range(2):
                    project(BATCH + 2 * b + j, b, j)
                if b == 1:
                    pe.wait_ge(cum_ready, 1)
                    for t in range(TILES):
                        h, c = t // (TILES // 2), t % (TILES // 2)
                        last = pe.transpose(p_ct[h][:, c * HEADS:(c + 1) * HEADS], cum[:, t * P:(t + 1) * P],
                                            k["ident"][0:HEADS, 0:HEADS])
                    last.then_inc(ct_done, 1)
                if b:
                    pe.wait_ge(cb_masked, b)
                    pe.wait_ge(bt_copied, b)
                pe.wait_ge(evicted_a, BATCH + b + 1)
                pe.wait_ge(evicted_v, b + 1)
                for q in range(CHUNKS):
                    at = slice((b * CHUNKS + q) * P, (b * CHUNKS + q + 1) * P)
                    last = pe.matmul(p_cb[:, q, :], b_t[:, at], k["c_t"][:, at], start=True, stop=True)
                last.then_inc(cb_done, 1)
                for q in range(CHUNKS):
                    at = slice((b * CHUNKS + q) * P, (b * CHUNKS + q + 1) * P)
                    last = pe.transpose(p_bt[:, q, :], b_t[:, at], k["ident"][:, :])
                last.then_inc(bt_done, 1)
            pe.wait_ge(tok_ready, 2)
            pe.wait_ge(ln_in, 1)
            for h in range(2):
                last = pe.matmul(p_cq[h][:, 0:HC], pick_last[:, :], cum_tok[:, h * HC:(h + 1) * HC],
                                 start=True, stop=True)
            last.then_inc(cq_done, 1)

        @block.scalar
        def _(act):
            act.wait_ge(biases, 2 * 16)
            act.activation(neg_a[:, :], a_log[:, :], ACT.Exp).then_inc(steps_a, 1)
            for b in range(BATCH):
                at = slice(b * SEQ, (b + 1) * SEQ)
                act.wait_ge(proj_done, b + 1)
                act.activation(dt_pre[:, at], p_proj[b % 2][0:HEADS, :], ACT.Identity,
                               bias=dt_bias[:, 0:1]).then_inc(evicted_a, 1)
            act.wait_ge(evicted_a, BATCH)
            act.wait_ge(consts, 4)
            act.activation(soft[:, :], dt_pre[:, :], ACT.Abs).then_inc(steps_a, 1)
            act.wait_ge(steps_a, 2)
            act.activation(soft[:, :], soft[:, :], ACT.Exp, scale=-1.0).then_inc(steps_a, 1)
            act.wait_ge(steps_a, 3)
            act.activation(soft[:, :], soft[:, :], ACT.Ln, bias=1.0).then_inc(steps_a, 1)
            act.wait_ge(ln_in, 1)
            act.activation(k["ath"][:, :], den[:, :], ACT.Ln).then_inc(ln_done, 1)
            for b in range(BATCH):
                act.wait_ge(proj_done, BATCH + 2 * b + 1)
                act.activation(b_t[:, b * SEQ:(b + 1) * SEQ], p_proj[0][:, :], ACT.Identity).then_inc(evicted_a, 1)
                if b == 1:
                    act.wait_ge(cum_ready, 1)
                    act.activation(cum_hi[:, :], cum[:, :], ACT.Identity).then_inc(hi_ready, 1)
                act.wait_ge(bt_done, b + 1)
                act.activation(k["b_tok"][:, b * CHUNKS:(b + 1) * CHUNKS, :], p_bt[:, :, :], ACT.Identity
                               ).then_inc(bt_copied, 1)
                if b == 1:
                    act.wait_ge(tok_ready, 2)
                    act.activation(k["e_cum"][:, :], cum_tok[:, :], ACT.Exp)
            act.wait_ge(cq_done, 1)
            for h in range(2):
                act.activation(k["e_all"][:, h * HC:(h + 1) * HC], p_cq[h][:, 0:HC], ACT.Exp).then_inc(steps_a, 1)
            act.wait_ge(diff_ready, 2)
            act.activation(k["e_rest"][:, :], k["e_rest"][:, :], ACT.Exp)

        @block.vector
        def _(dve):
            dve.wait_ge(loaded, 8 * 16)
            dve.tensor_copy(k["ident_b"][:, :], k["ident"][:, :]).then_inc(consts, 1)
            dve.tensor_copy(k["neg_mask"][:, :], neg_mask_f[:, :]).then_inc(consts, 1)
            dve.tensor_copy(k["rows"][:, :, :], rows_f).then_inc(consts, 1)
            dve.tensor_copy(k["cols"][:, :, :], cols_f).then_inc(consts, 1)
            dve.tensor_reduce(sum3[:, :], k["w_sum"][:, :].rearrange("p (w c) -> p w c", w=3), AX.X, ALU.add
                              ).then_inc(sizes, 1)
            dve.wait_ge(mean_done, 1)
            dve.tensor_scalar(s3[:, :], p_cq[0][:, 0:3], 1.0 / (HIDDEN * DIM), None, ALU.mult).then_inc(sizes, 1)
            dve.wait_ge(sizes, 2)
            dve.tensor_scalar(k["inv3"][:, :], s3[:, :], EPS_BIT, None, ALU.add).then_inc(sizes, 1)
            dve.tensor_scalar(den[:, :], s3[:, :], -1.0, 1.0, ALU.mult, ALU.add).then_inc(sizes, 1)
            dve.wait_ge(sizes, 4)
            dve.reciprocal(k["inv3"][:, :], k["inv3"][:, :])
            dve.reciprocal(den[:, :], den[:, :]).then_inc(sizes, 1)
            dve.wait_ge(sizes, 5)
            dve.scalar_tensor_tensor(out=den[:, :], in0=s3[:, :], scalar=1.0, in1=den[:, :],
                                     op0=ALU.add, op1=ALU.mult).then_inc(ln_in, 1)
            dve.wait_ge(ln_done, 1)
            dve.tensor_scalar(k["ath"][:, :], k["ath"][:, :], 0.5 / 127.0, None, ALU.mult)
            dve.wait_ge(steps_a, 4)
            dve.scalar_tensor_tensor(out=soft[:, :], in0=dt_pre[:, :], scalar=0.0, in1=soft[:, :],
                                     op0=ALU.max, op1=ALU.add).then_inc(steps_v, 1)

            def copy_c(b):
                dve.wait_ge(proj_done, BATCH + 2 * b + 2)
                dve.tensor_copy(k["c_t"][:, b * SEQ:(b + 1) * SEQ], p_proj[1][:, :]).then_inc(evicted_v, 1)

            def mask_cb(b):
                dve.wait_ge(cb_done, b + 1)
                dve.tensor_tensor(k["cb"][:, b * CHUNKS:(b + 1) * CHUNKS, :], p_cb[:, :, :],
                                  tri[:, :].unsqueeze(1).to_broadcast([P, CHUNKS, P]), ALU.mult
                                  ).then_inc(cb_masked, 1)

            dve.wait_ge(steps_v, 1)
            dve.tensor_scalar(soft[:, :], soft[:, :], neg_a[:, 0:1], -1.0, ALU.mult, ALU.mult).then_inc(steps_v, 1)
            copy_c(0)
            dve.wait_ge(steps_v, 2)
            dve.wait_ge(keep_in, 16)
            dve.tensor_tensor_scan(cum[:, :], dt_pre[:, :], soft[:, :], 0.0, ALU.mult, ALU.add).then_inc(cum_ready, 1)
            mask_cb(0)
            copy_c(1)
            dve.wait_ge(ct_done, 1)
            for h in range(2):
                dve.tensor_copy(cum_tok[:, h * HC:(h + 1) * HC], p_ct[h][:, 0:HC]).then_inc(tok_ready, 1)
            mask_cb(1)
            dve.wait_ge(hi_ready, 1)
            dve.tensor_tensor(cum_lo[:, :], cum[:, :], cum_hi[:, :], ALU.subtract).then_inc(lo_ready, 1)
            for b in (2, 3):
                copy_c(b)
                mask_cb(b)
            dve.wait_ge(tok_ready, 2)
            dve.wait_ge(steps_a, 6)
            for h in range(2):
                dve.tensor_tensor(k["e_rest"][:, h * HC:(h + 1) * HC], p_cq[h][:, 0:HC],
                                  cum_tok[:, h * HC:(h + 1) * HC], ALU.subtract).then_inc(diff_ready, 1)


def count(per_group, g, local):
    return g * per_group + local


def mixer(nc, d, k):
    with ExitStack() as ctx:
        def sb(name, shape, dt=F32):
            return ctx.enter_context(nc.sbuf_tensor(name, shape, dt))

        def sem(name):
            return ctx.enter_context(nc.semaphore("mx_" + name))

        stage = sb("stage", [P, 2, DIM])
        wi_hi = sb("wi_hi", [P, 2 * GT, KT, P], F32R)
        wi_lo = sb("wi_lo", [P, 2 * GT, KT, P], F32R)
        wo_hi = sb("wo_hi", [P, GT, DIM], F32R)
        wo_lo = sb("wo_lo", [P, GT, DIM], F32R)
        half = sb("half", [P, 12])
        d_now = sb("d_now", [P, GH])
        all_now = sb("all_now", [P, TILES, GH])
        pad = sb("pad", [P, GT, TAPS - 1 + SEQ])
        conv = sb("conv", [P, GT, SEQ])
        th_x = sb("th_x", [P, SEQ])
        z2 = sb("z2", [P, 2, GT, SEQ])
        x_tok = sb("x_tok", [P, 2, CHUNKS, GC])
        m_t = sb("m_t", [P, 2, GH, P])
        x_dec = sb("x_dec", [P, GH, HEAD])
        xd = sb("xd", [P, GH, HEAD])
        y = sb("y", [P, 2, GC])
        h_first = sb("h_first", [P, GH, HEAD])
        h_next = sb("h_next", [P, GH, HEAD])
        h_dec = sb("h_dec", [P, GH, HEAD])
        sq = sb("sq", [P, GC], BF16)
        gate = sb("gate", [P, GT, P])
        g_hi = sb("g_hi", [P, 2, GT, P], F32R)
        g_lo = sb("g_lo", [P, 2, GT, P], F32R)

        def bank(name, shape):
            return ctx.enter_context(nc.psum_tensor(name, shape, F32))

        p_proj = [bank(f"p_proj{i}", [P, SEQ]) for i in range(2)]
        p_d = bank("p_d", [P, GH, P])
        p_y = bank("p_y", [P, 2, GH, HEAD])
        p_s = bank("p_s", [P, 512])
        p_yt = bank("p_yt", [P, 512])
        p_xt = bank("p_xt", [P, CHUNKS, P])
        p_o = bank("p_o", [P, DIM])

        raw_in = [sem(f"raw_in{i}") for i in range(2)]
        rows_in = [sem(f"rows_in{i}") for i in range(2)]
        h_in = sem("h_in")
        w_hi_done, w_lo_done = sem("w_hi"), sem("w_lo")
        par_done = sem("par")
        tables_done = sem("tables")
        proj_done = sem("proj")
        raw_done, tap_done = sem("raw"), sem("tap")
        conv_done = sem("conv")
        xth_done, zth_done = sem("xth"), sem("zth")
        x_done, z_done = sem("x"), sem("z")
        xt_done, xtok_done = sem("xt"), sem("xtok")
        d_done, e_done, m_done = sem("d"), sem("e"), sem("m")
        y_mm, ys_done, xd_done, yx_done, y_done = sem("y_mm"), sem("ys"), sem("xd"), sem("yx"), sem("y")
        xdec_done, s_done, hdec_done, h_done = sem("xdec"), sem("s"), sem("hdec"), sem("h")
        yt_done, gate_done, ghi_done, glo_done = sem("yt"), sem("gate"), sem("ghi"), sem("glo")
        sq_done, o_done, acc_done = sem("sq"), sem("o"), sem("acc")

        def wait(eng, s, per_group, g, local, unit=1):
            v = count(per_group, g, local)
            if isinstance(v, int) and v <= 0:
                return
            eng.wait_ge(s, v * unit)

        def exists(g, slot):
            return not isinstance(g, int) or 0 <= g * SLOTS + slot < GROUPS * SLOTS

        def groups(eng, body):
            for s in range(-4, SLOTS):
                body(0, s)
            with eng.Fori(1, GROUPS - 1) as g:
                for s in range(SLOTS):
                    body(g, s)
            for s in range(SLOTS + 2):
                body(GROUPS - 1, s)

        def kind(s):
            return (s + 4) // 4, s % 4, s % 4 < GT

        def x_count(i, j):
            return GT * i + j + 1

        def state_count(i, q):
            return (CHUNKS - 1) * i + min(q + 1, CHUNKS - 1)

        block = ctx.enter_context(nc.Block())

        @block.sync
        def _(sp):
            def load_weights(g, n, src):
                wait(sp, w_lo_done, 6, g, 4 + n - 2 + 1)
                sp.dma_start(stage[:, n % 2, :], src).then_inc(raw_in[n % 2], 16)

            def load_rows(g, s):
                wait(sp, d_done, 16, g, s - 1)
                at = slice((s % SLOTS) * P, (s % SLOTS + 1) * P)
                gg = g + s // SLOTS
                heads = bass.ds(gg * GH, GH)
                sp.dma_start(k["rows"][0:2, s % 2, :].bitcast(F32).rearrange("r (h t) -> r h t", h=GH),
                             d["cum"][:, heads, at]).then_inc(rows_in[s % 2], 16)
                for part in range(2):
                    sp.dma_start(k["cols"][2 + part * GH:2 + (part + 1) * GH, s % 2, :].bitcast(F32),
                                 d["cum"][part, heads, at]).then_inc(rows_in[s % 2], 16)

            def body(g, s):
                if s == -4:
                    for n in range(2, 6):
                        load_weights(-1, n, d["w_in"][0, n - 2])
                    sp.dma_start(h_first[:, :, :], d["h_first"][0]).then_inc(h_in, 16)
                    for n in range(2):
                        load_rows(0, n)
                if s == 0:
                    for n in range(2):
                        load_weights(g, n, d["w_out"][g, n])
                if 0 <= s and exists(g, s + 2):
                    load_rows(g, s + 2)
                if s in (4, 5, 8, 9) and exists(g, SLOTS):
                    j = (4, 5, 8, 9).index(s)
                    load_weights(g, j + 2, d["w_in"][g + 1, j])
                if s == 14 and exists(g, SLOTS):
                    wait(sp, y_mm, 16, g, 13)
                    wait(sp, hdec_done, 12, g, 10)
                    sp.dma_start(h_first[:, :, :], d["h_first"][g + 1]).then_inc(h_in, 16)
            groups(sp, body)

        @block.tensor
        def _(pe):
            def split_products(out, w_hi, w_lo, x_hi, x_lo, order=(0, 1, 2)):
                n = len(w_hi)
                for p, k_th in enumerate(order):
                    w, x = ((w_hi, x_hi), (w_hi, x_lo), (w_lo, x_hi))[k_th]
                    for c in range(n):
                        last = pe.matmul(out, w[c], x[c], start=(p == 0 and c == 0),
                                         stop=(p == 2 and c == n - 1))
                return last

            def body(g, s):
                if exists(g, s + 4):
                    i, j, is_x = kind(s)
                    b = i % BATCH
                    if i % BATCH == 0:
                        wait(pe, w_lo_done, 6, g, (6 if i else 0) + j + 1)
                    if is_x:
                        wait(pe, z_done, 8, g, x_count(i - 1, j))
                    else:
                        wait(pe, raw_done, 8, g, x_count(i, j - GT))
                        wait(pe, tap_done, 8, g, x_count(i, j - GT))
                    at = slice(b * SEQ, (b + 1) * SEQ)
                    split_products(p_proj[j % 2][:, :],
                                   [wi_hi[:, j, c, :] for c in range(KT)], [wi_lo[:, j, c, :] for c in range(KT)],
                                   [k["x_hi"][:, c, at] for c in range(KT)], [k["x_lo"][:, c, at] for c in range(KT)]
                                   ).then_inc(proj_done, 1)
                if exists(g, s + 1):
                    wait(pe, e_done, 16, g, s + 1)
                    wait(pe, rows_in[(s + 1) % 2], 24, g, 3 * ((s + 1) // 2 + 1), 16)
                    pe.matmul(p_d[:, :, :], k["cols"][:, (s + 1) % 2, :],
                              k["rows"][:, (s + 1) % 2, :].rearrange("r (h t) -> r h t", h=GH),
                              start=True, stop=False)
                    pe.matmul(p_d[:, :, :], k["ident_b"][:, :],
                              k["neg_mask"][:, :].unsqueeze(1).to_broadcast([P, GH, P]),
                              start=False, stop=True).then_inc(d_done, 1)
                if exists(g, s - 2):
                    wait(pe, glo_done, 16, g, s - 1)
                    wait(pe, acc_done, 16, g, s - 2)
                    if s == 2:
                        wait(pe, w_lo_done, 6, g, 6)
                    o = s % 2
                    split_products(p_o[:, :], [g_hi[:, o, c, :] for c in range(GT)],
                                   [g_lo[:, o, c, :] for c in range(GT)],
                                   [wo_hi[:, c, :] for c in range(GT)], [wo_lo[:, c, :] for c in range(GT)]
                                   ).then_inc(o_done, 1)
                i, q = s // CHUNKS, s % CHUNKS
                if exists(g, s):
                    wait(pe, y_done, 16, g, s)
                    if q == 0:
                        state = h_first
                        if i == 0:
                            wait(pe, h_in, 1, g, 1, 16)
                        wait(pe, xtok_done, 8, g, x_count(i, GT - 1))
                    else:
                        state = h_next
                        wait(pe, h_done, 12, g, state_count(i, q - 1))
                    at = slice((s % SLOTS) * P, (s % SLOTS + 1) * P)
                    pe.matmul(p_y[:, 1, :, :], k["c_t"][:, at], state[:, :, :], start=True, stop=True)
                    wait(pe, m_done, 16, g, s + 1)
                    for h in range(GH):
                        last = pe.matmul(p_y[:, 0, h, :], m_t[:, s % 2, h, :],
                                         x_tok[:, i % 2, q, h * HEAD:(h + 1) * HEAD], start=True, stop=True)
                    last.then_inc(y_mm, 1)
                if q >= 2 and exists(g, s + 4):
                    j = q - 2
                    wait(pe, x_done, 8, g, x_count(i + 1, j))
                    wait(pe, xtok_done, 8, g, x_count(i + 1, j) - 1)
                    for c in range(CHUNKS):
                        last = pe.transpose(p_xt[:, c, :], conv[:, j, c * P:(c + 1) * P], k["ident"][:, :])
                    last.then_inc(xt_done, 1)
                if q < CHUNKS - 1 and exists(g, s):
                    wait(pe, xdec_done, 12, g, state_count(i, q))
                    wait(pe, h_done, 12, g, state_count(i, q) - 1)
                    pe.matmul(p_s[:, 0:GC], k["b_tok"][:, s % SLOTS, :],
                              x_dec[:, :, :].rearrange("p h c -> p (h c)"), start=True, stop=True
                              ).then_inc(s_done, 1)
                if exists(g, s - 1):
                    wait(pe, y_done, 16, g, s)
                    wait(pe, gate_done, 16, g, s - 1)
                    for c in range(GT):
                        last = pe.transpose(p_yt[:, c * P:(c + 1) * P], y[:, (s - 1) % 2, c * P:(c + 1) * P],
                                            k["ident"][:, :])
                    last.then_inc(yt_done, 1)
            groups(pe, body)

        @block.scalar
        def _(act):
            def weight_hi(g, n):
                wait(act, raw_in[n % 2], 3, g, (4 + n) // 2 + 1, 16)
                if n < 2:
                    wait(act, o_done, 16, g, 0)
                    wait(act, par_done, 2, g, 2)
                    act.activation(wo_hi[:, n, :], stage[:, n % 2, :], ACT.Identity,
                                   scale=half[:, 6 * n + 5:6 * n + 6]).then_inc(w_hi_done, 1)
                else:
                    wait(act, proj_done, 16, g, 12 + n - 2 + 1)
                    act.activation(wi_hi[:, n - 2, :, :].rearrange("p c m -> p (c m)"), stage[:, n % 2, :],
                                   ACT.Identity).then_inc(w_hi_done, 1)

            def body(g, s):
                if s == -4:
                    for n in range(2, 6):
                        weight_hi(-1, n)
                if exists(g, s - 2):
                    wait(act, gate_done, 16, g, s - 1)
                    wait(act, o_done, 16, g, s - 3)
                    act.activation(g_hi[:, s % 2, :, :], gate[:, :, :], ACT.Identity).then_inc(ghi_done, 1)
                if exists(g, s - 1):
                    wait(act, y_done, 16, g, s)
                    wait(act, sq_done, 16, g, s - 1)
                    gg = g if s else g - 1
                    at = ((s - 1) % SLOTS) * GROUPS + gg
                    act.activation(sq[:, :], y[:, (s - 1) % 2, :], ACT.Square,
                                   accum_out=k["y_sq"][:, bass.ds(at, 1)]).then_inc(sq_done, 1)
                i, j, is_x = kind(s)
                if exists(g, s + 4):
                    wait(act, proj_done, 16, g, 4 * i + j + 1)
                    if is_x:
                        wait(act, conv_done, 24, g, 3 * x_count(i - 1, j))
                        act.activation(pad[:, j, TAPS - 1:], p_proj[j % 2][:, :], ACT.Identity).then_inc(raw_done, 1)
                        wait(act, par_done, 2, g, 2 * (i // BATCH) + 2)
                        wait(act, xt_done, 8, g, x_count(i - 1, j))
                        act.activation(conv[:, j, :], p_proj[j % 2][:, :], ACT.Identity,
                                       bias=half[:, 6 * j + 4:6 * j + 5], scale=half[:, 6 * j + 3:6 * j + 4]
                                       ).then_inc(tap_done, 1)
                    else:
                        wait(act, gate_done, 16, g, 4 * (i - 1))
                        act.activation(z2[:, i % 2, j - GT, :], p_proj[j % 2][:, :], ACT.Tanh, scale=0.5
                                       ).then_inc(zth_done, 1)
                if exists(g, s + 1):
                    wait(act, d_done, 16, g, s + 2)
                    wait(act, y_mm, 16, g, s)
                    act.activation(m_t[:, (s + 1) % 2, :, :], p_d[:, :, :], ACT.Exp).then_inc(e_done, 1)
                if j in (1, 2) and exists(g, s + 3):
                    wait(act, conv_done, 24, g, 3 * x_count(i, j - 1))
                    wait(act, x_done, 8, g, x_count(i, j - 1) - 1)
                    act.activation(th_x[:, :], conv[:, j - 1, :], ACT.Tanh).then_inc(xth_done, 1)
                if s == 1:
                    for n in range(2):
                        weight_hi(g, n)
                i, q = s // CHUNKS, s % CHUNKS
                if q >= 2 and exists(g, s + 4):
                    j = q - 2
                    wait(act, xt_done, 8, g, x_count(i + 1, j))
                    wait(act, y_mm, 16, g, 4 * i)
                    wait(act, xd_done, 16, g, 4 * i)
                    wait(act, xdec_done, 12, g, 3 * i)
                    act.activation(x_tok[:, (i + 1) % 2, :, j * P:(j + 1) * P], p_xt[:, :, :], ACT.Identity
                                   ).then_inc(xtok_done, 1)
                if 8 <= s < 12 and exists(g, SLOTS):
                    weight_hi(g, s - 6)
            groups(act, body)

        @block.vector
        def _(dve):
            def weight_lo(g, n):
                wait(dve, w_hi_done, 6, g, 4 + n + 1)
                if n < 2:
                    dve.scalar_tensor_tensor(out=wo_lo[:, n, :], in0=stage[:, n % 2, :],
                                             scalar=half[:, 6 * n + 5:6 * n + 6], in1=wo_hi[:, n, :],
                                             op0=ALU.mult, op1=ALU.subtract).then_inc(w_lo_done, 1)
                else:
                    dve.tensor_tensor(wi_lo[:, n - 2, :, :].rearrange("p c m -> p (c m)"), stage[:, n % 2, :],
                                      wi_hi[:, n - 2, :, :].rearrange("p c m -> p (c m)"), ALU.subtract
                                      ).then_inc(w_lo_done, 1)

            def parameters(g):
                dve.tensor_scalar(half[:, :], k["params"][:, bass.ds(g, 1), 0:12], 0.5, None, ALU.mult
                                  ).then_inc(par_done, 1)
                dve.tensor_copy(pad[:, :, 0:TAPS - 1], k["params"][:, bass.ds(g, 1), 12:18]
                                .rearrange("p g (j t) -> p (g j) t", j=GT)).then_inc(par_done, 1)

            def tables(g):
                dve.tensor_copy(d_now[:, :], k["d_row"][:, bass.ds(g * GH, GH)]).then_inc(tables_done, 1)
                dve.tensor_copy(all_now[:, :, :], k["e_all"][:, :].rearrange("p (t h) -> p t h", h=HEADS)
                                [:, :, bass.ds(g * GH, GH)]).then_inc(tables_done, 1)

            def per_head(e, t, g):
                return e[:, bass.ds(g * GH + t * HEADS, GH)].unsqueeze(2).to_broadcast([P, GH, HEAD])

            def body(g, s):
                if s == -4:
                    parameters(0)
                    tables(0)
                    for n in range(2, 6):
                        weight_lo(-1, n)
                if s == 2:
                    for n in range(2):
                        weight_lo(g, n)
                if exists(g, s - 2):
                    wait(dve, yt_done, 16, g, s - 1)
                    wait(dve, glo_done, 16, g, s - 2)
                    i, q = (s - 2) // CHUNKS, (s - 2) % CHUNKS
                    wait(dve, z_done, 8, g, x_count(i, GT - 1))
                    dve.tensor_tensor(gate[:, :, :], p_yt[:, 0:GC].rearrange("p (c t) -> p c t", c=GT),
                                      z2[:, i % 2, :, q * P:(q + 1) * P], ALU.mult).then_inc(gate_done, 1)
                i, q = s // CHUNKS, s % CHUNKS
                if q < CHUNKS - 1 and exists(g, s):
                    wait(dve, xtok_done, 8, g, x_count(i, GT - 1))
                    wait(dve, s_done, 12, g, state_count(i, q) - 1)
                    dve.tensor_tensor(x_dec[:, :, :],
                                      x_tok[:, i % 2, q, :].rearrange("p (h c) -> p h c", h=GH),
                                      per_head(k["e_rest"], s % SLOTS, g), ALU.mult).then_inc(xdec_done, 1)
                if exists(g, s - 2):
                    wait(dve, ghi_done, 16, g, s - 1)
                    dve.tensor_tensor(g_lo[:, s % 2, :, :], gate[:, :, :], g_hi[:, s % 2, :, :], ALU.subtract
                                      ).then_inc(glo_done, 1)
                i, j, is_x = kind(s)
                if j in (2, 3) and exists(g, s + 2):
                    wait(dve, xth_done, 8, g, x_count(i, j - 2))
                    dve.scalar_tensor_tensor(out=conv[:, j - 2, :], in0=th_x[:, :], scalar=1.0,
                                             in1=conv[:, j - 2, :], op0=ALU.add, op1=ALU.mult).then_inc(x_done, 1)
                i, j, is_x = kind(s - 1)
                if s > -4 and exists(g, s + 3):
                    if is_x:
                        n = x_count(i, j)
                        wait(dve, raw_done, 8, g, n)
                        wait(dve, par_done, 2, g, 2 * (i // BATCH) + 2)
                        wait(dve, tap_done, 8, g, n)
                        for tap in range(TAPS - 1):
                            wait(dve, conv_done, 24, g, 3 * (n - 1) + tap)
                            dve.scalar_tensor_tensor(out=conv[:, j, :], in0=pad[:, j, tap:tap + SEQ],
                                                     scalar=half[:, 6 * j + tap:6 * j + tap + 1], in1=conv[:, j, :],
                                                     op0=ALU.mult, op1=ALU.add).then_inc(conv_done, 1)
                    else:
                        n = x_count(i, j - GT)
                        wait(dve, zth_done, 8, g, n)
                        dve.scalar_tensor_tensor(out=z2[:, i % 2, j - GT, :], in0=z2[:, i % 2, j - GT, :], scalar=1.0,
                                                 in1=p_proj[j % 2][:, :], op0=ALU.add, op1=ALU.mult
                                                 ).then_inc(z_done, 1)
                if exists(g, s + 1):
                    wait(dve, e_done, 16, g, s + 2)
                    dve.tensor_tensor(m_t[:, (s + 1) % 2, :, :], m_t[:, (s + 1) % 2, :, :],
                                      k["cb"][:, (s + 1) % SLOTS, :].unsqueeze(1).to_broadcast([P, GH, P]), ALU.mult
                                      ).then_inc(m_done, 1)
                i, q = s // CHUNKS, s % CHUNKS
                yv = y[:, s % 2, :].rearrange("p (h c) -> p h c", h=GH)
                if exists(g, s):
                    t = s % SLOTS
                    wait(dve, y_mm, 16, g, s + 1)
                    wait(dve, yt_done, 16, g, s - 1)
                    wait(dve, sq_done, 16, g, s - 1)
                    dve.tensor_tensor(yv, p_y[:, 1, :, :], per_head(k["e_cum"], t, g), ALU.mult
                                      ).then_inc(ys_done, 1)
                    if q < CHUNKS - 1:
                        wait(dve, s_done, 12, g, state_count(i, q))
                        wait(dve, hdec_done, 12, g, state_count(i, q))
                        dve.tensor_tensor(h_next[:, :, :], h_dec[:, :, :],
                                          p_s[:, 0:GC].rearrange("p (h c) -> p h c", h=GH), ALU.add
                                          ).then_inc(h_done, 1)
                if exists(g, s - 2):
                    wait(dve, o_done, 16, g, s - 1)
                    t = (s - 2) % SLOTS
                    dve.tensor_tensor(k["acc"][:, t, :], k["acc"][:, t, :], p_o[:, :], ALU.add
                                      ).then_inc(acc_done, 1)
                if exists(g, s):
                    wait(dve, yx_done, 16, g, s + 1)
                    dve.tensor_tensor(yv, yv, p_y[:, 0, :, :], ALU.add).then_inc(y_done, 1)
                if 8 <= s < 12 and exists(g, SLOTS):
                    weight_lo(g, s - 6)
                if s == 15 and exists(g, SLOTS):
                    tables(g + 1)
                if s == 10 and exists(g, SLOTS):
                    wait(dve, tap_done, 8, g, 8)
                    wait(dve, conv_done, 24, g, 24)
                    parameters(g + 1)
            groups(dve, body)

        @block.gpsimd
        def _(pool):
            def per_head(e):
                return e.unsqueeze(2).to_broadcast([P, GH, HEAD])

            def body(g, s):
                if not exists(g, s) or s < 0:
                    return
                i, q, t = s // CHUNKS, s % CHUNKS, s % SLOTS
                wait(pool, xtok_done, 8, g, x_count(i, GT - 1))
                wait(pool, yx_done, 16, g, s)
                if s == 0:
                    wait(pool, tables_done, 2, g, 2)
                pool.tensor_tensor(xd[:, :, :], x_tok[:, i % 2, q, :].rearrange("p (h c) -> p h c", h=GH),
                                   per_head(d_now[:, :]), ALU.mult).then_inc(xd_done, 1)
                if q < CHUNKS - 1:
                    if q == 0:
                        state = h_first
                        if i == 0:
                            wait(pool, h_in, 1, g, 1, 16)
                    else:
                        state = h_next
                    wait(pool, h_done, 12, g, state_count(i, q) - 1)
                    pool.tensor_tensor(h_dec[:, :, :], state[:, :, :],
                                       per_head(all_now[:, t, :]), ALU.mult).then_inc(hdec_done, 1)
                wait(pool, ys_done, 16, g, s + 1)
                wait(pool, xd_done, 16, g, s + 1)
                yv = y[:, s % 2, :].rearrange("p (h c) -> p h c", h=GH)
                pool.tensor_tensor(yv, yv, xd[:, :, :], ALU.add).then_inc(yx_done, 1)
            groups(pool, body)


def ffn(nc, d, k):
    with ExitStack() as ctx:
        def sb(name, shape, dt=F32):
            return ctx.enter_context(nc.sbuf_tensor(name, shape, dt))

        def sem(name):
            return ctx.enter_context(nc.semaphore("ff_" + name))

        h1 = k["acc"]
        n_w = 3 * HIDDEN * DIM // P // WCOLS
        per_w = n_w // 3
        NQ = HIDDEN // DIM
        HH = HT // 2
        tern = sb("tern", [P, 3, KT * HIDDEN], BF16)
        raw = sb("ff_raw", [P, 2, WCOLS])
        resid = sb("ff_resid", [P, 2, DIM])
        g12 = sb("g12", [P, 2, DIM])
        g3 = sb("g3", [P, HIDDEN])
        stats = sb("ff_stats", [P, TILES, 6])
        mv = sb("ff_mv", [P, TILES, 2])
        names = ("ff_r", "ff_tmp", "ff_v", "ff_rstd", "ff_ms", "ff_rb", "ff_rn", "ff_minus")
        r, tmp, v, rstd, ms, rb, rn, minus_mean = (sb(n, [P, TILES]) for n in names)
        ath = k["ath"]
        u12 = sb("u12", [P, 2, DIM])
        size12, top12, scale12 = (sb(n, [P, 2]) for n in ("size12", "top12", "scale12"))
        deq12 = sb("deq12", [P, 2, 2])
        q12 = sb("q12", [P, 2, DIM], BF16)
        q_t = sb("q_t", [P, 2, 2 * KT, P], BF16)
        sw = sb("sw", [P, 2, DIM])
        h = sb("ff_h", [P, 2, HIDDEN])
        u3 = sb("u3", [P, 2, HIDDEN])
        hsq = sb("hsq", [P, HIDDEN], BF16)
        hss = sb("hss", [P, 2])
        size3, ms3, rb3, t3, top3, scale3 = (sb(n, [P, 1]) for n in ("size3", "ms3", "rb3", "t3", "top3", "scale3"))
        deq3 = sb("deq3", [P, 2])
        q3 = sb("q3", [P, HIDDEN], BF16)
        q3_t = sb("q3_t", [P, HT, P], BF16)
        res = sb("res", [P, 2, DIM])

        def bank(name, shape, dt=F32):
            return ctx.enter_context(nc.psum_tensor(name, shape, dt))

        p1 = [bank(f"p_w1_{i}", [P, DIM]) for i in range(2)]
        p2 = [bank(f"p_w2_{i}", [P, DIM]) for i in range(2)]
        p_q = bank("p_q", [P, 2 * KT, P], BF16)
        p_h = [bank(f"p_h{i}", [P, HH, P], BF16) for i in range(2)]
        p_o = bank("p_out", [P, DIM])

        loaded, first = sem("loaded"), sem("first")
        resid_in = [sem(f"resid{i}") for i in range(2)]
        raw_in = [sem(f"raw{i}") for i in range(2)]
        h1_done, tanh_done, tern_done = sem("h1"), sem("tanh"), sem("tern")
        prep_step, u12_done, deq_done = sem("prep_step"), sem("u12"), sem("deq")
        q12_done, qt_done, qtc_done = sem("q12"), sem("qt"), sem("qtc")
        w12_done, sw_done, h_done = sem("w12"), sem("sw"), sem("h")
        hss_done, u3_ready = sem("hss"), sem("u3r")
        hid_step, u3_done, q3_done = sem("hid_step"), sem("u3"), sem("q3")
        deq3_done = sem("deq3")
        ht_done, htc_done, o_done, res_done = sem("ht"), sem("htc"), sem("o"), sem("res")
        out_done = [sem(f"out{i}") for i in range(2)]
        PREP_STEPS, HIDDEN_STEPS = 6, 16

        def wait(eng, s, per_tile, t, local=0, unit=1):
            g, k_th = t
            value = (2 * per_tile * unit) * g + (per_tile * k_th + local) * unit
            if isinstance(value, int) and value <= 0:
                return
            eng.wait_ge(s, value)

        def tile(t, off):
            return t[0], t[1] + off

        def exists(t):
            return not isinstance(t[0], int) or 0 <= 2 * t[0] + t[1] < TILES

        def number(t):
            return 2 * t[0] + t[1]

        def slots(eng, body):
            for t in range(6):
                body((0, t))
            with eng.Fori(3, TILES // 2 - 1) as g:
                for t in range(2):
                    body((g, t))
            for t in range(TILES - 2, TILES + 3):
                body((0, t))

        block = ctx.enter_context(nc.Block())

        @block.sync
        def _(sp):
            for n in range(2):
                sp.dma_start(resid[:, n % 2, :], d["resid"][n]).then_inc(resid_in[n % 2], 16)
            for n in range(2):
                sp.dma_start(raw[:, n % 2, :], d["w_ffn"][n]).then_inc(raw_in[n % 2], 16)
            for n in range(2):
                sp.dma_start(g12[:, n, :], d["g12"][n].partition_broadcast(P)).then_inc(loaded, 16)
            sp.dma_start(g3[:, :], d["g3"].partition_broadcast(P)).then_inc(loaded, 16)
            def chunk(n):
                sp.wait_ge(tern_done, n - 1)
                sp.dma_start(raw[:, n % 2, :], d["w_ffn"][n]).then_inc(raw_in[n % 2], 16)

            for n in range(2, TILES):
                sp.wait_ge(h1_done, n - 1)
                sp.dma_start(resid[:, n % 2, :], d["resid"][n]).then_inc(resid_in[n % 2], 16)
                if n % 2:
                    chunk(n // 2 + 1)
            for n in range(TILES // 2 + 1, n_w):
                chunk(n)

            def body(t):
                u = tile(t, -3)
                if exists(u):
                    wait(sp, res_done, 1, u, 1)
                    sp.dma_start(d["out"][bass.ds(number(u) * P, P), :], res[:, u[1] % 2, :]
                                 ).then_inc(out_done[u[1] % 2], 16)
            slots(sp, body)
            for i in range(2):
                sp.wait_ge(out_done[i], 16 * TILES // 2)

        @block.tensor
        def _(pe):
            def turn_inputs(t):
                wait(pe, q12_done, 2, t, 2)
                wait(pe, qtc_done, 1, t)
                for w in range(2):
                    for c in range(KT):
                        last = pe.transpose(p_q[:, w * KT + c, :], q12[:, w, c * P:(c + 1) * P], k["ident_b"][:, :])
                last.then_inc(qt_done, 1)

            def turn_hidden(t, half):
                wait(pe, q3_done, 1, t, 1)
                wait(pe, htc_done, 2, t, half - 1)
                for c in range(HH):
                    at = (half * HH + c) * P
                    last = pe.transpose(p_h[half][:, c, :], q3[:, at:at + P], k["ident_b"][:, :])
                last.then_inc(ht_done, 1)

            def up(t, n):
                wait(pe, qtc_done, 1, t, 1)
                wait(pe, h_done, NQ, t, n - 1)
                for w, p in ((0, p1), (1, p2)):
                    for c in range(KT):
                        at = c * HIDDEN + n * DIM
                        last = pe.matmul(p[n % 2][:, :], q_t[:, t[1] % 2, w * KT + c, :], tern[:, w, at:at + DIM],
                                         start=(c == 0), stop=(c == KT - 1))
                last.then_inc(w12_done, 1)

            def down(t):
                wait(pe, res_done, 1, t)
                for c in range(HT):
                    if c % HH == 0:
                        wait(pe, htc_done, 2, t, 1 + c // HH)
                    last = pe.matmul(p_o[:, :], q3_t[:, c, :], tern[:, 2, c * DIM:(c + 1) * DIM],
                                     start=(c == 0), stop=(c == HT - 1))
                last.then_inc(o_done, 1)

            turn_inputs((0, 0))
            pe.wait_ge(tern_done, 2 * per_w)

            def body(t):
                back = tile(t, -2)
                if isinstance(t[0], int) and t[1] == 2:
                    pe.wait_ge(tern_done, n_w)
                for n in range(NQ):
                    if exists(t):
                        up(t, n)
                    if n < 2 and exists(back):
                        turn_hidden(back, n)
                    if n == 2 and exists(tile(t, 1)):
                        turn_inputs(tile(t, 1))
                if exists(back):
                    down(back)
            slots(pe, body)

        @block.scalar
        def _(act):
            def squashed(i):
                act.wait_ge(raw_in[i % 2], 16 * (i // 2 + 1))
                act.activation(raw[:, i % 2, :], raw[:, i % 2, :], ACT.Tanh,
                               scale=k["inv3"][:, i // per_w:i // per_w + 1]).then_inc(tanh_done, 1)

            def quantised_inputs(t):
                for w in range(2):
                    wait(act, u12_done, 2, t, w + 1)
                    wait(act, qt_done, 1, t)
                    act.activation(q12[:, w, :], u12[:, w, :], ACT.Copy, bias=-MAGIC).then_inc(q12_done, 1)

            def copy_inputs(t):
                wait(act, qt_done, 1, t, 1)
                wait(act, w12_done, NQ, tile(t, -1))
                act.activation(q_t[:, t[1] % 2, :, :], p_q[:, :, :], ACT.Copy).then_inc(qtc_done, 1)

            def copy_hidden(t, half):
                wait(act, ht_done, 2, t, half + 1)
                wait(act, o_done, 1, t)
                act.activation(q3_t[:, half * HH:(half + 1) * HH, :], p_h[half][:, :, :], ACT.Copy
                               ).then_inc(htc_done, 1)

            for i in range(2 * per_w):
                squashed(i)
            quantised_inputs((0, 0))
            copy_inputs((0, 0))
            quantised_inputs((0, 1))

            def body(t):
                back = tile(t, -2)
                for n in range(NQ):
                    if exists(t):
                        wait(act, w12_done, NQ, t, n + 1)
                        wait(act, deq_done, 1, t, 1)
                        wait(act, h_done, NQ, t, n - 1)
                        act.activation(sw[:, n % 2, :], p1[n % 2][:, :], ACT.Silu,
                                       scale=deq12[:, t[1] % 2, 0:1]).then_inc(sw_done, 1)
                    if n < 2 and exists(back):
                        copy_hidden(back, n)
                    if n == 2 and exists(tile(t, 1)):
                        copy_inputs(tile(t, 1))
                u = tile(t, -1)
                if exists(t):
                    wait(act, h_done, NQ, t, NQ)
                    wait(act, hss_done, 1, t)
                    act.activation(hsq[:, :], h[:, t[1] % 2, :], ACT.Square,
                                   accum_out=hss[:, t[1] % 2:t[1] % 2 + 1]).then_inc(hss_done, 1)
                if exists(u):
                    wait(act, u3_done, 1, u, 1)
                    wait(act, ht_done, 2, u)
                    act.activation(q3[:, :], u3[:, u[1] % 2, :], ACT.Copy, bias=-MAGIC).then_inc(q3_done, 1)
                if exists(tile(t, 2)):
                    quantised_inputs(tile(t, 2))
                if isinstance(t[0], int) and t[1] < 2:
                    for i in range(2):
                        squashed(2 * per_w + 2 * t[1] + i)
            slots(act, body)

        @block.gpsimd
        def _(pool):
            pool.wait_ge(loaded, 3 * 16)

            def body(t):
                if not exists(t):
                    return
                for n in range(NQ):
                    at = slice(n * DIM, (n + 1) * DIM)
                    wait(pool, h_done, NQ, t, n + 1)
                    wait(pool, q3_done, 1, t, -1)
                    pool.tensor_tensor(u3[:, t[1] % 2, at], h[:, t[1] % 2, at], g3[:, at], ALU.mult
                                       ).then_inc(u3_ready, 1)
            slots(pool, body)

        @block.vector
        def _(dve):
            n_first = 0

            def link(ins):
                nonlocal n_first
                n_first += 1
                ins.then_inc(first, 1)
                dve.wait_ge(first, n_first)

            link(dve.tensor_reduce(v[:, :], k["y_sq"][:, :].rearrange("p (t g) -> p t g", g=GROUPS), AX.X, ALU.add))
            link(dve.tensor_scalar(v[:, :], v[:, :], 1.0 / INNER, EPS_RMS, ALU.mult, ALU.add))
            n_first = newton_rsqrt(dve, first, n_first, r[:, :], v[:, :], tmp[:, :])
            def ternary(i):
                w = i // per_w
                dve.wait_ge(tanh_done, i + 1)
                dve.tensor_scalar(tern[:, w, (i % per_w) * WCOLS:(i % per_w + 1) * WCOLS], raw[:, i % 2, :],
                                  MAGIC, -MAGIC, ALU.add, ALU.add).then_inc(tern_done, 1)

            for t in range(TILES):
                dve.wait_ge(resid_in[t % 2], 16 * (t // 2 + 1))
                dve.scalar_tensor_tensor(out=h1[:, t, :], in0=h1[:, t, :], scalar=r[:, t:t + 1],
                                         in1=resid[:, t % 2, :], op0=ALU.mult, op1=ALU.add).then_inc(h1_done, 1)
                if t:
                    dve.wait_ge(h1_done, t)
                    dve.bn_stats(stats[:, t - 1, :], h1[:, t - 1, :]).then_inc(first, 1)
                    n_first += 1
                if t % 2:
                    ternary(t // 2)
            dve.wait_ge(h1_done, TILES)
            link(dve.bn_stats(stats[:, TILES - 1, :], h1[:, TILES - 1, :]))
            for t in range(TILES):
                dve.bn_aggr(mv[:, t, :], stats[:, t, :]).then_inc(first, 1)
            n_first += TILES
            dve.wait_ge(first, n_first)
            link(dve.tensor_scalar(v[:, :], mv[:, :, 1], EPS_NORM, None, ALU.add))
            dve.tensor_scalar(minus_mean[:, :], mv[:, :, 0], -1.0, None, ALU.mult).then_inc(first, 1)
            n_first += 1
            n_first = newton_rsqrt(dve, first, n_first, rstd[:, :], v[:, :], tmp[:, :])
            link(dve.tensor_tensor(ms[:, :], rstd[:, :], rstd[:, :], ALU.mult))
            link(dve.tensor_tensor(ms[:, :], ms[:, :], mv[:, :, 1], ALU.mult))
            link(dve.tensor_scalar(ms[:, :], ms[:, :], EPS_BIT, None, ALU.add))
            n_first = newton_rsqrt(dve, first, n_first, rb[:, :], ms[:, :], tmp[:, :])
            link(dve.tensor_tensor(rn[:, :], rb[:, :], rstd[:, :], ALU.mult))
            dve.wait_ge(loaded, 3 * 16)

            def prepare(t, step):
                def after(n):
                    wait(dve, prep_step, PREP_STEPS, t, n)

                def col(a):
                    return a[:, bass.ds(number(t), 1)]
                if step < 2:
                    w = step
                    wait(dve, q12_done, 2, t)
                    dve.scalar_tensor_tensor(out=u12[:, w, :], in0=h1_of(t), scalar=col(minus_mean),
                                             in1=g12[:, w, :], op0=ALU.add, op1=ALU.mult).then_inc(prep_step, 1)
                elif step == 2:
                    after(2)
                    dve.tensor_reduce(size12[:, :], u12[:, :, :], AX.X, ALU.max, apply_absolute_value=True
                                      ).then_inc(prep_step, 1)
                elif step == 3:
                    after(3)
                    dve.tensor_scalar(top12[:, :], size12[:, :], col(rn), 1e-4, ALU.mult, ALU.max
                                      ).then_inc(prep_step, 1)
                elif step == 4:
                    after(4)
                    wait(dve, h_done, NQ, tile(t, -1))
                    dve.tensor_tensor(deq12[:, t[1] % 2, :], top12[:, :], ath[:, 0:2], ALU.mult
                                      ).then_inc(deq_done, 1)
                elif step == 5:
                    dve.reciprocal(scale12[:, :], top12[:, :]).then_inc(prep_step, 1)
                elif step == 6:
                    after(5)
                    dve.tensor_scalar(scale12[:, :], scale12[:, :], 127.0, col(rn), ALU.mult, ALU.mult
                                      ).then_inc(prep_step, 1)
                else:
                    after(6)
                    w = step - 7
                    dve.tensor_scalar(u12[:, w, :], u12[:, w, :], scale12[:, w:w + 1], MAGIC, ALU.mult, ALU.add
                                      ).then_inc(u12_done, 1)

            def h1_of(t):
                return h1[:, bass.ds(number(t), 1), :].rearrange("p a c -> p (a c)")

            def hidden(t, step):
                if step:
                    wait(dve, hid_step, HIDDEN_STEPS, t, min(step, HIDDEN_STEPS))
                if step == 0:
                    wait(dve, u3_ready, NQ, t, NQ)
                    ins = dve.tensor_reduce(size3[:, :], u3[:, t[1] % 2, :], AX.X, ALU.max,
                                            apply_absolute_value=True)
                elif step == 1:
                    wait(dve, hss_done, 1, t, 1)
                    ins = dve.tensor_scalar(ms3[:, :], hss[:, t[1] % 2:t[1] % 2 + 1], 1.0 / HIDDEN, EPS_BIT,
                                            ALU.mult, ALU.add)
                elif step == 2:
                    ins = dve.tensor_scalar(t3[:, :].bitcast(I32), ms3[:, :].bitcast(I32), 1, None,
                                            ALU.logical_shift_right)
                elif step == 3:
                    ins = dve.tensor_scalar(rb3[:, :].bitcast(I32), t3[:, :].bitcast(I32), -1.0, RSQRT_GUESS,
                                            ALU.mult, ALU.add)
                elif step < 13 and step % 3 == 1:
                    ins = dve.tensor_tensor(t3[:, :], rb3[:, :], rb3[:, :], ALU.mult)
                elif step < 13 and step % 3 == 2:
                    ins = dve.scalar_tensor_tensor(out=t3[:, :], in0=t3[:, :], scalar=-0.5, in1=ms3[:, :],
                                                   op0=ALU.mult, op1=ALU.mult)
                elif step < 13:
                    ins = dve.scalar_tensor_tensor(out=rb3[:, :], in0=t3[:, :], scalar=1.5, in1=rb3[:, :],
                                                   op0=ALU.add, op1=ALU.mult)
                elif step == 13:
                    ins = dve.tensor_scalar(top3[:, :], size3[:, :], rb3[:, 0:1], 1e-4, ALU.mult, ALU.max)
                elif step == 14:
                    ins = dve.reciprocal(scale3[:, :], top3[:, :])
                elif step == 15:
                    ins = dve.tensor_scalar(scale3[:, :], scale3[:, :], 127.0, rb3[:, 0:1], ALU.mult, ALU.mult)
                elif step == 16:
                    dve.tensor_tensor(deq3[:, t[1] % 2:t[1] % 2 + 1], top3[:, :], ath[:, 2:3], ALU.mult
                                      ).then_inc(deq3_done, 1)
                    return
                else:
                    dve.tensor_scalar(u3[:, t[1] % 2, :], u3[:, t[1] % 2, :], scale3[:, 0:1], MAGIC,
                                      ALU.mult, ALU.add).then_inc(u3_done, 1)
                    return
                ins.then_inc(hid_step, 1)

            def product(t, n):
                at = slice(n * DIM, (n + 1) * DIM)
                wait(dve, sw_done, NQ, t, n + 1)
                wait(dve, hss_done, 1, t, -1)
                wait(dve, u3_ready, NQ, t, -NQ)
                dve.scalar_tensor_tensor(out=h[:, t[1] % 2, at], in0=p2[n % 2][:, :],
                                         scalar=deq12[:, t[1] % 2, 1:2], in1=sw[:, n % 2, :],
                                         op0=ALU.mult, op1=ALU.mult).then_inc(h_done, 1)

            def result(t):
                wait(dve, o_done, 1, t, 1)
                wait(dve, deq3_done, 1, t, 1)
                g, k_th = t
                if not isinstance(g, int) or k_th >= 2:
                    dve.wait_ge(out_done[k_th % 2], 16 * g + 16 * (k_th // 2))
                dve.scalar_tensor_tensor(out=res[:, t[1] % 2, :], in0=p_o[:, :], scalar=deq3[:, t[1] % 2:t[1] % 2 + 1],
                                         in1=h1_of(t), op0=ALU.mult, op1=ALU.add).then_inc(res_done, 1)

            for t in range(2):
                for step in range(9):
                    prepare((0, t), step)

            def body(t):
                u, ahead = tile(t, -1), tile(t, 2)

                def hidden_steps(*steps):
                    if exists(u):
                        for step in steps:
                            hidden(u, step)

                def prepare_steps(*steps):
                    if exists(ahead):
                        for step in steps:
                            prepare(ahead, step)

                if exists(tile(t, -3)):
                    result(tile(t, -3))
                hidden_steps(0)
                for n in range(NQ):
                    hidden_steps(3 * n + 1)
                    if exists(t):
                        product(t, n)
                    hidden_steps(3 * n + 2)
                    prepare_steps(n)
                    hidden_steps(3 * n + 3)
                hidden_steps(13)
                prepare_steps(4)
                hidden_steps(14)
                prepare_steps(5)
                hidden_steps(15)
                prepare_steps(6)
                hidden_steps(16, 17)
                prepare_steps(7, 8)
                if isinstance(t[0], int) and t[1] < 2:
                    for i in range(2):
                        ternary(2 * per_w + 2 * t[1] + i)
            slots(dve, body)


def build(nc, d):
    d = dict(d)
    d["resid"] = nc.dram_tensor("resid_scratch", [TILES, P, DIM], F32, kind="Internal").ap()
    d["cum"] = nc.dram_tensor("cum_scratch", [2, HEADS, TOKENS], F32, kind="Internal").ap()
    with ExitStack() as ctx:
        def sb(name, shape, dt=F32):
            return ctx.enter_context(nc.sbuf_tensor(name, shape, dt))

        TC = TILES * HEADS
        k = {
            "acc": sb("acc", [P, TILES, DIM]),
            "w_sum": sb("w_sum", [P, 12]),
            "inv3": sb("inv3", [P, 3]),
            "ath": sb("ath", [P, 3]),
            "y_sq": sb("y_sq", [P, TILES * GROUPS]),
            "ident": sb("ident_f", [P, P]),
            "ident_b": sb("ident_b", [P, P], BF16),
        }
        with ExitStack() as inner:
            def sbi(name, shape, dt=F32):
                return inner.enter_context(nc.sbuf_tensor(name, shape, dt))

            k.update({
                "x_hi": sbi("x_hi", [P, KT, TOKENS], F32R),
                "x_lo": sbi("x_lo", [P, KT, TOKENS], F32R),
                "b_tok": sbi("b_tok", [P, TILES, P]),
                "c_t": sbi("c_t", [P, TOKENS]),
                "cb": sbi("cb", [P, TILES, P]),
                "e_cum": sbi("e_cum", [P, TC]),
                "e_all": sbi("e_all", [P, TC]),
                "e_rest": sbi("e_rest", [P, TC]),
                "d_row": sbi("d_row", [P, HEADS]),
                "params": sbi("params", [P, GROUPS, 18]),
                "neg_mask": sbi("neg_mask", [P, P], BF16),
                "rows": sbi("rows", [10, 2, GH * P], F32R),
                "cols": sbi("cols", [10, 2, P], F32R),
            })
            with ExitStack() as early:
                for name, dt in (("bcd_raw", F32), ("bcd_hi", F32R), ("bcd_lo", F32R)):
                    k[name] = early.enter_context(nc.sbuf_tensor(name, [P, KT, 3 * P], dt))
                embed(nc, d, k)
                decays(nc, d, k)
            mixer(nc, d, k)
        ffn(nc, d, k)


def layouts(x, L0_tok_W, L0_tok_delta_values, L0_tok_token_indices, L0_attn_norm_w, L0_attn_in_proj_w,
            L0_attn_conv_w, L0_attn_conv_b, L0_attn_dt_bias, L0_attn_A_log, L0_attn_D_param,
            L0_attn_inner_norm_w, L0_attn_out_proj_w, L0_attn_conv_state, L0_attn_ssm_state,
            L0_ffn_w1, L0_ffn_g1, L0_ffn_w2, L0_ffn_g2, L0_ffn_w3, L0_ffn_g3):
    c = np.ascontiguousarray
    w = np.asarray(L0_attn_in_proj_w)
    turned = c(w.T).reshape(KT, P, w.shape[0]).transpose(1, 0, 2)
    z, xc = turned[:, :, :INNER], turned[:, :, INNER:2 * INNER]
    w_in = np.stack([xc.reshape(P, KT, GROUPS, GT, P), z.reshape(P, KT, GROUPS, GT, P)], 3)
    w_in = w_in.transpose(2, 3, 4, 0, 1, 5).reshape(GROUPS, 2 * GT, P, KT * P)
    at = 2 * INNER
    w_bcd = np.concatenate([turned[:, :, at:at + 2 * STATE], turned[:, :, at + 2 * STATE:],
                            turned[:, :, :P - HEADS]], 2)
    per_channel = np.concatenate([np.asarray(L0_attn_conv_w), np.asarray(L0_attn_conv_b)[:, None],
                                  np.asarray(L0_attn_inner_norm_w)[:, None]], 1)
    params = np.concatenate([per_channel.reshape(GROUPS, GT, P, 6).transpose(2, 0, 1, 3).reshape(P, GROUPS, 12),
                             np.asarray(L0_attn_conv_state)[0].reshape(GROUPS, GT, P, 3).transpose(2, 0, 1, 3)
                             .reshape(P, GROUPS, 6)], 2)
    kmajor = lambda a, n: c(np.asarray(a).T).reshape(n, P, -1).transpose(1, 0, 2).reshape(P, -1, WCOLS).transpose(1, 0, 2)
    first = np.asarray(L0_attn_ssm_state)[0].reshape(GROUPS, GH, STATE, HEAD).transpose(0, 2, 1, 3)
    i = np.arange(P)
    rows = np.zeros((10, 2, GH, P), np.float32)
    cols = np.zeros((10, 2, P), np.float32)
    cols[0:2] = 1.0
    for part in range(2):
        for h in range(GH):
            rows[2 + part * GH + h, :, h, :] = -1.0
    return {
        "id_col": c(np.asarray(x).reshape(TILES, P).T),
        "id_row": c(np.asarray(x).reshape(TOKENS)),
        "tok": c(np.asarray(L0_tok_token_indices).reshape(TRAINED, 1)),
        "delta": c(np.asarray(L0_tok_delta_values).reshape(DIM, TRAINED).T),
        "W": c(np.asarray(L0_tok_W)),
        "norm_w": c(np.asarray(L0_attn_norm_w)),
        "w_in": c(w_in), "w_bcd": c(w_bcd), "params": c(params),
        "w_out": c(np.asarray(L0_attn_out_proj_w).T).reshape(GROUPS, GT, P, DIM),
        "dt_bias": c(np.asarray(L0_attn_dt_bias).reshape(HEADS, 1)),
        "a_log": c(np.asarray(L0_attn_A_log).reshape(HEADS, 1)),
        "D": c(np.asarray(L0_attn_D_param)),
        "h_first": c(first),
        "w_ffn": c(np.concatenate([kmajor(L0_ffn_w1, KT), kmajor(L0_ffn_w2, KT), kmajor(L0_ffn_w3, HT)], 0)),
        "g12": c(np.stack([np.asarray(L0_ffn_g1), np.asarray(L0_ffn_g2)])),
        "g3": c(np.asarray(L0_ffn_g3)),
        "ident": np.eye(P, dtype=np.float32),
        "ones": np.ones((P, P), np.float32),
        "tri": (i[:, None] <= i[None, :]).astype(np.float32),
        "neg_mask": np.where(i[:, None] <= i[None, :], 0.0, -1e38).astype(np.float32),
        "pick_last": np.broadcast_to((i == P - 1)[:, None], (P, P)).astype(np.float32),
        "keep": (np.arange(TOKENS) % P != 0).astype(np.float32),
        "rows": rows.reshape(10, 2, GH * P), "cols": cols,
    }


def kernel(**inputs):
    import concourse.bacc as bacc
    from concourse.bass_utils import run_bass_kernel_spmd

    nc = bacc.Bacc("TRN2", target_bir_lowering=False, num_devices=1)
    arrays, d = {}, {}
    for name, a in layouts(**inputs).items():
        a = np.ascontiguousarray(a)
        arrays[f"in_{name}"] = a
        d[name] = nc.dram_tensor(f"in_{name}", a.shape, mybir.dt.from_np(a.dtype), kind="ExternalInput").ap()
    d["out"] = nc.dram_tensor("out_dram", [TOKENS, DIM], F32, kind="ExternalOutput").ap()
    build(nc, d)
    result = run_bass_kernel_spmd(nc, [arrays], core_ids=[0])
    return result.results[0]["out_dram"].reshape(BATCH, SEQ, DIM)
```

```python
from contextlib import ExitStack

import numpy as np

import concourse.bass as bass
from concourse import mybir

F32 = mybir.dt.float32
F32R = mybir.dt.float32r
BF16 = mybir.dt.bfloat16
I32 = mybir.dt.int32
ALU = mybir.AluOpType
ACT = mybir.ActivationFunctionType
AX = mybir.AxisListType

P = 128
VOCAB, DIM, TRAINED = 32000, 512, 64
BATCH, SEQ = 4, 512
TOKENS = BATCH * SEQ
TILES = TOKENS // P
KT = DIM // P
HEADS, HEAD, STATE, TAPS = 48, 64, 128, 4
INNER = HEADS * HEAD
GH = 4
GC = GH * HEAD
GROUPS = HEADS // GH
GT = GC // P
CHUNKS = SEQ // P
SLOTS = BATCH * CHUNKS
HIDDEN = 2048
HT = HIDDEN // P
EPS_NORM, EPS_RMS, EPS_BIT = 1e-5, 1e-5, 1e-8
MAGIC = 12582912.0
RSQRT_GUESS = 1597463007.0
WCOLS = 2048


def newton_rsqrt(eng, sem, count, y, v, t, steps=3):
    def link(ins):
        nonlocal count
        count += 1
        ins.then_inc(sem, 1)
        eng.wait_ge(sem, count)

    link(eng.tensor_scalar(t.bitcast(I32), v.bitcast(I32), 1, None, ALU.logical_shift_right))
    link(eng.tensor_scalar(y.bitcast(I32), t.bitcast(I32), -1.0, RSQRT_GUESS, ALU.mult, ALU.add))
    for _ in range(steps):
        link(eng.tensor_tensor(t, y, y, ALU.mult))
        link(eng.scalar_tensor_tensor(out=t, in0=t, scalar=-0.5, in1=v, op0=ALU.mult, op1=ALU.mult))
        link(eng.scalar_tensor_tensor(out=y, in0=t, scalar=1.5, in1=y, op0=ALU.add, op1=ALU.mult))
    return count


def embed(nc, d, k):
    with ExitStack() as ctx:
        def sb(name, shape, dt=F32):
            return ctx.enter_context(nc.sbuf_tensor(name, shape, dt))

        def sem(name):
            return ctx.enter_context(nc.semaphore(name))

        id_row = k["b_tok"][0:TRAINED, :, :].rearrange("p t c -> p (t c)").bitcast(I32)
        row_f = k["c_t"][0:TRAINED, :]
        row_wrap = k["cb"][0:TRAINED, :, :].rearrange("p t c -> p (t c)")
        hit = sb("hit", [TRAINED, TOKENS], BF16)
        id_col = sb("id_col", [P, TILES], I32)
        col_f = sb("col_f", [P, TILES])
        col_wrap = sb("col_wrap", [P, TILES])
        row_id = sb("row_id", [P, TILES], I32)
        tok = sb("tok", [TRAINED, 1], I32)
        tok_f = sb("tok_f", [TRAINED, 1])
        tok_wrap = sb("tok_wrap", [TRAINED, 1])
        delta = sb("delta", [TRAINED, DIM])
        delta_rest = sb("delta_rest", [TRAINED, DIM])
        delta_parts = sb("delta_parts", [TRAINED, 3, DIM], BF16)
        norm_row = sb("norm_row", [P, DIM])
        stats = sb("stats", [P, TILES, 6])
        mv = sb("mv", [P, TILES, 2])
        var, root, tmp = (sb(n, [P, 2, TILES]) for n in ("var", "root", "tmp_c"))
        rrms, shift = (sb(n, [P, TILES]) for n in ("rrms", "shift"))
        x1 = sb("x1", [P, 4, DIM])
        resid = sb("resid", [P, 2, DIM])
        xs = sb("xs", [P, 2, DIM])
        w_raw = sb("w_raw", [P, 2, WCOLS])
        p_delta = [ctx.enter_context(nc.psum_tensor(f"p_delta{i}", [P, DIM], F32)) for i in range(4)]
        p_xt = [ctx.enter_context(nc.psum_tensor(f"p_xt{i}", [P, KT, P], F32)) for i in range(4)]

        loaded, ids_ready, chain = sem("em_loaded"), sem("em_ids"), sem("em_chain")
        hit_ready, delta_done = sem("em_hit"), sem("em_delta")
        gathered = [sem(f"em_gathered{i}") for i in range(4)]
        bcd_loaded, bcd_hi_done, stats_ready = sem("em_bcd"), sem("em_bcdhi"), sem("em_stats")
        added, x1_ready, resid_ready, xs_ready = sem("em_added"), sem("em_x1"), sem("em_resid"), sem("em_xs")
        resid_stored = [sem(f"em_stored{i}") for i in range(2)]
        xt_done, hi_done, lo_done = sem("em_xt"), sem("em_hi"), sem("em_lo")
        w_loaded = [sem(f"em_w{i}") for i in range(2)]
        w_summed = sem("em_wsum")
        h0 = k["acc"]
        n_w = 3 * HIDDEN * DIM // P // WCOLS
        QT = TILES // 4
        block = ctx.enter_context(nc.Block())

        @block.sync
        def _(sp):
            sp.dma_start(id_col[:, :], d["id_col"]).then_inc(loaded, 16)
            sp.dma_start(tok[:, :], d["tok"]).then_inc(loaded, 16)
            sp.dma_start(id_row, d["id_row"].partition_broadcast(TRAINED)).then_inc(loaded, 16)
            sp.dma_start(delta[:, :], d["delta"]).then_inc(loaded, 16)
            sp.dma_start(norm_row[:, :], d["norm_w"].partition_broadcast(P)).then_inc(loaded, 16)
            sp.dma_start(k["ident"][:, :], d["ident"]).then_inc(loaded, 16)
            sp.dma_start(k["bcd_raw"][:, :, :], d["w_bcd"]).then_inc(bcd_loaded, 16)
            def chunk(n):
                if n >= 2:
                    sp.wait_ge(w_summed, n - 1)
                sp.dma_start(w_raw[:, n % 2, :], d["w_ffn"][n]).then_inc(w_loaded[n % 2], 16)

            for n in range(n_w - 2):
                chunk(n)
            for t in range(TILES):
                sp.wait_ge(resid_ready, t + 1)
                sp.dma_start(d["resid"][t], resid[:, t % 2, :]).then_inc(resid_stored[t % 2], 16)
                if t in (3, 7):
                    chunk(n_w - 2 + t // 4)
            for i in range(2):
                sp.wait_ge(resid_stored[i], 16 * TILES // 2)

        @block.gpsimd
        def _(pool):
            pool.wait_ge(ids_ready, 1)
            for t in range(TILES):
                pool.indirect_dma_start(out=h0[:, t, :], out_offset=None, in_=d["W"],
                                        in_offset=bass.IndirectOffsetOnAxis(ap=row_id[:, t:t + 1], axis=0)
                                        ).then_inc(gathered[t // QT], 16)
            for t in range(TILES):
                pool.wait_ge(x1_ready, t + 1)
                if t >= 2:
                    pool.wait_ge(resid_stored[t % 2], 16 * (t // 2))
                pool.tensor_tensor(resid[:, t % 2, :], h0[:, t, :], x1[:, t % 4, :], ALU.add
                                   ).then_inc(resid_ready, 1)

        @block.scalar
        def _(act):
            act.wait_ge(bcd_loaded, 16)
            act.activation(k["bcd_hi"][:, :, :], k["bcd_raw"][:, :, :], ACT.Identity).then_inc(bcd_hi_done, 1)

            def sizes(n):
                act.wait_ge(w_loaded[n % 2], 16 * (n // 2 + 1))
                act.activation(w_raw[:, n % 2, :], w_raw[:, n % 2, :], ACT.Abs,
                               accum_out=k["w_sum"][:, n:n + 1]).then_inc(w_summed, 1)

            def normalised(t):
                if t >= 4:
                    act.wait_ge(xs_ready, t - 3)
                    act.wait_ge(resid_ready, t - 3)
                act.activation(x1[:, t % 4, :], h0[:, t, :], ACT.Identity, scale=root[:, 0, t:t + 1],
                               bias=shift[:, t:t + 1]).then_inc(x1_ready, 1)

            for n in range(n_w - 4):
                sizes(n)
            act.wait_ge(stats_ready, 1)
            for t in range(3):
                normalised(t)
            for t in range(TILES):
                act.wait_ge(xt_done, t + 1)
                act.activation(k["x_hi"][:, :, t * P:(t + 1) * P], p_xt[t % 4][:, :, :], ACT.Identity
                               ).then_inc(hi_done, 1)
                if t + 3 < TILES:
                    normalised(t + 3)
                if t % 4 == 1:
                    sizes(n_w - 4 + t // 4)

        @block.tensor
        def _(pe):
            pe.wait_ge(hit_ready, 1)
            for t in range(TILES):
                if t >= 4:
                    pe.wait_ge(added, t - 3)
                for i in range(3):
                    last = pe.matmul(p_delta[t % 4][:, :], hit[:, t * P:(t + 1) * P], delta_parts[:, i, :],
                                     start=(i == 0), stop=(i == 2))
                last.then_inc(delta_done, 1)
            for t in range(TILES):
                pe.wait_ge(xs_ready, t + 1)
                if t >= 4:
                    pe.wait_ge(lo_done, t - 3)
                for j in range(KT):
                    last = pe.transpose(p_xt[t % 4][:, j, :], xs[:, t % 2, j * P:(j + 1) * P],
                                        k["ident"][:, :])
                last.then_inc(xt_done, 1)

        @block.vector
        def _(dve):
            n = 0

            def link(ins):
                nonlocal n
                n += 1
                ins.then_inc(chain, 1)
                dve.wait_ge(chain, n)

            def wrapped(f, wrap, ints):
                link(dve.tensor_copy(f, ints))
                link(dve.tensor_scalar(wrap, f, 0.0, float(VOCAB), ALU.is_lt, ALU.mult))
                link(dve.tensor_tensor(f, f, wrap, ALU.add))

            dve.wait_ge(loaded, 6 * 16)
            wrapped(col_f[:, :], col_wrap[:, :], id_col[:, :])
            link(dve.tensor_scalar(col_f[:, :], col_f[:, :], 0.0, float(VOCAB - 1), ALU.max, ALU.min))
            dve.tensor_copy(row_id[:, :], col_f[:, :]).then_inc(ids_ready, 1)
            wrapped(tok_f[:, :], tok_wrap[:, :], tok[:, :])
            link(dve.tensor_copy(delta_parts[:, 0, :], delta[:, :]))
            link(dve.tensor_tensor(delta_rest[:, :], delta[:, :], delta_parts[:, 0, :], ALU.subtract))
            link(dve.tensor_copy(delta_parts[:, 1, :], delta_rest[:, :]))
            link(dve.tensor_tensor(delta_parts[:, 2, :], delta_rest[:, :], delta_parts[:, 1, :], ALU.subtract))
            wrapped(row_f, row_wrap, id_row)
            link(dve.tensor_scalar(row_f, row_f, 0.0, float(VOCAB - 1), ALU.max, ALU.min))
            dve.tensor_scalar(hit[:, :], row_f, tok_f[:, 0:1], None, ALU.is_equal).then_inc(hit_ready, 1)
            dve.wait_ge(bcd_hi_done, 1)
            dve.tensor_tensor(k["bcd_lo"][:, :, :], k["bcd_raw"][:, :, :], k["bcd_hi"][:, :, :], ALU.subtract)
            for t in range(TILES):
                if t % QT == 0:
                    dve.wait_ge(gathered[t // QT], 16 * QT)
                dve.wait_ge(delta_done, t + 1)
                dve.tensor_tensor(h0[:, t, :], h0[:, t, :], p_delta[t % 4][:, :], ALU.add).then_inc(added, 1)
                if t:
                    dve.wait_ge(added, t)
                    dve.bn_stats(stats[:, t - 1, :], h0[:, t - 1, :]).then_inc(chain, 1)
                    n += 1
            dve.wait_ge(added, TILES)
            link(dve.bn_stats(stats[:, TILES - 1, :], h0[:, TILES - 1, :]))
            for t in range(TILES):
                dve.bn_aggr(mv[:, t, :], stats[:, t, :]).then_inc(chain, 1)
            n += TILES
            dve.wait_ge(chain, n)
            link(dve.tensor_scalar(var[:, 0, :], mv[:, :, 1], EPS_NORM, None, ALU.add))
            link(dve.scalar_tensor_tensor(out=var[:, 1, :], in0=var[:, 0, :], scalar=EPS_RMS, in1=mv[:, :, 1],
                                          op0=ALU.mult, op1=ALU.add))
            n = newton_rsqrt(dve, chain, n, root[:, :, :], var[:, :, :], tmp[:, :, :])
            dve.scalar_tensor_tensor(out=shift[:, :], in0=mv[:, :, 0], scalar=-1.0, in1=root[:, 0, :],
                                     op0=ALU.mult, op1=ALU.mult).then_inc(stats_ready, 1)
            link(dve.tensor_tensor(rrms[:, :], var[:, 0, :], root[:, 0, :], ALU.mult))
            link(dve.tensor_tensor(rrms[:, :], rrms[:, :], root[:, 1, :], ALU.mult))
            for t in range(TILES + 2):
                if t < TILES:
                    dve.wait_ge(x1_ready, t + 1)
                    if t >= 2:
                        dve.wait_ge(xt_done, t - 1)
                    dve.scalar_tensor_tensor(out=xs[:, t % 2, :], in0=x1[:, t % 4, :], scalar=rrms[:, t:t + 1],
                                             in1=norm_row[:, :], op0=ALU.mult, op1=ALU.mult).then_inc(xs_ready, 1)
                if t >= 2:
                    u = t - 2
                    dve.wait_ge(hi_done, u + 1)
                    dve.tensor_tensor(k["x_lo"][:, :, u * P:(u + 1) * P], p_xt[u % 4][:, :, :],
                                      k["x_hi"][:, :, u * P:(u + 1) * P], ALU.subtract).then_inc(lo_done, 1)


def decays(nc, d, k):
    with ExitStack() as ctx:
        def sb(name, shape, dt=F32):
            return ctx.enter_context(nc.sbuf_tensor(name, shape, dt))

        def sem(name):
            return ctx.enter_context(nc.semaphore(name))

        TC = TILES * HEADS
        w_hi, w_lo = k["bcd_hi"], k["bcd_lo"]
        b_t = sb("b_t", [P, TOKENS])
        dt_pre = sb("dt_pre", [HEADS, TOKENS])
        soft = sb("soft", [HEADS, TOKENS])
        cum = sb("cum", [HEADS, TOKENS])
        cum_hi = sb("cum_hi", [HEADS, TOKENS], F32R)
        cum_lo = sb("cum_lo", [HEADS, TOKENS], F32R)
        cum_tok = sb("cum_tok", [P, TC])
        tri = sb("tri", [P, P])
        pick_last = sb("pick_last", [P, P])
        dt_bias = sb("dt_bias", [HEADS, 1])
        a_log = sb("a_log", [HEADS, 1])
        neg_a = sb("neg_a", [HEADS, 1])
        ones = k["c_t"][:, 0:P]
        sum3, s3, inv3, den = (sb(n, [P, 3]) for n in ("sum3", "s3", "inv3", "den"))
        rows_f = soft[0:10, 0:2 * GH * P].rearrange("r (n c) -> r n c", n=2)
        cols_f = soft[0:10, 2 * GH * P:2 * GH * P + 2 * P].rearrange("r (n c) -> r n c", n=2)
        p_proj = [ctx.enter_context(nc.psum_tensor(f"p_bcd{i}", [P, SEQ], F32)) for i in range(2)]
        p_cb = ctx.enter_context(nc.psum_tensor("p_cb", [P, 4, P], F32))
        p_bt = ctx.enter_context(nc.psum_tensor("p_bt", [P, 4, P], F32))
        p_ct = [ctx.enter_context(nc.psum_tensor(f"p_ct{i}", [P, 512], F32)) for i in range(2)]
        p_cq = [ctx.enter_context(nc.psum_tensor(f"p_cq{i}", [P, 512], F32)) for i in range(2)]
        HC = TC // 2

        loaded, biases = sem("bd_loaded"), sem("bd_biases")
        proj_done, evicted_a, evicted_v = sem("bd_proj"), sem("bd_eva"), sem("bd_evv")
        steps_a, steps_v, consts = sem("bd_sa"), sem("bd_sv"), sem("bd_consts")
        cb_done, cb_masked, bt_done, bt_copied = sem("bd_cb"), sem("bd_cbm"), sem("bd_bt"), sem("bd_btc")
        cum_ready, hi_ready, lo_ready, stored = sem("bd_cum"), sem("bd_hi"), sem("bd_lo"), sem("bd_stored")
        ct_done, tok_ready, cq_done, diff_ready = sem("bd_ct"), sem("bd_tok"), sem("bd_cq"), sem("bd_diff")
        keep_in = sem("bd_keep")
        sizes, mean_done, ln_in, ln_done = sem("bd_sizes"), sem("bd_mean"), sem("bd_lnin"), sem("bd_ln")
        block = ctx.enter_context(nc.Block())

        @block.sync
        def _(sp):
            for to, of in ((dt_bias[:, :], d["dt_bias"]), (a_log[:, :], d["a_log"])):
                sp.dma_start(to, of).then_inc(biases, 16)
            for to, of in ((ones, d["ones"]), (tri[:, :], d["tri"]),
                           (pick_last[:, :], d["pick_last"]),
                           (rows_f, d["rows"]), (cols_f, d["cols"]),
                           (k["d_row"][:, :], d["D"].partition_broadcast(P))):
                sp.dma_start(to, of).then_inc(loaded, 16)
            sp.wait_ge(steps_v, 1)
            sp.dma_start(dt_pre[:, :], d["keep"].partition_broadcast(HEADS)).then_inc(keep_in, 16)
            sp.wait_ge(hi_ready, 1)
            sp.dma_start(d["cum"][0], cum_hi[:, :].bitcast(F32)).then_inc(stored, 16)
            sp.wait_ge(lo_ready, 1)
            sp.dma_start(d["cum"][1], cum_lo[:, :].bitcast(F32)).then_inc(stored, 16)
            sp.wait_ge(stored, 32)

        @block.gpsimd
        def _(pool):
            pool.memset(k["acc"][:, :, :], 0.0)

        @block.tensor
        def _(pe):
            def project(n, b, j):
                if n >= 2:
                    pe.wait_ge(*bank_read[n - 2])
                i = 0
                for w, x in ((w_hi, k["x_hi"]), (w_hi, k["x_lo"]), (w_lo, k["x_hi"])):
                    for c in range(KT):
                        last = pe.matmul(p_proj[n % 2][:, :], w[:, c, j * P:(j + 1) * P],
                                         x[:, c, b * SEQ:(b + 1) * SEQ], start=(i == 0), stop=(i == 3 * KT - 1))
                        i += 1
                last.then_inc(proj_done, 1)

            bank_read = [(evicted_a, b + 1) for b in range(BATCH)]
            for b in range(BATCH):
                bank_read += [(evicted_a, BATCH + b + 1), (evicted_v, b + 1)]
            for b in range(BATCH):
                project(b, b, 2)
            pe.wait_ge(sizes, 1)
            pe.matmul(p_cq[0][:, 0:3], ones, sum3[:, :], start=True, stop=True).then_inc(mean_done, 1)
            for b in range(BATCH):
                for j in range(2):
                    project(BATCH + 2 * b + j, b, j)
                if b == 1:
                    pe.wait_ge(cum_ready, 1)
                    for t in range(TILES):
                        h, c = t // (TILES // 2), t % (TILES // 2)
                        last = pe.transpose(p_ct[h][:, c * HEADS:(c + 1) * HEADS], cum[:, t * P:(t + 1) * P],
                                            k["ident"][0:HEADS, 0:HEADS])
                    last.then_inc(ct_done, 1)
                if b:
                    pe.wait_ge(cb_masked, b)
                    pe.wait_ge(bt_copied, b)
                pe.wait_ge(evicted_a, BATCH + b + 1)
                pe.wait_ge(evicted_v, b + 1)
                for q in range(CHUNKS):
                    at = slice((b * CHUNKS + q) * P, (b * CHUNKS + q + 1) * P)
                    last = pe.matmul(p_cb[:, q, :], b_t[:, at], k["c_t"][:, at], start=True, stop=True)
                last.then_inc(cb_done, 1)
                for q in range(CHUNKS):
                    at = slice((b * CHUNKS + q) * P, (b * CHUNKS + q + 1) * P)
                    last = pe.transpose(p_bt[:, q, :], b_t[:, at], k["ident"][:, :])
                last.then_inc(bt_done, 1)
            pe.wait_ge(tok_ready, 2)
            pe.wait_ge(ln_in, 1)
            for h in range(2):
                last = pe.matmul(p_cq[h][:, 0:HC], pick_last[:, :], cum_tok[:, h * HC:(h + 1) * HC],
                                 start=True, stop=True)
            last.then_inc(cq_done, 1)

        @block.scalar
        def _(act):
            act.wait_ge(biases, 2 * 16)
            act.activation(neg_a[:, :], a_log[:, :], ACT.Exp).then_inc(steps_a, 1)
            for b in range(BATCH):
                at = slice(b * SEQ, (b + 1) * SEQ)
                act.wait_ge(proj_done, b + 1)
                act.activation(dt_pre[:, at], p_proj[b % 2][0:HEADS, :], ACT.Identity,
                               bias=dt_bias[:, 0:1]).then_inc(evicted_a, 1)
            act.wait_ge(evicted_a, BATCH)
            act.wait_ge(consts, 3)
            act.activation(soft[:, :], dt_pre[:, :], ACT.Abs).then_inc(steps_a, 1)
            act.wait_ge(steps_a, 2)
            act.activation(soft[:, :], soft[:, :], ACT.Exp, scale=-1.0).then_inc(steps_a, 1)
            act.wait_ge(steps_a, 3)
            act.activation(soft[:, :], soft[:, :], ACT.Ln, bias=1.0).then_inc(steps_a, 1)
            act.wait_ge(ln_in, 1)
            act.activation(k["ath"][:, :], den[:, :], ACT.Ln).then_inc(ln_done, 1)
            for b in range(BATCH):
                act.wait_ge(proj_done, BATCH + 2 * b + 1)
                act.activation(b_t[:, b * SEQ:(b + 1) * SEQ], p_proj[0][:, :], ACT.Identity).then_inc(evicted_a, 1)
                if b == 1:
                    act.wait_ge(cum_ready, 1)
                    act.activation(cum_hi[:, :], cum[:, :], ACT.Identity).then_inc(hi_ready, 1)
                act.wait_ge(bt_done, b + 1)
                act.activation(k["b_tok"][:, b * CHUNKS:(b + 1) * CHUNKS, :], p_bt[:, :, :], ACT.Identity
                               ).then_inc(bt_copied, 1)
                if b == 1:
                    act.wait_ge(tok_ready, 2)
                    act.activation(k["e_cum"][:, :], cum_tok[:, :], ACT.Exp)
            act.wait_ge(cq_done, 1)
            for h in range(2):
                act.activation(k["e_all"][:, h * HC:(h + 1) * HC], p_cq[h][:, 0:HC], ACT.Exp).then_inc(steps_a, 1)
            act.wait_ge(diff_ready, 2)
            act.activation(k["e_rest"][:, :], k["e_rest"][:, :], ACT.Exp)

        @block.vector
        def _(dve):
            dve.wait_ge(loaded, 6 * 16)
            dve.tensor_copy(k["ident_b"][:, :], k["ident"][:, :]).then_inc(consts, 1)
            dve.tensor_copy(k["rows"][:, :, :], rows_f).then_inc(consts, 1)
            dve.tensor_copy(k["cols"][:, :, :], cols_f).then_inc(consts, 1)
            dve.tensor_reduce(sum3[:, :], k["w_sum"][:, :].rearrange("p (w c) -> p w c", w=3), AX.X, ALU.add
                              ).then_inc(sizes, 1)
            dve.wait_ge(mean_done, 1)
            dve.tensor_scalar(s3[:, :], p_cq[0][:, 0:3], 1.0 / (HIDDEN * DIM), None, ALU.mult).then_inc(sizes, 1)
            dve.wait_ge(sizes, 2)
            dve.tensor_scalar(inv3[:, :], s3[:, :], EPS_BIT, None, ALU.add).then_inc(sizes, 1)
            dve.tensor_scalar(den[:, :], s3[:, :], -1.0, 1.0, ALU.mult, ALU.add).then_inc(sizes, 1)
            dve.wait_ge(sizes, 4)
            dve.reciprocal(inv3[:, :], inv3[:, :]).then_inc(sizes, 1)
            dve.reciprocal(den[:, :], den[:, :]).then_inc(sizes, 1)
            dve.wait_ge(sizes, 6)
            dve.tensor_copy(k["inv_all"][:, :].rearrange("p (w c) -> p w c", w=3),
                            inv3[:, :].unsqueeze(2).to_broadcast([P, 3, GROUPS // 3]))
            dve.scalar_tensor_tensor(out=den[:, :], in0=s3[:, :], scalar=1.0, in1=den[:, :],
                                     op0=ALU.add, op1=ALU.mult).then_inc(ln_in, 1)
            dve.wait_ge(ln_done, 1)
            dve.tensor_scalar(k["ath"][:, :], k["ath"][:, :], 0.5 / 127.0, None, ALU.mult)
            dve.wait_ge(steps_a, 4)
            dve.scalar_tensor_tensor(out=soft[:, :], in0=dt_pre[:, :], scalar=0.0, in1=soft[:, :],
                                     op0=ALU.max, op1=ALU.add).then_inc(steps_v, 1)

            def copy_c(b):
                dve.wait_ge(proj_done, BATCH + 2 * b + 2)
                dve.tensor_copy(k["c_t"][:, b * SEQ:(b + 1) * SEQ], p_proj[1][:, :]).then_inc(evicted_v, 1)

            def mask_cb(b):
                dve.wait_ge(cb_done, b + 1)
                dve.tensor_tensor(k["cb"][:, b * CHUNKS:(b + 1) * CHUNKS, :], p_cb[:, :, :],
                                  tri[:, :].unsqueeze(1).to_broadcast([P, CHUNKS, P]), ALU.mult
                                  ).then_inc(cb_masked, 1)

            dve.wait_ge(steps_v, 1)
            dve.tensor_scalar(soft[:, :], soft[:, :], neg_a[:, 0:1], -1.0, ALU.mult, ALU.mult).then_inc(steps_v, 1)
            copy_c(0)
            dve.wait_ge(steps_v, 2)
            dve.wait_ge(keep_in, 16)
            dve.tensor_tensor_scan(cum[:, :], dt_pre[:, :], soft[:, :], 0.0, ALU.mult, ALU.add).then_inc(cum_ready, 1)
            mask_cb(0)
            copy_c(1)
            dve.wait_ge(ct_done, 1)
            for h in range(2):
                dve.tensor_copy(cum_tok[:, h * HC:(h + 1) * HC], p_ct[h][:, 0:HC]).then_inc(tok_ready, 1)
            mask_cb(1)
            dve.wait_ge(hi_ready, 1)
            dve.tensor_tensor(cum_lo[:, :], cum[:, :], cum_hi[:, :], ALU.subtract).then_inc(lo_ready, 1)
            for b in (2, 3):
                copy_c(b)
                mask_cb(b)
            dve.wait_ge(tok_ready, 2)
            dve.wait_ge(steps_a, 6)
            for h in range(2):
                dve.tensor_tensor(k["e_rest"][:, h * HC:(h + 1) * HC], p_cq[h][:, 0:HC],
                                  cum_tok[:, h * HC:(h + 1) * HC], ALU.subtract).then_inc(diff_ready, 1)


def count(per_group, g, local):
    return g * per_group + local


def mixer(nc, d, k):
    with ExitStack() as ctx:
        def sb(name, shape, dt=F32):
            return ctx.enter_context(nc.sbuf_tensor(name, shape, dt))

        def sem(name):
            return ctx.enter_context(nc.semaphore("mx_" + name))

        PIECE = WCOLS // 4
        stage = sb("stage", [P, 2, DIM])
        wi_hi = sb("wi_hi", [P, 2 * GT, KT, P], F32R)
        wi_lo = sb("wi_lo", [P, 2 * GT, KT, P], F32R)
        wo_hi = sb("wo_hi", [P, GT, DIM], F32R)
        wo_lo = sb("wo_lo", [P, GT, DIM], F32R)
        half = sb("half", [P, 12])
        params = sb("params", [P, 18])
        inv_now = sb("inv_now", [P, 1])
        piece = sb("piece", [P, PIECE], BF16)
        d_now = sb("d_now", [P, GH])
        all_now = sb("all_now", [P, TILES, GH])
        pad = sb("pad", [P, GT, TAPS - 1 + SEQ])
        conv = sb("conv", [P, GT, SEQ])
        th_x = sb("th_x", [P, SEQ])
        z2 = sb("z2", [P, 2, GT, SEQ])
        x_tok = sb("x_tok", [P, 2, CHUNKS, GC])
        m_t = sb("m_t", [P, 2, GH, P])
        x_dec = sb("x_dec", [P, GH, HEAD])
        xd = sb("xd", [P, GH, HEAD])
        y = sb("y", [P, 2, GC])
        h_first = sb("h_first", [P, GH, HEAD])
        h_next = sb("h_next", [P, GH, HEAD])
        h_dec = sb("h_dec", [P, GH, HEAD])
        sq = sb("sq", [P, GC], BF16)
        gate = sb("gate", [P, GT, P])
        g_hi = sb("g_hi", [P, 2, GT, P], F32R)
        g_lo = sb("g_lo", [P, 2, GT, P], F32R)

        def bank(name, shape):
            return ctx.enter_context(nc.psum_tensor(name, shape, F32))

        p_proj = [bank(f"p_proj{i}", [P, SEQ]) for i in range(2)]
        p_d = bank("p_d", [P, GH, P])
        p_y = bank("p_y", [P, 2, GH, HEAD])
        p_s = bank("p_s", [P, 512])
        p_yt = bank("p_yt", [P, 512])
        p_xt = bank("p_xt", [P, CHUNKS, P])
        p_o = bank("p_o", [P, DIM])

        raw_in = [sem(f"raw_in{i}") for i in range(2)]
        par_in = sem("par_in")
        tanh_done, piece_done, piece_stored = sem("tanh"), sem("piece"), sem("pstored")
        rows_in = [sem(f"rows_in{i}") for i in range(2)]
        h_in = sem("h_in")
        w_hi_done, w_lo_done = sem("w_hi"), sem("w_lo")
        par_done = sem("par")
        tables_done = sem("tables")
        proj_done = sem("proj")
        raw_done, tap_done = sem("raw"), sem("tap")
        conv_done = sem("conv")
        xth_done, zth_done = sem("xth"), sem("zth")
        x_done, z_done = sem("x"), sem("z")
        xt_done, xtok_done = sem("xt"), sem("xtok")
        d_done, relu_done, e_done, m_done = sem("d"), sem("relu"), sem("e"), sem("m")
        y_mm, ys_done, xd_done, yx_done, y_done = sem("y_mm"), sem("ys"), sem("xd"), sem("yx"), sem("y")
        xdec_done, s_done, hdec_done, h_done = sem("xdec"), sem("s"), sem("hdec"), sem("h")
        yt_done, gate_done, ghi_done, glo_done = sem("yt"), sem("gate"), sem("ghi"), sem("glo")
        sq_done, o_done, acc_done = sem("sq"), sem("o"), sem("acc")

        def wait(eng, s, per_group, g, local, unit=1):
            v = count(per_group, g, local)
            if isinstance(v, int) and v <= 0:
                return
            eng.wait_ge(s, v * unit)

        PIECE_SLOTS = (4, 7, 13, 15)

        def exists(g, slot):
            return not isinstance(g, int) or 0 <= g * SLOTS + slot < GROUPS * SLOTS

        def groups(eng, body):
            for s in range(-4, SLOTS):
                body(0, s)
            with eng.Fori(1, GROUPS - 1) as g:
                for s in range(SLOTS):
                    body(g, s)
            for s in range(SLOTS + 2):
                body(GROUPS - 1, s)

        def kind(s):
            return (s + 4) // 4, s % 4, s % 4 < GT

        def x_count(i, j):
            return GT * i + j + 1

        def state_count(i, q):
            return (CHUNKS - 1) * i + min(q + 1, CHUNKS - 1)

        block = ctx.enter_context(nc.Block())

        @block.sync
        def _(sp):
            def load_weights(g, n, src):
                if n < 2:
                    wait(sp, piece_done, 4, g, 0)
                    wait(sp, w_lo_done, 6, g, 4)
                elif n < 4:
                    wait(sp, piece_done, 4, g, n - 1)
                else:
                    wait(sp, w_lo_done, 6, g, 4 + n - 1)
                sp.dma_start(stage[:, n % 2, :], src).then_inc(raw_in[n % 2], 16)

            def load_piece(g, i):
                if i >= 2 and not exists(g, SLOTS):
                    wait(sp, piece_done, 4, g, i - 1)
                else:
                    wait(sp, w_lo_done, 6, g, 4 + i + 1 + (2 if i >= 2 else 0))
                sp.dma_start(stage[:, i % 2, 0:PIECE], d["w_ffn"][g, :, i * PIECE:(i + 1) * PIECE]
                             ).then_inc(raw_in[i % 2], 16)

            def store_piece(g, i):
                wait(sp, piece_done, 4, g, i + 1)
                sp.dma_start(d["tern"][g, :, i * PIECE // 2:(i + 1) * PIECE // 2], piece[:, :].bitcast(F32)).then_inc(piece_stored, 16)

            def load_params(g):
                wait(sp, par_done, 2, g, 0)
                sp.dma_start(params[:, :], d["params"][g]).then_inc(par_in, 16)

            def load_rows(g, s):
                wait(sp, d_done, 16, g, s - 1)
                at = slice((s % SLOTS) * P, (s % SLOTS + 1) * P)
                gg = g + s // SLOTS
                heads = bass.ds(gg * GH, GH)
                sp.dma_start(k["rows"][0:2, s % 2, :].bitcast(F32).rearrange("r (h t) -> r h t", h=GH),
                             d["cum"][:, heads, at]).then_inc(rows_in[s % 2], 16)
                for part in range(2):
                    sp.dma_start(k["cols"][2 + part * GH:2 + (part + 1) * GH, s % 2, :].bitcast(F32),
                                 d["cum"][part, heads, at]).then_inc(rows_in[s % 2], 16)

            def body(g, s):
                if s == -4:
                    load_params(0)
                    for n in range(2, 6):
                        if n >= 4:
                            wait(sp, w_lo_done, 6, 0, n - 3)
                        sp.dma_start(stage[:, n % 2, :], d["w_in"][0, n - 2]).then_inc(raw_in[n % 2], 16)
                    sp.dma_start(h_first[:, :, :], d["h_first"][0]).then_inc(h_in, 16)
                    for n in range(2):
                        load_rows(0, n)
                if s == 5:
                    store_piece(g, 0)
                if s == 8:
                    store_piece(g, 1)
                if s == 14:
                    store_piece(g, 2)
                if s == 1 and not (isinstance(g, int) and g == 0):
                    store_piece(g - 1, 3)
                if s == SLOTS + 1:
                    store_piece(g, 3)
                if s == 0:
                    for n in range(2):
                        load_weights(g, n, d["w_out"][g, n])
                if 0 <= s and exists(g, s + 2):
                    load_rows(g, s + 2)
                if s in (2, 3):
                    load_piece(g, s - 2)
                if s == 12:
                    for i in (2, 3):
                        load_piece(g, i)
                if s in (6, 8, 9, 10) and exists(g, SLOTS):
                    j = (6, 8, 9, 10).index(s)
                    load_weights(g, j + 2, d["w_in"][g + 1, j])
                if s == 4 and exists(g, SLOTS):
                    load_params(g + 1)
                if s == 14 and exists(g, SLOTS):
                    wait(sp, y_mm, 16, g, 13)
                    wait(sp, hdec_done, 12, g, 10)
                    sp.dma_start(h_first[:, :, :], d["h_first"][g + 1]).then_inc(h_in, 16)
            groups(sp, body)
            sp.wait_ge(piece_stored, 16 * 4 * GROUPS)

        @block.tensor
        def _(pe):
            def split_products(out, *passes):
                for p, (w, x, before) in enumerate(passes):
                    if before is not None:
                        wait(pe, *before)
                    for c in range(len(w)):
                        last = pe.matmul(out, w[c], x[c], start=(p == 0 and c == 0),
                                         stop=(p == len(passes) - 1 and c == len(w) - 1))
                return last

            def body(g, s):
                if exists(g, s + 1):
                    wait(pe, relu_done, 16, g, s + 1)
                    wait(pe, rows_in[(s + 1) % 2], 24, g, 3 * ((s + 1) // 2 + 1), 16)
                    pe.matmul(p_d[:, :, :], k["cols"][:, (s + 1) % 2, :],
                              k["rows"][:, (s + 1) % 2, :].rearrange("r (h t) -> r h t", h=GH),
                              start=True, stop=True).then_inc(d_done, 1)
                if exists(g, s + 4):
                    i, j, is_x = kind(s)
                    b = i % BATCH
                    if i % BATCH == 0:
                        wait(pe, w_lo_done, 6, g, (6 if i else 0) + j + 1)
                    if is_x:
                        wait(pe, z_done, 8, g, x_count(i - 1, j))
                    else:
                        wait(pe, raw_done, 8, g, x_count(i, j - GT))
                        wait(pe, tap_done, 8, g, x_count(i, j - GT))
                    at = slice(b * SEQ, (b + 1) * SEQ)
                    w_hi, w_lo = ([w[:, j, c, :] for c in range(KT)] for w in (wi_hi, wi_lo))
                    x_hi, x_lo = ([k[x][:, c, at] for c in range(KT)] for x in ("x_hi", "x_lo"))
                    split_products(p_proj[j % 2][:, :], (w_hi, x_hi, None), (w_hi, x_lo, None), (w_lo, x_hi, None)
                                   ).then_inc(proj_done, 1)
                if exists(g, s - 2):
                    wait(pe, acc_done, 16, g, s - 2)
                    y_hi, y_lo = ([y_part[:, s % 2, c, :] for c in range(GT)] for y_part in (g_hi, g_lo))
                    w_hi, w_lo = ([w[:, c, :] for c in range(GT)] for w in (wo_hi, wo_lo))
                    rounded, rest = (ghi_done, 16, g, s - 1), (glo_done, 16, g, s - 1)
                    if s == 2:
                        wait(pe, w_hi_done, 6, g, 6)
                        last = split_products(p_o[:, :], (y_hi, w_hi, rounded), (y_lo, w_hi, rest),
                                              (y_hi, w_lo, (w_lo_done, 6, g, 6)))
                    else:
                        last = split_products(p_o[:, :], (y_hi, w_hi, rounded), (y_hi, w_lo, None),
                                              (y_lo, w_hi, rest))
                    last.then_inc(o_done, 1)
                i, q = s // CHUNKS, s % CHUNKS
                if exists(g, s):
                    wait(pe, y_done, 16, g, s)
                    if q == 0:
                        state = h_first
                        if i == 0:
                            wait(pe, h_in, 1, g, 1, 16)
                        wait(pe, xtok_done, 8, g, x_count(i, GT - 1))
                    else:
                        state = h_next
                        wait(pe, h_done, 12, g, state_count(i, q - 1))
                    at = slice((s % SLOTS) * P, (s % SLOTS + 1) * P)
                    pe.matmul(p_y[:, 1, :, :], k["c_t"][:, at], state[:, :, :], start=True, stop=True)
                    wait(pe, m_done, 16, g, s + 1)
                    for h in range(GH):
                        last = pe.matmul(p_y[:, 0, h, :], m_t[:, s % 2, h, :],
                                         x_tok[:, i % 2, q, h * HEAD:(h + 1) * HEAD], start=True, stop=True)
                    last.then_inc(y_mm, 1)
                if q >= 2 and exists(g, s + 4):
                    j = q - 2
                    wait(pe, x_done, 8, g, x_count(i + 1, j))
                    wait(pe, xtok_done, 8, g, x_count(i + 1, j) - 1)
                    for c in range(CHUNKS):
                        last = pe.transpose(p_xt[:, c, :], conv[:, j, c * P:(c + 1) * P], k["ident"][:, :])
                    last.then_inc(xt_done, 1)
                if q < CHUNKS - 1 and exists(g, s):
                    wait(pe, xdec_done, 12, g, state_count(i, q))
                    wait(pe, h_done, 12, g, state_count(i, q) - 1)
                    pe.matmul(p_s[:, 0:GC], k["b_tok"][:, s % SLOTS, :],
                              x_dec[:, :, :].rearrange("p h c -> p (h c)"), start=True, stop=True
                              ).then_inc(s_done, 1)
                if exists(g, s - 1):
                    wait(pe, y_done, 16, g, s)
                    wait(pe, gate_done, 16, g, s - 1)
                    for c in range(GT):
                        last = pe.transpose(p_yt[:, c * P:(c + 1) * P], y[:, (s - 1) % 2, c * P:(c + 1) * P],
                                            k["ident"][:, :])
                    last.then_inc(yt_done, 1)
            groups(pe, body)

        @block.scalar
        def _(act):
            def weight_hi(g, n):
                if isinstance(g, int) and g < 0:
                    act.wait_ge(raw_in[n % 2], 16 * (n // 2))
                else:
                    wait(act, raw_in[n % 2], 5, g, 2 + (n // 2 + 1 if n < 2 else n // 2 + 2), 16)
                if n < 2:
                    wait(act, o_done, 16, g, 0)
                    wait(act, par_done, 2, g, 2)
                    act.activation(wo_hi[:, n, :], stage[:, n % 2, :], ACT.Identity,
                                   scale=half[:, 6 * n + 5:6 * n + 6]).then_inc(w_hi_done, 1)
                else:
                    wait(act, proj_done, 16, g, 12 + n - 2 + 1)
                    act.activation(wi_hi[:, n - 2, :, :].rearrange("p c m -> p (c m)"), stage[:, n % 2, :],
                                   ACT.Identity).then_inc(w_hi_done, 1)

            def piece_tanh(g, i):
                k_th = (2, 2, 5, 5)[i] if exists(g, SLOTS) or i < 2 else 3
                wait(act, raw_in[i % 2], 5, g, 2 + k_th, 16)
                wait(act, tables_done, 3, g, 3)
                act.activation(stage[:, i % 2, 0:PIECE], stage[:, i % 2, 0:PIECE], ACT.Tanh, scale=inv_now[:, 0:1]
                               ).then_inc(tanh_done, 1)

            def body(g, s):
                if s == -4:
                    for n in range(2, 6):
                        weight_hi(-1, n)
                if exists(g, s + 1):
                    wait(act, d_done, 16, g, s + 2)
                    wait(act, y_mm, 16, g, s)
                    act.activation(m_t[:, (s + 1) % 2, :, :], p_d[:, :, :], ACT.Relu, scale=-1.0).then_inc(relu_done, 1)
                    wait(act, relu_done, 16, g, s + 2)
                    act.activation(m_t[:, (s + 1) % 2, :, :], m_t[:, (s + 1) % 2, :, :], ACT.Exp, scale=-1.0
                                   ).then_inc(e_done, 1)
                if exists(g, s - 2):
                    wait(act, gate_done, 16, g, s - 1)
                    wait(act, o_done, 16, g, s - 3)
                    act.activation(g_hi[:, s % 2, :, :], gate[:, :, :], ACT.Identity).then_inc(ghi_done, 1)
                if exists(g, s - 1):
                    wait(act, y_done, 16, g, s)
                    wait(act, sq_done, 16, g, s - 1)
                    gg = g if s else g - 1
                    at = ((s - 1) % SLOTS) * GROUPS + gg
                    act.activation(sq[:, :], y[:, (s - 1) % 2, :], ACT.Square,
                                   accum_out=k["y_sq"][:, bass.ds(at, 1)]).then_inc(sq_done, 1)
                if s in PIECE_SLOTS:
                    piece_tanh(g, PIECE_SLOTS.index(s))
                i, j, is_x = kind(s)
                if exists(g, s + 4):
                    wait(act, proj_done, 16, g, 4 * i + j + 1)
                    if is_x:
                        wait(act, conv_done, 24, g, 3 * x_count(i - 1, j))
                        act.activation(pad[:, j, TAPS - 1:], p_proj[j % 2][:, :], ACT.Identity).then_inc(raw_done, 1)
                        wait(act, par_done, 2, g, 2 * (i // BATCH) + 2)
                        wait(act, xt_done, 8, g, x_count(i - 1, j))
                        act.activation(conv[:, j, :], p_proj[j % 2][:, :], ACT.Identity,
                                       bias=half[:, 6 * j + 4:6 * j + 5], scale=half[:, 6 * j + 3:6 * j + 4]
                                       ).then_inc(tap_done, 1)
                    else:
                        wait(act, gate_done, 16, g, 4 * (i - 1))
                        act.activation(z2[:, i % 2, j - GT, :], p_proj[j % 2][:, :], ACT.Tanh, scale=0.5
                                       ).then_inc(zth_done, 1)
                if s == 1:
                    for n in range(2):
                        weight_hi(g, n)
                if 8 <= s < 12 and exists(g, SLOTS):
                    weight_hi(g, s - 6)
                if j in (1, 2) and exists(g, s + 3):
                    wait(act, conv_done, 24, g, 3 * x_count(i, j - 1))
                    wait(act, x_done, 8, g, x_count(i, j - 1) - 1)
                    act.activation(th_x[:, :], conv[:, j - 1, :], ACT.Tanh).then_inc(xth_done, 1)
                i, q = s // CHUNKS, s % CHUNKS
                if q >= 2 and exists(g, s + 4):
                    j = q - 2
                    wait(act, xt_done, 8, g, x_count(i + 1, j))
                    wait(act, y_mm, 16, g, 4 * i)
                    wait(act, xd_done, 16, g, 4 * i)
                    wait(act, xdec_done, 12, g, 3 * i)
                    act.activation(x_tok[:, (i + 1) % 2, :, j * P:(j + 1) * P], p_xt[:, :, :], ACT.Identity
                                   ).then_inc(xtok_done, 1)
            groups(act, body)

        @block.vector
        def _(dve):
            def weight_lo(g, n):
                wait(dve, w_hi_done, 6, g, 4 + n + 1)
                if n < 2:
                    dve.scalar_tensor_tensor(out=wo_lo[:, n, :], in0=stage[:, n % 2, :],
                                             scalar=half[:, 6 * n + 5:6 * n + 6], in1=wo_hi[:, n, :],
                                             op0=ALU.mult, op1=ALU.subtract).then_inc(w_lo_done, 1)
                else:
                    dve.tensor_tensor(wi_lo[:, n - 2, :, :].rearrange("p c m -> p (c m)"), stage[:, n % 2, :],
                                      wi_hi[:, n - 2, :, :].rearrange("p c m -> p (c m)"), ALU.subtract
                                      ).then_inc(w_lo_done, 1)

            def parameters(g):
                wait(dve, par_in, 1, g, 1, 16)
                dve.tensor_scalar(half[:, :], params[:, 0:12], 0.5, None, ALU.mult).then_inc(par_done, 1)
                dve.tensor_copy(pad[:, :, 0:TAPS - 1], params[:, 12:18].rearrange("p (j t) -> p j t", j=GT)
                                ).then_inc(par_done, 1)

            def tables(g):
                dve.tensor_copy(d_now[:, :], k["d_row"][:, bass.ds(g * GH, GH)]).then_inc(tables_done, 1)
                dve.tensor_copy(all_now[:, :, :], k["e_all"][:, :].rearrange("p (t h) -> p t h", h=HEADS)
                                [:, :, bass.ds(g * GH, GH)]).then_inc(tables_done, 1)
                dve.tensor_copy(inv_now[:, :], k["inv_all"][:, bass.ds(g, 1)]).then_inc(tables_done, 1)

            def round_piece(g, i):
                wait(dve, tanh_done, 4, g, i + 1)
                wait(dve, piece_stored, 4, g, i, 16)
                dve.tensor_scalar(piece[:, :], stage[:, i % 2, 0:PIECE], MAGIC, -MAGIC, ALU.add, ALU.add
                                  ).then_inc(piece_done, 1)

            def per_head(e, t, g):
                return e[:, bass.ds(g * GH + t * HEADS, GH)].unsqueeze(2).to_broadcast([P, GH, HEAD])

            def body(g, s):
                if s == -4:
                    parameters(0)
                    tables(0)
                    for n in range(2, 6):
                        weight_lo(-1, n)
                if exists(g, s - 2):
                    wait(dve, yt_done, 16, g, s - 1)
                    wait(dve, glo_done, 16, g, s - 2)
                    i, q = (s - 2) // CHUNKS, (s - 2) % CHUNKS
                    wait(dve, z_done, 8, g, x_count(i, GT - 1))
                    dve.tensor_tensor(gate[:, :, :], p_yt[:, 0:GC].rearrange("p (c t) -> p c t", c=GT),
                                      z2[:, i % 2, :, q * P:(q + 1) * P], ALU.mult).then_inc(gate_done, 1)
                i, q = s // CHUNKS, s % CHUNKS
                if q < CHUNKS - 1 and exists(g, s):
                    wait(dve, xtok_done, 8, g, x_count(i, GT - 1))
                    wait(dve, s_done, 12, g, state_count(i, q) - 1)
                    dve.tensor_tensor(x_dec[:, :, :],
                                      x_tok[:, i % 2, q, :].rearrange("p (h c) -> p h c", h=GH),
                                      per_head(k["e_rest"], s % SLOTS, g), ALU.mult).then_inc(xdec_done, 1)
                if exists(g, s - 2):
                    wait(dve, ghi_done, 16, g, s - 1)
                    dve.tensor_tensor(g_lo[:, s % 2, :, :], gate[:, :, :], g_hi[:, s % 2, :, :], ALU.subtract
                                      ).then_inc(glo_done, 1)
                if s == 2:
                    for n in range(2):
                        weight_lo(g, n)
                i, j, is_x = kind(s)
                if j in (2, 3) and exists(g, s + 2):
                    wait(dve, xth_done, 8, g, x_count(i, j - 2))
                    dve.scalar_tensor_tensor(out=conv[:, j - 2, :], in0=th_x[:, :], scalar=1.0,
                                             in1=conv[:, j - 2, :], op0=ALU.add, op1=ALU.mult).then_inc(x_done, 1)
                i, j, is_x = kind(s - 1)
                if s > -4 and exists(g, s + 3):
                    if is_x:
                        n = x_count(i, j)
                        wait(dve, raw_done, 8, g, n)
                        wait(dve, par_done, 2, g, 2 * (i // BATCH) + 2)
                        wait(dve, tap_done, 8, g, n)
                        for tap in range(TAPS - 1):
                            wait(dve, conv_done, 24, g, 3 * (n - 1) + tap)
                            dve.scalar_tensor_tensor(out=conv[:, j, :], in0=pad[:, j, tap:tap + SEQ],
                                                     scalar=half[:, 6 * j + tap:6 * j + tap + 1], in1=conv[:, j, :],
                                                     op0=ALU.mult, op1=ALU.add).then_inc(conv_done, 1)
                    else:
                        n = x_count(i, j - GT)
                        wait(dve, zth_done, 8, g, n)
                        dve.scalar_tensor_tensor(out=z2[:, i % 2, j - GT, :], in0=z2[:, i % 2, j - GT, :], scalar=1.0,
                                                 in1=p_proj[j % 2][:, :], op0=ALU.add, op1=ALU.mult
                                                 ).then_inc(z_done, 1)
                if exists(g, s + 1):
                    wait(dve, e_done, 16, g, s + 2)
                    dve.tensor_tensor(m_t[:, (s + 1) % 2, :, :], m_t[:, (s + 1) % 2, :, :],
                                      k["cb"][:, (s + 1) % SLOTS, :].unsqueeze(1).to_broadcast([P, GH, P]), ALU.mult
                                      ).then_inc(m_done, 1)
                if 8 <= s < 12 and exists(g, SLOTS):
                    weight_lo(g, s - 6)
                if s in PIECE_SLOTS:
                    round_piece(g, PIECE_SLOTS.index(s))
                i, q = s // CHUNKS, s % CHUNKS
                yv = y[:, s % 2, :].rearrange("p (h c) -> p h c", h=GH)
                if exists(g, s):
                    t = s % SLOTS
                    wait(dve, y_mm, 16, g, s + 1)
                    wait(dve, yt_done, 16, g, s - 1)
                    wait(dve, sq_done, 16, g, s - 1)
                    dve.tensor_tensor(yv, p_y[:, 1, :, :], per_head(k["e_cum"], t, g), ALU.mult
                                      ).then_inc(ys_done, 1)
                    if q < CHUNKS - 1:
                        wait(dve, s_done, 12, g, state_count(i, q))
                        wait(dve, hdec_done, 12, g, state_count(i, q))
                        dve.tensor_tensor(h_next[:, :, :], h_dec[:, :, :],
                                          p_s[:, 0:GC].rearrange("p (h c) -> p h c", h=GH), ALU.add
                                          ).then_inc(h_done, 1)
                if exists(g, s - 2):
                    wait(dve, o_done, 16, g, s - 1)
                    t = (s - 2) % SLOTS
                    dve.tensor_tensor(k["acc"][:, t, :], k["acc"][:, t, :], p_o[:, :], ALU.add
                                      ).then_inc(acc_done, 1)
                if exists(g, s):
                    wait(dve, yx_done, 16, g, s + 1)
                    dve.tensor_tensor(yv, yv, p_y[:, 0, :, :], ALU.add).then_inc(y_done, 1)
                if s == 15 and exists(g, SLOTS):
                    tables(g + 1)
                if s == 10 and exists(g, SLOTS):
                    wait(dve, tap_done, 8, g, 8)
                    wait(dve, conv_done, 24, g, 24)
                    parameters(g + 1)
            groups(dve, body)

        @block.gpsimd
        def _(pool):
            def per_head(e):
                return e.unsqueeze(2).to_broadcast([P, GH, HEAD])

            def body(g, s):
                if not exists(g, s) or s < 0:
                    return
                i, q, t = s // CHUNKS, s % CHUNKS, s % SLOTS
                wait(pool, xtok_done, 8, g, x_count(i, GT - 1))
                wait(pool, yx_done, 16, g, s)
                if s == 0:
                    wait(pool, tables_done, 3, g, 3)
                pool.tensor_tensor(xd[:, :, :], x_tok[:, i % 2, q, :].rearrange("p (h c) -> p h c", h=GH),
                                   per_head(d_now[:, :]), ALU.mult).then_inc(xd_done, 1)
                if q < CHUNKS - 1:
                    if q == 0:
                        state = h_first
                        if i == 0:
                            wait(pool, h_in, 1, g, 1, 16)
                    else:
                        state = h_next
                    wait(pool, h_done, 12, g, state_count(i, q) - 1)
                    pool.tensor_tensor(h_dec[:, :, :], state[:, :, :],
                                       per_head(all_now[:, t, :]), ALU.mult).then_inc(hdec_done, 1)
                wait(pool, ys_done, 16, g, s + 1)
                wait(pool, xd_done, 16, g, s + 1)
                yv = y[:, s % 2, :].rearrange("p (h c) -> p h c", h=GH)
                pool.tensor_tensor(yv, yv, xd[:, :, :], ALU.add).then_inc(yx_done, 1)
            groups(pool, body)


def ffn(nc, d, k):
    with ExitStack() as ctx:
        def sb(name, shape, dt=F32):
            return ctx.enter_context(nc.sbuf_tensor(name, shape, dt))

        def sem(name):
            return ctx.enter_context(nc.semaphore("ff_" + name))

        h1 = k["acc"]
        n_w = 3 * HIDDEN * DIM // P // WCOLS
        per_w = n_w // 3
        NQ = HIDDEN // DIM
        HH = HT // 2
        tern = sb("tern", [P, 3, KT * HIDDEN], BF16)
        AHEAD = 4
        resid = sb("ff_resid", [P, AHEAD, DIM])
        g12 = sb("g12", [P, 2, DIM])
        g3 = sb("g3", [P, HIDDEN])
        stats = sb("ff_stats", [P, TILES, 6])
        mv = sb("ff_mv", [P, TILES, 2])
        names = ("ff_r", "ff_tmp", "ff_v", "ff_rn", "ff_minus")
        r, tmp, v, rn, minus_mean = (sb(n, [P, TILES]) for n in names)
        ath = k["ath"]
        u12 = sb("u12", [P, 2, DIM])
        size12, top12, scale12 = (sb(n, [P, 2]) for n in ("size12", "top12", "scale12"))
        deq12 = sb("deq12", [P, 2, 2])
        q12 = sb("q12", [P, 2, DIM], BF16)
        q_t = sb("q_t", [P, 2, 2 * KT, P], BF16)
        sw = sb("sw", [P, 2, DIM])
        h = sb("ff_h", [P, 2, HIDDEN])
        u3 = sb("u3", [P, 2, HIDDEN])
        hsq = sb("hsq", [P, HIDDEN], BF16)
        hss = sb("hss", [P, 2])
        size3, ms3, rb3, t3, top3, scale3 = (sb(n, [P, 1]) for n in ("size3", "ms3", "rb3", "t3", "top3", "scale3"))
        deq3 = sb("deq3", [P, 2])
        q3 = sb("q3", [P, HIDDEN], BF16)
        q3_t = sb("q3_t", [P, HT, P], BF16)
        res = sb("res", [P, 2, DIM])

        def bank(name, shape, dt=F32):
            return ctx.enter_context(nc.psum_tensor(name, shape, dt))

        p1 = [bank(f"p_w1_{i}", [P, DIM]) for i in range(2)]
        p2 = [bank(f"p_w2_{i}", [P, DIM]) for i in range(2)]
        p_q = bank("p_q", [P, 2 * KT, P], BF16)
        p_h = [bank(f"p_h{i}", [P, HH, P], BF16) for i in range(2)]
        p_o = bank("p_out", [P, DIM])

        loaded, g3_loaded, first = sem("loaded"), sem("g3_loaded"), sem("first")
        resid_in = [sem(f"resid{i}") for i in range(AHEAD)]
        h1_done, up_in, down_in = sem("h1"), sem("up_in"), sem("down_in")
        prep_step, u12_done, deq_done = sem("prep_step"), sem("u12"), sem("deq")
        q12_done, qt_done, qtc_done = sem("q12"), sem("qt"), sem("qtc")
        w12_done, sw_done, h_done = sem("w12"), sem("sw"), sem("h")
        hss_done, u3_ready = sem("hss"), sem("u3r")
        hid_step, u3_done, q3_done = sem("hid_step"), sem("u3"), sem("q3")
        deq3_done = sem("deq3")
        ht_done, htc_done, o_done, res_done = sem("ht"), sem("htc"), sem("o"), sem("res")
        out_done = [sem(f"out{i}") for i in range(2)]
        PREP_STEPS, HIDDEN_STEPS = 6, 16

        def wait(eng, s, per_tile, t, local=0, unit=1):
            g, k_th = t
            value = (2 * per_tile * unit) * g + (per_tile * k_th + local) * unit
            if isinstance(value, int) and value <= 0:
                return
            eng.wait_ge(s, value)

        def tile(t, off):
            return t[0], t[1] + off

        def exists(t):
            return not isinstance(t[0], int) or 0 <= 2 * t[0] + t[1] < TILES

        def number(t):
            return 2 * t[0] + t[1]

        def slots(eng, body):
            for t in range(6):
                body((0, t))
            with eng.Fori(3, TILES // 2 - 1) as g:
                for t in range(2):
                    body((g, t))
            for t in range(TILES - 2, TILES + 3):
                body((0, t))

        block = ctx.enter_context(nc.Block())

        @block.sync
        def _(sp):
            def residual(n):
                if n >= AHEAD:
                    sp.wait_ge(h1_done, n - AHEAD + 1)
                sp.dma_start(resid[:, n % AHEAD, :], d["resid"][n]).then_inc(resid_in[n % AHEAD], 16)

            for n in range(TILES):
                residual(n)
                if n % 2:
                    i = n // 2
                    sp.dma_start(tern[:, i // per_w, (i % per_w) * WCOLS:(i % per_w + 1) * WCOLS].bitcast(F32), d["tern"][i]
                                 ).then_inc(up_in, 16)
                if n == 1:
                    for w in range(2):
                        sp.dma_start(g12[:, w, :], d["g12"][w].partition_broadcast(P)).then_inc(loaded, 16)
            sp.dma_start(g3[:, :], d["g3"].partition_broadcast(P)).then_inc(g3_loaded, 16)
            for i in range(per_w):
                sp.dma_start(tern[:, 2, i * WCOLS:(i + 1) * WCOLS].bitcast(F32), d["tern"][2 * per_w + i]).then_inc(down_in, 16)

            def body(t):
                u = tile(t, -3)
                if exists(u):
                    wait(sp, res_done, 1, u, 1)
                    sp.dma_start(d["out"][bass.ds(number(u) * P, P), :], res[:, u[1] % 2, :]
                                 ).then_inc(out_done[u[1] % 2], 16)
            slots(sp, body)
            for i in range(2):
                sp.wait_ge(out_done[i], 16 * TILES // 2)

        @block.tensor
        def _(pe):
            def turn_inputs(t):
                wait(pe, q12_done, 2, t, 2)
                wait(pe, qtc_done, 1, t)
                for w in range(2):
                    for c in range(KT):
                        last = pe.transpose(p_q[:, w * KT + c, :], q12[:, w, c * P:(c + 1) * P], k["ident_b"][:, :])
                last.then_inc(qt_done, 1)

            def turn_hidden(t, half):
                wait(pe, q3_done, 1, t, 1)
                wait(pe, htc_done, 2, t, half - 1)
                for c in range(HH):
                    at = (half * HH + c) * P
                    last = pe.transpose(p_h[half][:, c, :], q3[:, at:at + P], k["ident_b"][:, :])
                last.then_inc(ht_done, 1)

            def up(t, n):
                wait(pe, qtc_done, 1, t, 1)
                wait(pe, h_done, NQ, t, n - 1)
                for w, p in ((0, p1), (1, p2)):
                    for c in range(KT):
                        at = c * HIDDEN + n * DIM
                        last = pe.matmul(p[n % 2][:, :], q_t[:, t[1] % 2, w * KT + c, :], tern[:, w, at:at + DIM],
                                         start=(c == 0), stop=(c == KT - 1))
                last.then_inc(w12_done, 1)

            def down(t):
                wait(pe, res_done, 1, t)
                for c in range(HT):
                    if c % HH == 0:
                        wait(pe, htc_done, 2, t, 1 + c // HH)
                    last = pe.matmul(p_o[:, :], q3_t[:, c, :], tern[:, 2, c * DIM:(c + 1) * DIM],
                                     start=(c == 0), stop=(c == HT - 1))
                last.then_inc(o_done, 1)

            turn_inputs((0, 0))
            pe.wait_ge(up_in, 16 * 2 * per_w)

            def body(t):
                back = tile(t, -2)
                if isinstance(t[0], int) and t[1] == 2:
                    pe.wait_ge(down_in, 16 * per_w)
                for n in range(NQ):
                    if exists(t):
                        up(t, n)
                    if n in (1, 2) and exists(back):
                        turn_hidden(back, n - 1)
                    if n == 3 and exists(tile(t, 1)):
                        turn_inputs(tile(t, 1))
                if exists(back):
                    down(back)
            slots(pe, body)

        @block.scalar
        def _(act):
            def scaled_inputs(t):
                wait(act, prep_step, PREP_STEPS, t, PREP_STEPS)
                for w in range(2):
                    act.activation(u12[:, w, :], u12[:, w, :], ACT.Copy, scale=scale12[:, w:w + 1], bias=MAGIC
                                   ).then_inc(u12_done, 1)

            def quantised_inputs(t):
                for w in range(2):
                    wait(act, u12_done, 2, t, w + 1)
                    wait(act, qt_done, 1, t)
                    act.activation(q12[:, w, :], u12[:, w, :], ACT.Copy, bias=-MAGIC).then_inc(q12_done, 1)

            def copy_inputs(t):
                wait(act, qt_done, 1, t, 1)
                wait(act, w12_done, NQ, tile(t, -1))
                act.activation(q_t[:, t[1] % 2, :, :], p_q[:, :, :], ACT.Copy).then_inc(qtc_done, 1)

            def copy_hidden(t, half):
                wait(act, ht_done, 2, t, half + 1)
                wait(act, o_done, 1, t)
                act.activation(q3_t[:, half * HH:(half + 1) * HH, :], p_h[half][:, :, :], ACT.Copy
                               ).then_inc(htc_done, 1)

            scaled_inputs((0, 0))
            quantised_inputs((0, 0))
            copy_inputs((0, 0))
            scaled_inputs((0, 1))

            def body(t):
                back = tile(t, -2)
                for n in range(NQ):
                    if exists(t):
                        wait(act, w12_done, NQ, t, n + 1)
                        wait(act, deq_done, 1, t, 1)
                        wait(act, h_done, NQ, t, n - 1)
                        act.activation(sw[:, n % 2, :], p1[n % 2][:, :], ACT.Silu,
                                       scale=deq12[:, t[1] % 2, 0:1]).then_inc(sw_done, 1)
                    if n == 0 and exists(tile(t, 1)):
                        quantised_inputs(tile(t, 1))
                    if n in (1, 2) and exists(back):
                        copy_hidden(back, n - 1)
                    if n == 3 and exists(tile(t, 1)):
                        copy_inputs(tile(t, 1))
                u = tile(t, -1)
                if exists(t):
                    wait(act, h_done, NQ, t, NQ)
                    wait(act, hss_done, 1, t)
                    act.activation(hsq[:, :], h[:, t[1] % 2, :], ACT.Square,
                                   accum_out=hss[:, t[1] % 2:t[1] % 2 + 1]).then_inc(hss_done, 1)
                if exists(tile(t, 2)):
                    scaled_inputs(tile(t, 2))
                if exists(u):
                    wait(act, u3_done, 1, u, 1)
                    wait(act, ht_done, 2, u)
                    act.activation(q3[:, :], u3[:, u[1] % 2, :], ACT.Copy, bias=-MAGIC).then_inc(q3_done, 1)
            slots(act, body)

        @block.gpsimd
        def _(pool):
            pool.wait_ge(g3_loaded, 16)

            def body(t):
                if not exists(t):
                    return
                for n in range(NQ):
                    at = slice(n * DIM, (n + 1) * DIM)
                    wait(pool, h_done, NQ, t, n + 1)
                    wait(pool, q3_done, 1, t, -1)
                    pool.tensor_tensor(u3[:, t[1] % 2, at], h[:, t[1] % 2, at], g3[:, at], ALU.mult
                                       ).then_inc(u3_ready, 1)
            slots(pool, body)

        @block.vector
        def _(dve):
            n_first = 0

            def link(ins):
                nonlocal n_first
                n_first += 1
                ins.then_inc(first, 1)
                dve.wait_ge(first, n_first)

            link(dve.tensor_reduce(v[:, :], k["y_sq"][:, :].rearrange("p (t g) -> p t g", g=GROUPS), AX.X, ALU.add))
            link(dve.tensor_scalar(v[:, :], v[:, :], 1.0 / INNER, EPS_RMS, ALU.mult, ALU.add))
            n_first = newton_rsqrt(dve, first, n_first, r[:, :], v[:, :], tmp[:, :])
            for t in range(TILES):
                dve.wait_ge(resid_in[t % AHEAD], 16 * (t // AHEAD + 1))
                dve.scalar_tensor_tensor(out=h1[:, t, :], in0=h1[:, t, :], scalar=r[:, t:t + 1],
                                         in1=resid[:, t % AHEAD, :], op0=ALU.mult, op1=ALU.add).then_inc(h1_done, 1)
                if t:
                    dve.wait_ge(h1_done, t)
                    dve.bn_stats(stats[:, t - 1, :], h1[:, t - 1, :]).then_inc(first, 1)
                    n_first += 1
            dve.wait_ge(h1_done, TILES)
            link(dve.bn_stats(stats[:, TILES - 1, :], h1[:, TILES - 1, :]))
            for t in range(TILES):
                dve.bn_aggr(mv[:, t, :], stats[:, t, :]).then_inc(first, 1)
            n_first += TILES
            dve.wait_ge(first, n_first)
            link(dve.tensor_scalar(v[:, :], mv[:, :, 1], EPS_NORM, None, ALU.add))
            link(dve.scalar_tensor_tensor(out=v[:, :], in0=v[:, :], scalar=EPS_BIT, in1=mv[:, :, 1],
                                          op0=ALU.mult, op1=ALU.add))
            dve.tensor_scalar(minus_mean[:, :], mv[:, :, 0], -1.0, None, ALU.mult).then_inc(first, 1)
            n_first += 1
            n_first = newton_rsqrt(dve, first, n_first, rn[:, :], v[:, :], tmp[:, :])
            dve.wait_ge(loaded, 2 * 16)

            def prepare(t, step):
                def after(n):
                    wait(dve, prep_step, PREP_STEPS, t, n)

                def col(a):
                    return a[:, bass.ds(number(t), 1)]
                if step < 2:
                    w = step
                    wait(dve, q12_done, 2, t)
                    dve.scalar_tensor_tensor(out=u12[:, w, :], in0=h1_of(t), scalar=col(minus_mean),
                                             in1=g12[:, w, :], op0=ALU.add, op1=ALU.mult).then_inc(prep_step, 1)
                elif step == 2:
                    after(2)
                    dve.tensor_reduce(size12[:, :], u12[:, :, :], AX.X, ALU.max, apply_absolute_value=True
                                      ).then_inc(prep_step, 1)
                elif step == 3:
                    after(3)
                    dve.tensor_scalar(top12[:, :], size12[:, :], col(rn), 1e-4, ALU.mult, ALU.max
                                      ).then_inc(prep_step, 1)
                elif step == 4:
                    after(4)
                    wait(dve, h_done, NQ, tile(t, -1))
                    dve.tensor_tensor(deq12[:, t[1] % 2, :], top12[:, :], ath[:, 0:2], ALU.mult
                                      ).then_inc(deq_done, 1)
                elif step == 5:
                    wait(dve, q12_done, 2, t)
                    dve.reciprocal(scale12[:, :], top12[:, :]).then_inc(prep_step, 1)
                else:
                    after(5)
                    dve.tensor_scalar(scale12[:, :], scale12[:, :], 127.0, col(rn), ALU.mult, ALU.mult
                                      ).then_inc(prep_step, 1)

            def h1_of(t):
                return h1[:, bass.ds(number(t), 1), :].rearrange("p a c -> p (a c)")

            def hidden(t, step):
                if step:
                    wait(dve, hid_step, HIDDEN_STEPS, t, min(step, HIDDEN_STEPS))
                if step == 0:
                    wait(dve, u3_ready, NQ, t, NQ)
                    ins = dve.tensor_reduce(size3[:, :], u3[:, t[1] % 2, :], AX.X, ALU.max,
                                            apply_absolute_value=True)
                elif step == 1:
                    wait(dve, hss_done, 1, t, 1)
                    ins = dve.tensor_scalar(ms3[:, :], hss[:, t[1] % 2:t[1] % 2 + 1], 1.0 / HIDDEN, EPS_BIT,
                                            ALU.mult, ALU.add)
                elif step == 2:
                    ins = dve.tensor_scalar(t3[:, :].bitcast(I32), ms3[:, :].bitcast(I32), 1, None,
                                            ALU.logical_shift_right)
                elif step == 3:
                    ins = dve.tensor_scalar(rb3[:, :].bitcast(I32), t3[:, :].bitcast(I32), -1.0, RSQRT_GUESS,
                                            ALU.mult, ALU.add)
                elif step < 13 and step % 3 == 1:
                    ins = dve.tensor_tensor(t3[:, :], rb3[:, :], rb3[:, :], ALU.mult)
                elif step < 13 and step % 3 == 2:
                    ins = dve.scalar_tensor_tensor(out=t3[:, :], in0=t3[:, :], scalar=-0.5, in1=ms3[:, :],
                                                   op0=ALU.mult, op1=ALU.mult)
                elif step < 13:
                    ins = dve.scalar_tensor_tensor(out=rb3[:, :], in0=t3[:, :], scalar=1.5, in1=rb3[:, :],
                                                   op0=ALU.add, op1=ALU.mult)
                elif step == 13:
                    ins = dve.tensor_scalar(top3[:, :], size3[:, :], rb3[:, 0:1], 1e-4, ALU.mult, ALU.max)
                elif step == 14:
                    ins = dve.reciprocal(scale3[:, :], top3[:, :])
                elif step == 15:
                    ins = dve.tensor_scalar(scale3[:, :], scale3[:, :], 127.0, rb3[:, 0:1], ALU.mult, ALU.mult)
                elif step == 16:
                    dve.tensor_tensor(deq3[:, t[1] % 2:t[1] % 2 + 1], top3[:, :], ath[:, 2:3], ALU.mult
                                      ).then_inc(deq3_done, 1)
                    return
                else:
                    dve.tensor_scalar(u3[:, t[1] % 2, :], u3[:, t[1] % 2, :], scale3[:, 0:1], MAGIC,
                                      ALU.mult, ALU.add).then_inc(u3_done, 1)
                    return
                ins.then_inc(hid_step, 1)

            def product(t, n):
                at = slice(n * DIM, (n + 1) * DIM)
                wait(dve, sw_done, NQ, t, n + 1)
                wait(dve, hss_done, 1, t, -1)
                wait(dve, u3_ready, NQ, t, -NQ)
                dve.scalar_tensor_tensor(out=h[:, t[1] % 2, at], in0=p2[n % 2][:, :],
                                         scalar=deq12[:, t[1] % 2, 1:2], in1=sw[:, n % 2, :],
                                         op0=ALU.mult, op1=ALU.mult).then_inc(h_done, 1)

            def result(t):
                wait(dve, o_done, 1, t, 1)
                wait(dve, deq3_done, 1, t, 1)
                g, k_th = t
                if not isinstance(g, int) or k_th >= 2:
                    dve.wait_ge(out_done[k_th % 2], 16 * g + 16 * (k_th // 2))
                dve.scalar_tensor_tensor(out=res[:, t[1] % 2, :], in0=p_o[:, :], scalar=deq3[:, t[1] % 2:t[1] % 2 + 1],
                                         in1=h1_of(t), op0=ALU.mult, op1=ALU.add).then_inc(res_done, 1)

            for t in range(2):
                for step in range(7):
                    prepare((0, t), step)

            def body(t):
                u, ahead = tile(t, -1), tile(t, 2)

                def hidden_steps(*steps):
                    if exists(u):
                        for step in steps:
                            hidden(u, step)

                def prepare_steps(*steps):
                    if exists(ahead):
                        for step in steps:
                            prepare(ahead, step)

                hidden_steps(0)
                for n in range(NQ):
                    hidden_steps(3 * n + 1)
                    if exists(t):
                        product(t, n)
                    hidden_steps(3 * n + 2)
                    if n:
                        prepare_steps(n - 1)
                    if n == 1 and exists(tile(t, -3)):
                        result(tile(t, -3))
                    hidden_steps(3 * n + 3)
                prepare_steps(3)
                hidden_steps(13)
                prepare_steps(4)
                hidden_steps(14)
                prepare_steps(5)
                hidden_steps(15)
                prepare_steps(6)
                hidden_steps(16, 17)
            slots(dve, body)


def build(nc, d):
    d = dict(d)
    d["resid"] = nc.dram_tensor("resid_scratch", [TILES, P, DIM], F32, kind="Internal").ap()
    d["tern"] = nc.dram_tensor("tern_scratch", [GROUPS, P, WCOLS // 2], F32, kind="Internal").ap()
    d["cum"] = nc.dram_tensor("cum_scratch", [2, HEADS, TOKENS], F32, kind="Internal").ap()
    with ExitStack() as ctx:
        def sb(name, shape, dt=F32):
            return ctx.enter_context(nc.sbuf_tensor(name, shape, dt))

        TC = TILES * HEADS
        k = {
            "acc": sb("acc", [P, TILES, DIM]),
            "w_sum": sb("w_sum", [P, 12]),
            "inv_all": sb("inv_all", [P, GROUPS]),
            "ath": sb("ath", [P, 3]),
            "y_sq": sb("y_sq", [P, TILES * GROUPS]),
            "ident": sb("ident_f", [P, P]),
            "ident_b": sb("ident_b", [P, P], BF16),
        }
        with ExitStack() as inner:
            def sbi(name, shape, dt=F32):
                return inner.enter_context(nc.sbuf_tensor(name, shape, dt))

            k.update({
                "x_hi": sbi("x_hi", [P, KT, TOKENS], F32R),
                "x_lo": sbi("x_lo", [P, KT, TOKENS], F32R),
                "b_tok": sbi("b_tok", [P, TILES, P]),
                "c_t": sbi("c_t", [P, TOKENS]),
                "cb": sbi("cb", [P, TILES, P]),
                "e_cum": sbi("e_cum", [P, TC]),
                "e_all": sbi("e_all", [P, TC]),
                "e_rest": sbi("e_rest", [P, TC]),
                "d_row": sbi("d_row", [P, HEADS]),
                "rows": sbi("rows", [10, 2, GH * P], F32R),
                "cols": sbi("cols", [10, 2, P], F32R),
            })
            with ExitStack() as early:
                for name, dt in (("bcd_raw", F32), ("bcd_hi", F32R), ("bcd_lo", F32R)):
                    k[name] = early.enter_context(nc.sbuf_tensor(name, [P, KT, 3 * P], dt))
                embed(nc, d, k)
                decays(nc, d, k)
            mixer(nc, d, k)
        ffn(nc, d, k)


def layouts(x, L0_tok_W, L0_tok_delta_values, L0_tok_token_indices, L0_attn_norm_w, L0_attn_in_proj_w,
            L0_attn_conv_w, L0_attn_conv_b, L0_attn_dt_bias, L0_attn_A_log, L0_attn_D_param,
            L0_attn_inner_norm_w, L0_attn_out_proj_w, L0_attn_conv_state, L0_attn_ssm_state,
            L0_ffn_w1, L0_ffn_g1, L0_ffn_w2, L0_ffn_g2, L0_ffn_w3, L0_ffn_g3):
    c = np.ascontiguousarray
    w = np.asarray(L0_attn_in_proj_w)
    turned = c(w.T).reshape(KT, P, w.shape[0]).transpose(1, 0, 2)
    z, xc = turned[:, :, :INNER], turned[:, :, INNER:2 * INNER]
    w_in = np.stack([xc.reshape(P, KT, GROUPS, GT, P), z.reshape(P, KT, GROUPS, GT, P)], 3)
    w_in = w_in.transpose(2, 3, 4, 0, 1, 5).reshape(GROUPS, 2 * GT, P, KT * P)
    at = 2 * INNER
    w_bcd = np.concatenate([turned[:, :, at:at + 2 * STATE], turned[:, :, at + 2 * STATE:],
                            turned[:, :, :P - HEADS]], 2)
    per_channel = np.concatenate([np.asarray(L0_attn_conv_w), np.asarray(L0_attn_conv_b)[:, None],
                                  np.asarray(L0_attn_inner_norm_w)[:, None]], 1)
    params = np.concatenate([per_channel.reshape(GROUPS, GT, P, 6).transpose(2, 0, 1, 3).reshape(P, GROUPS, 12),
                             np.asarray(L0_attn_conv_state)[0].reshape(GROUPS, GT, P, 3).transpose(2, 0, 1, 3)
                             .reshape(P, GROUPS, 6)], 2).transpose(1, 0, 2)
    kmajor = lambda a, n: c(np.asarray(a).T).reshape(n, P, -1).transpose(1, 0, 2).reshape(P, -1, WCOLS).transpose(1, 0, 2)
    first = np.asarray(L0_attn_ssm_state)[0].reshape(GROUPS, GH, STATE, HEAD).transpose(0, 2, 1, 3)
    i = np.arange(P)
    rows = np.zeros((10, 2, GH, P), np.float32)
    cols = np.zeros((10, 2, P), np.float32)
    cols[0:2] = 1.0
    for part in range(2):
        for h in range(GH):
            rows[2 + part * GH + h, :, h, :] = -1.0
    return {
        "id_col": c(np.asarray(x).reshape(TILES, P).T),
        "id_row": c(np.asarray(x).reshape(TOKENS)),
        "tok": c(np.asarray(L0_tok_token_indices).reshape(TRAINED, 1)),
        "delta": c(np.asarray(L0_tok_delta_values).reshape(DIM, TRAINED).T),
        "W": c(np.asarray(L0_tok_W)),
        "norm_w": c(np.asarray(L0_attn_norm_w)),
        "w_in": c(w_in), "w_bcd": c(w_bcd), "params": c(params),
        "w_out": c(np.asarray(L0_attn_out_proj_w).T).reshape(GROUPS, GT, P, DIM),
        "dt_bias": c(np.asarray(L0_attn_dt_bias).reshape(HEADS, 1)),
        "a_log": c(np.asarray(L0_attn_A_log).reshape(HEADS, 1)),
        "D": c(np.asarray(L0_attn_D_param)),
        "h_first": c(first),
        "w_ffn": c(np.concatenate([kmajor(L0_ffn_w1, KT), kmajor(L0_ffn_w2, KT), kmajor(L0_ffn_w3, HT)], 0)),
        "g12": c(np.stack([np.asarray(L0_ffn_g1), np.asarray(L0_ffn_g2)])),
        "g3": c(np.asarray(L0_ffn_g3)),
        "ident": np.eye(P, dtype=np.float32),
        "ones": np.ones((P, P), np.float32),
        "tri": (i[:, None] <= i[None, :]).astype(np.float32),
        "pick_last": np.broadcast_to((i == P - 1)[:, None], (P, P)).astype(np.float32),
        "keep": (np.arange(TOKENS) % P != 0).astype(np.float32),
        "rows": rows.reshape(10, 2, GH * P), "cols": cols,
    }


def kernel(**inputs):
    import concourse.bacc as bacc
    from concourse.bass_utils import run_bass_kernel_spmd

    nc = bacc.Bacc("TRN2", target_bir_lowering=False, num_devices=1)
    arrays, d = {}, {}
    for name, a in layouts(**inputs).items():
        a = np.ascontiguousarray(a)
        arrays[f"in_{name}"] = a
        d[name] = nc.dram_tensor(f"in_{name}", a.shape, mybir.dt.from_np(a.dtype), kind="ExternalInput").ap()
    d["out"] = nc.dram_tensor("out_dram", [TOKENS, DIM], F32, kind="ExternalOutput").ap()
    build(nc, d)
    result = run_bass_kernel_spmd(nc, [arrays], core_ids=[0])
    return result.results[0]["out_dram"].reshape(BATCH, SEQ, DIM)
```
